# Optimizing a Trainium2 kernel written in Bass

```python
import numpy as np
import jax
import jax.numpy as jnp

def _softmax(x, axis=-1):
    return jax.nn.softmax(x, axis=axis)

def _gelu(x):
    return jax.nn.gelu(x, approximate=True)

def _silu(x):
    return jax.nn.silu(x)

def _sigmoid(x):
    return jax.nn.sigmoid(x)

def _layernorm(x, axis=-1, eps=1e-05):
    m = jnp.mean(x, axis=axis, keepdims=True)
    v = jnp.var(x, axis=axis, keepdims=True)
    return (x - m) / jnp.sqrt(v + eps)

def _scatter_add(tgt, idx, src, axis=0):
    return tgt.at[idx].add(src)

def _segment_sum(src, seg, n):
    return jax.ops.segment_sum(src, seg, n)
kernel_name = 'mk_perceiver_d1_seqx_r8_2c7224'

def setup_inputs(seed: int=0):
    np.random.seed(seed)
    _w = jnp.asarray

    def _rec_inputs():
        import jax
        import jax.numpy as jnp
        _rk = jax.random.key(seed)
        x = -0.0002928 + 1 * jax.random.normal(jax.random.fold_in(_rk, 1), (64, 64, 128), jnp.float32)
        _lenS = 64 - jax.random.randint(jax.random.fold_in(_rk, 7), (64,), 0, max(1, 64 // 4) + 1, jnp.int32)
        _lenS2 = 128 - jax.random.randint(jax.random.fold_in(_rk, 8), (64,), 0, max(1, 128 // 4) + 1, jnp.int32)
        _ctx_1024P = jax.random.normal(jax.random.fold_in(_rk, 11), (64, 16, 128), jnp.float32)
        _ctx_1024c = jax.random.dirichlet(jax.random.fold_in(_rk, 511), 0.3 * jnp.ones((16,), jnp.float32), (64, 128))
        _ctx_1024t = jnp.einsum('bsk,bkd->bsd', _ctx_1024c, _ctx_1024P)
        _ctx_1024t = _ctx_1024t * jax.lax.rsqrt(jnp.mean(jnp.square(_ctx_1024t)) + 1e-12) * 0.953939
        ctx_1024 = -1.39393e-06 + 0.999914 * (_ctx_1024t + 0.3 * jax.random.normal(jax.random.fold_in(_rk, 611), (64, 128, 128), jnp.float32))
        _validS = jnp.arange(64)[None, :] < _lenS[:, None]
        _validS2 = jnp.arange(128)[None, :] < _lenS2[:, None]
        _causal = jnp.tril(jnp.ones((64, 64), dtype=bool))
        mask_Bx1x1xS2_ik0 = jnp.where(jnp.broadcast_to(_validS2[:, None, None, :], (64, 1, 1, 128)), 0, 1).astype(jnp.int32)
        return (x, ctx_1024, mask_Bx1x1xS2_ik0)
    x, ctx_1024, mask_Bx1x1xS2_ik0 = _rec_inputs()

    def _L0_xattn_setup():
        import jax, jax.numpy as jnp
        import numpy as np
        B, S, D, H = (2, 256, 128, 16)
        DEPTH = D // H

        def _split_heads(x):
            b, s, _ = x.shape
            return x.reshape(b, s, H, DEPTH).transpose(0, 2, 1, 3)
        key = jax.random.key(seed)
        ks = jax.random.split(key, 12)
        inp = {'query': jax.random.normal(ks[0], (B, S, D), jnp.float32), 'key': jax.random.normal(ks[1], (B, S, D), jnp.float32), 'value': jax.random.normal(ks[2], (B, S, D), jnp.float32), 'mask': jax.random.randint(ks[3], (B, 1, 1, S), 0, 2, jnp.int32), 'Wq': jax.random.normal(ks[4], (D, D), jnp.float32) / np.sqrt(D), 'bq': jnp.zeros((D,), jnp.float32), 'Wk': jax.random.normal(ks[5], (D, D), jnp.float32) / np.sqrt(D), 'bk': jnp.zeros((D,), jnp.float32), 'Wv': jax.random.normal(ks[6], (D, D), jnp.float32) / np.sqrt(D), 'bv': jnp.zeros((D,), jnp.float32), 'Wo': jax.random.normal(ks[7], (D, D), jnp.float32) / np.sqrt(D), 'bo': jnp.zeros((D,), jnp.float32)}
        return inp
    _L0_xattn_all = _L0_xattn_setup()
    _L0_xattn_in = {k: v for k, v in _L0_xattn_all.items() if k in ('Wq', 'bq', 'Wk', 'bk', 'Wv', 'bv', 'Wo', 'bo')}
    del _L0_xattn_all

    def _L0_attn_setup():
        import jax, jax.numpy as jnp
        import numpy as np
        H = 4
        DK = 128
        DV = 32
        LOW_RANK = 16
        GATE_NORM = 16.0
        CHUNK = 64
        EPS = 1e-05

        def _gla_chunk(q, k, v, gk):
            B, T, _, _ = q.shape
            NC, C = (T // CHUNK, CHUNK)
            scale = DK ** (-0.5)

            def chunks(a):
                return a.reshape(B, NC, C, H, a.shape[-1]).transpose(1, 0, 3, 2, 4)
            qc, kc, vc, gc = (chunks(q), chunks(k), chunks(v), chunks(gk))
            G = jnp.cumsum(gc, axis=-2)
            qg = qc * jnp.exp(G) * scale
            k_intra = kc * jnp.exp(-G)
            kg = kc * jnp.exp(G[..., -1:, :] - G)
            g_last = jnp.exp(G[..., -1, :])
            A = jnp.einsum('nbhik,nbhjk->nbhij', qg, k_intra)
            A = jnp.where(jnp.tril(jnp.ones((C, C), bool)), A, 0.0)
            o_intra = jnp.einsum('nbhij,nbhjv->nbhiv', A, vc)

            def step(S, inp):
                qg_, kg_, v_, gl_, oi_ = inp
                o = oi_ + jnp.einsum('bhck,bhkv->bhcv', qg_, S)
                S = S * gl_[..., :, None] + jnp.einsum('bhck,bhcv->bhkv', kg_, v_)
                return (S, o)
            S0 = jnp.zeros((B, H, DK, DV), q.dtype)
            _, o = jax.lax.scan(step, S0, (qg, kg, vc, g_last, o_intra))
            return o.transpose(1, 0, 3, 2, 4).reshape(B, T, H, DV)
        key = jax.random.key(seed)
        ks = jax.random.split(key, 10)
        Dm = 128
        Kd, Vd = (H * DK, H * DV)

        def lin(k, fan_in, fan_out):
            return jax.random.normal(k, (fan_in, fan_out), jnp.float32) * fan_in ** (-0.5)
        return {'x': jax.random.normal(ks[0], (4, 256, Dm), jnp.float32), 'Wq': lin(ks[1], Dm, Kd), 'Wk': lin(ks[2], Dm, Kd), 'Wv': lin(ks[3], Dm, Vd), 'Wg': lin(ks[4], Dm, Vd), 'Wgk1': lin(ks[5], Dm, LOW_RANK), 'Wgk2': lin(ks[6], LOW_RANK, Kd), 'bgk2': jnp.zeros((Kd,), jnp.float32), 'Wo': lin(ks[7], Vd, Dm), 'gnw': jnp.ones((DV,), jnp.float32)}
    _L0_attn_all = _L0_attn_setup()
    _L0_attn_in = {k: v for k, v in _L0_attn_all.items() if k in ('Wq', 'Wk', 'Wv', 'Wg', 'Wgk1', 'Wgk2', 'bgk2', 'Wo', 'gnw')}
    del _L0_attn_all

    def _L0_ffn_setup():
        import jax, jax.numpy as jnp
        import numpy as np
        B, S, DIM, FFN, E = (4, 256, 128, 512, 8)
        key = jax.random.key(seed)
        k0, k1, k2, k3 = jax.random.split(key, 4)
        scale = 0.02
        return {'hidden_states': jax.random.normal(k0, (B, S, DIM), jnp.float32), 'router_w': jax.random.normal(k1, (DIM, E), jnp.float32) * scale, 'router_b': jnp.zeros((E,), jnp.float32), 'w1': jax.random.normal(k2, (E, DIM, 2 * FFN), jnp.float32) * scale, 'w2': jax.random.normal(k3, (E, FFN, DIM), jnp.float32) * scale}
    _L0_ffn_all = _L0_ffn_setup()
    _L0_ffn_in = {k: v for k, v in _L0_ffn_all.items() if k in ('router_w', 'router_b', 'w1', 'w2')}
    del _L0_ffn_all
    return {'x': x, 'ctx_1024': ctx_1024, 'mask_Bx1x1xS2_ik0': mask_Bx1x1xS2_ik0, 'L0_xattn_Wq': _L0_xattn_in['Wq'], 'L0_xattn_bq': _L0_xattn_in['bq'], 'L0_xattn_Wk': _L0_xattn_in['Wk'], 'L0_xattn_bk': _L0_xattn_in['bk'], 'L0_xattn_Wv': _L0_xattn_in['Wv'], 'L0_xattn_bv': _L0_xattn_in['bv'], 'L0_xattn_Wo': _L0_xattn_in['Wo'], 'L0_xattn_bo': _L0_xattn_in['bo'], 'L0_attn_Wq': _L0_attn_in['Wq'], 'L0_attn_Wk': _L0_attn_in['Wk'], 'L0_attn_Wv': _L0_attn_in['Wv'], 'L0_attn_Wg': _L0_attn_in['Wg'], 'L0_attn_Wgk1': _L0_attn_in['Wgk1'], 'L0_attn_Wgk2': _L0_attn_in['Wgk2'], 'L0_attn_bgk2': _L0_attn_in['bgk2'], 'L0_attn_Wo': _L0_attn_in['Wo'], 'L0_attn_gnw': _L0_attn_in['gnw'], 'L0_ffn_router_w': _L0_ffn_in['router_w'], 'L0_ffn_router_b': _L0_ffn_in['router_b'], 'L0_ffn_w1': _L0_ffn_in['w1'], 'L0_ffn_w2': _L0_ffn_in['w2']}

def reference(x, ctx_1024, mask_Bx1x1xS2_ik0, L0_xattn_Wq, L0_xattn_bq, L0_xattn_Wk, L0_xattn_bk, L0_xattn_Wv, L0_xattn_bv, L0_xattn_Wo, L0_xattn_bo, L0_attn_Wq, L0_attn_Wk, L0_attn_Wv, L0_attn_Wg, L0_attn_Wgk1, L0_attn_Wgk2, L0_attn_bgk2, L0_attn_Wo, L0_attn_gnw, L0_ffn_router_w, L0_ffn_router_b, L0_ffn_w1, L0_ffn_w2):
    import jax
    import jax.numpy as jnp

    def _L0_xattn_ref(query, key, value, mask, Wq, bq, Wk, bk, Wv, bv, Wo, bo):
        import jax, jax.numpy as jnp
        import numpy as np
        B, S, D, H = (2, 256, 128, 16)
        DEPTH = D // H

        def _split_heads(x):
            b, s, _ = x.shape
            return x.reshape(b, s, H, DEPTH).transpose(0, 2, 1, 3)
        q = _split_heads(query @ Wq + bq)
        k = _split_heads(key @ Wk + bk)
        v = _split_heads(value @ Wv + bv)
        scale = 1.0 / jnp.sqrt(jnp.asarray(DEPTH, jnp.float32))
        logits = jnp.einsum('bhqd,bhkd->bhqk', q, k) * scale
        logits = logits + mask.astype(jnp.float32) * -1000000000.0
        attn = jax.nn.softmax(logits, axis=-1)
        ctx = jnp.einsum('bhqk,bhkd->bhqd', attn, v)
        ctx = ctx.transpose(0, 2, 1, 3).reshape(query.shape[0], -1, D)
        return ctx @ Wo + bo

    def _L0_attn_ref(x, Wq, Wk, Wv, Wg, Wgk1, Wgk2, bgk2, Wo, gnw):
        import jax, jax.numpy as jnp
        import numpy as np
        H = 4
        DK = 128
        DV = 32
        LOW_RANK = 16
        GATE_NORM = 16.0
        CHUNK = 64
        EPS = 1e-05

        def _gla_chunk(q, k, v, gk):
            B, T, _, _ = q.shape
            NC, C = (T // CHUNK, CHUNK)
            scale = DK ** (-0.5)

            def chunks(a):
                return a.reshape(B, NC, C, H, a.shape[-1]).transpose(1, 0, 3, 2, 4)
            qc, kc, vc, gc = (chunks(q), chunks(k), chunks(v), chunks(gk))
            G = jnp.cumsum(gc, axis=-2)
            qg = qc * jnp.exp(G) * scale
            k_intra = kc * jnp.exp(-G)
            kg = kc * jnp.exp(G[..., -1:, :] - G)
            g_last = jnp.exp(G[..., -1, :])
            A = jnp.einsum('nbhik,nbhjk->nbhij', qg, k_intra)
            A = jnp.where(jnp.tril(jnp.ones((C, C), bool)), A, 0.0)
            o_intra = jnp.einsum('nbhij,nbhjv->nbhiv', A, vc)

            def step(S, inp):
                qg_, kg_, v_, gl_, oi_ = inp
                o = oi_ + jnp.einsum('bhck,bhkv->bhcv', qg_, S)
                S = S * gl_[..., :, None] + jnp.einsum('bhck,bhcv->bhkv', kg_, v_)
                return (S, o)
            S0 = jnp.zeros((B, H, DK, DV), q.dtype)
            _, o = jax.lax.scan(step, S0, (qg, kg, vc, g_last, o_intra))
            return o.transpose(1, 0, 3, 2, 4).reshape(B, T, H, DV)
        B, T, Dm = x.shape
        q = (x @ Wq).reshape(B, T, H, DK)
        k = (x @ Wk).reshape(B, T, H, DK)
        v = (x @ Wv).reshape(B, T, H, DV)
        gk = jax.nn.log_sigmoid(x @ Wgk1 @ Wgk2 + bgk2) / GATE_NORM
        gk = gk.reshape(B, T, H, DK)
        o = _gla_chunk(q, k, v, gk)
        g = (x @ Wg).reshape(B, T, H, DV)
        o = o * jax.lax.rsqrt(jnp.mean(o * o, axis=-1, keepdims=True) + EPS) * gnw
        o = o * (g * jax.nn.sigmoid(g))
        return o.reshape(B, T, H * DV) @ Wo

    def _L0_ffn_ref(hidden_states, router_w, router_b, w1, w2):
        import jax, jax.numpy as jnp
        import numpy as np
        B, S, DIM, FFN, E = (4, 256, 128, 512, 8)
        b, s, d = hidden_states.shape
        x = hidden_states.reshape(-1, d)
        logits = x @ router_w + router_b
        route = jax.nn.softmax(logits, axis=1)
        max_prob = jnp.max(route, axis=1, keepdims=True)
        max_ind = jnp.argmax(route, axis=1)
        out = jnp.zeros_like(x)
        num_experts = w1.shape[0]
        for e in range(num_experts):
            h = x @ w1[e]
            a, g = jnp.split(h, 2, axis=1)
            y = jax.nn.silu(a) * g @ w2[e]
            out = jnp.where((max_ind == e)[:, None], y, out)
        out = out * max_prob
        return out.reshape(b, s, d)
    x = x + _L0_xattn_ref(_layernorm(x, axis=-1), ctx_1024, ctx_1024, mask_Bx1x1xS2_ik0, L0_xattn_Wq, L0_xattn_bq, L0_xattn_Wk, L0_xattn_bk, L0_xattn_Wv, L0_xattn_bv, L0_xattn_Wo, L0_xattn_bo)
    x = x + _L0_attn_ref(_layernorm(x, axis=-1), L0_attn_Wq, L0_attn_Wk, L0_attn_Wv, L0_attn_Wg, L0_attn_Wgk1, L0_attn_Wgk2, L0_attn_bgk2, L0_attn_Wo, L0_attn_gnw)
    x = x + _L0_ffn_ref(_layernorm(x, axis=-1), L0_ffn_router_w, L0_ffn_router_b, L0_ffn_w1, L0_ffn_w2)
    return x

_drawn_inputs = setup_inputs


def setup_inputs(seed=0):
    import zlib

    import numpy as np

    out = dict(_drawn_inputs(seed))
    spreads = {'L0_xattn_bq': (0.0, 0.1),
     'L0_xattn_bk': (0.0, 0.8),
     'L0_xattn_bv': (0.0, 0.1),
     'L0_xattn_bo': (0.0, 0.1),
     'L0_attn_bgk2': (0.0, 0.403),
     'L0_attn_gnw': (1.0, 0.2),
     'L0_ffn_router_b': (0.0, 0.8)}
    factors = {'L0_ffn_router_w': 8.0, 'L0_ffn_w1': 8.0, 'L0_ffn_w2': 8.0}
    for name, (base, spread) in spreads.items():
        noise = np.random.default_rng([zlib.crc32(name.encode()), seed]).standard_normal(out[name].shape)
        drawn = base * np.exp(spread * noise) if base else spread * noise
        out[name] = jnp.asarray(drawn.astype(out[name].dtype))
    for name, factor in factors.items():
        out[name] = (out[name] * factor).astype(out[name].dtype)
    return out
```

```python
from contextlib import ExitStack

import concourse.bass as bass
from concourse import mybir

F32 = mybir.dt.float32
BF16 = mybir.dt.bfloat16
I32 = mybir.dt.int32
ALU = mybir.AluOpType
ACT = mybir.ActivationFunctionType
AX = mybir.AxisListType

P = 128
B, SQ, D = 64, 64, 128
SK = 128
H, DH = 16, 8
EPS = 1e-5
SCALE = DH ** -0.5
MASKED = -1000000000.0
NT = B * SQ // P
NU = 4
ROW = 2 * D + 2
VW = 2 * DH + 1


def cross_attention(nc, rows, xres, ident, wts, slots, later, x, ctx_in, mask, Wq, bq, Wk, bk, Wv, bv, Wo, bo, ident_in, heads_in):
    x_t = x.rearrange("(n b) s d -> n (b s) d", b=2)
    ctx_t = ctx_in.rearrange("(n b) k d -> n k b d", b=2)
    mask_t = mask.rearrange("(n b) a c k -> n (a c) (b k)", b=2)

    with ExitStack() as ctx:
        def sb(name, shape, dt=F32):
            return ctx.enter_context(nc.sbuf_tensor(name, shape, dt))

        def psum(name):
            return ctx.enter_context(nc.psum_tensor(name, [P, 512], F32))

        def sem(name):
            return ctx.enter_context(nc.semaphore(name))

        pad = sb("pad", [P, ROW])
        heads = sb("heads", [P, H])
        qt = sb("qt", [P, 2, P])
        wq, wk, wv = sb("wq", [D, P]), sb("wk", [D, P]), sb("wv", [D, P])
        wo2 = sb("wo2", [64, 2, D])
        bqc, bkc = sb("bqc", [P, 1]), sb("bkc", [P, 1])
        bvr, bor = sb("bvr", [P, P]), sb("bor", [P, D])
        onesb = sb("onesb", [P, P], BF16)
        halfs = sb("halfs", [P, 1])
        cin = sb("cin", [P, 2, 2, D])
        mki = sb("mki", [P, 2, 2 * SK], I32)
        mkb = sb("mkb", [P, 2, 2 * SK], BF16)
        stats, aggr, veps, rstd = sb("stats", [P, 2, 6]), sb("aggr", [P, 2, 2]), sb("veps", [P, 2]), sb("rstd", [P, 2])
        xn = sb("xn", [P, 2, D])
        xt = sb("xt", [P, 2, 384])
        kt = sb("kt", [P, 2, 2 * SK])
        vx = sb("vx", [P, 2, 2, 8, VW])
        qm = sb("qm", [P, 2, 2, H, SQ])
        mx = sb("mx", [P, 2, 4])
        dif, prob, pts = sb("dif", [P, NU, 512]), sb("prob", [P, NU, 512]), sb("pts", [P, NU, 512])
        rc = sb("rc", [P, 16])
        on = sb("on", [P, 2, 64])
        ot = sb("ot", [64, 2, 2, SQ])

        S = [psum("S0"), psum("S1")]
        PT = [psum("PT0"), psum("PT1")]
        TB = psum("TB")
        KO = psum("KO")
        VY = psum("VY")
        OB = psum("OB")
        o_ps = OB[:, 0:2 * 8 * VW].rearrange("p (b j w) -> p b j w", b=2, j=8)

        const_in, ones_set = sem("const_in"), sem("ones_set")
        tile_in = [sem("tile_in0"), sem("tile_in1")]
        s = {n: sem(n) for n in (
            "stats_ready", "aggr_ready", "veps_ready", "rstd_ready", "xn_ready", "turned", "turned_out",
            "kv_ready", "kv_out", "q_ready", "q_out", "k_out", "q_spread", "mask_ready", "residual_ready", "logits_ready", "max_ready",
            "dif_ready", "prob_ready", "pt_ready", "pt_out", "pv_ready", "rc_ready", "on_ready", "ot_ready",
            "ot_out", "y_ready", "x1_ready")}
        NCONST = 11
        block = ctx.enter_context(nc.Block())

        def run(eng, step, tail):
            for i in range(3):
                step(i, i % 2)
            with eng.Fori(3, NT - 3, 2) as i:
                step(i, 1)
                step(i + 1, 0)
            for i in range(NT - 3, NT):
                step(i, i % 2)
            tail(NT)

        def from_(i, k):
            return not isinstance(i, int) or i >= k

        def has(i, k):
            return not isinstance(i, int) or i + k < NT

        def half(i, p):
            return i // 2 if isinstance(i, int) else (i - p) // 2

        @block.sync
        def _(sp):
            for dst, src in ((ident[:, :], ident_in), (heads[:, :], heads_in), (wq[:, :], Wq), (wk[:, :], Wk),
                             (wv[:, :], Wv)):
                sp.dma_start(dst, src).then_inc(const_in, 16)

            def load(i, p):
                sp.dma_start(xres[:, bass.ds(i, 1), :], x_t[bass.ds(i, 1)].rearrange("n p d -> p n d")).then_inc(tile_in[p], 16)
                sp.dma_start(cin[:, p], ctx_t[bass.ds(i, 1)].rearrange("n k b d -> k (n b) d")).then_inc(tile_in[p], 16)
                if True:
                    sp.dma_start(mki[0:1, p, :], mask_t[bass.ds(i, 1)].rearrange("n a c -> (n a) c")).then_inc(tile_in[p], 16)

            sp.wait_ge(ones_set, 4)
            load(0, 0)
            load(1, 1)
            with sp.Fori(2, NT - 1, 2) as i:
                for p in range(2):
                    sp.wait_ge(s["turned"], i + p - 1)
                    sp.wait_ge(s["mask_ready"], i + p - 1)
                    load(i + p, p)

        @block.gpsimd
        def _(pool):
            nc.gpsimd.memset(onesb[:, :], 1.0).then_inc(ones_set, 1)
            nc.gpsimd.memset(halfs[:, :], -0.5).then_inc(ones_set, 1)
            nc.gpsimd.memset(mki[:, :, :], 0).then_inc(ones_set, 1)
            nc.gpsimd.memset(vx[:, :, :, :, :], 1.0).then_inc(ones_set, 1)
            pool.wait_ge(ones_set, 4)
            nc.gpsimd.memset(pad[:, :], 0.0).then_inc(ones_set, 1)
            pool.wait_ge(ones_set, 5)
            nc.gpsimd.memset(pad[:, 2 * D:2 * D + 1].bitcast(I32), 1 << 20).then_inc(ones_set, 1)
            pool.wait_ge(ones_set, 6)
            pool.dma_start(slots.rearrange("(n p) w -> p n w", p=P),
                           pad[:, :].rearrange("p (a w) -> p a w", a=1).broadcast_to([P, slots.shape[0] // P, ROW])).then_inc(wts["cleared"], 16)
            pool.wait_ge(const_in, 16 * NCONST)

            def power(i, p):
                pool.wait_ge(s["veps_ready"], i + 1)
                nc.gpsimd.tensor_tensor(rstd[:, p:p + 1], veps[:, p:p + 1], halfs[:, :], ALU.pow).then_inc(s["rstd_ready"], 1)

            def prepare(i, p):
                pool.wait_ge(tile_in[p], 48 * (half(i, p) + 1))
                if from_(i, 2):
                    pool.wait_ge(s["logits_ready"], NU * (i - 1))
                pool.wait_ge(s["stats_ready"], i + 1)
                pool.wait_ge(s["xn_ready"], i + 1)
                nc.gpsimd.tensor_tensor(xres[:, bass.ds(i, 1), :], xres[:, bass.ds(i, 1), :],
                                        bor[:, :].rearrange("p (n d) -> p n d", n=1), ALU.add).then_inc(s["residual_ready"], 1)
                nc.gpsimd.tensor_scalar(mkb[:, p, :], mki[:, p, :], MASKED, None, ALU.mult).then_inc(s["mask_ready"], 1)

            def spread(i, p):
                pool.wait_ge(s["q_out"], i + 1)
                if from_(i, 2):
                    pool.wait_ge(s["logits_ready"], NU * (i - 1))
                for b in range(2):
                    nc.gpsimd.tensor_tensor(
                        qm[:, p, b, :, :],
                        qt[:, p, SQ * b:SQ * b + SQ].rearrange("p (a c) -> p a c", a=1).broadcast_to([P, H, SQ]),
                        heads[:, :].rearrange("p (c a) -> p c a", a=1).broadcast_to([P, H, SQ]),
                        ALU.mult).then_inc(s["q_spread"], 1)

            power(0, 0)
            prepare(0, 0)
            power(1, 1)
            prepare(1, 1)
            spread(0, 0)
            for i in range(2, 4):
                spread(i - 1, 1 - i % 2)
                power(i, i % 2)
                prepare(i, i % 2)
            with pool.Fori(4, NT - 1, 2) as i:
                for p in range(2):
                    spread(i + p - 1, 1 - p)
                    power(i + p, p)
                    prepare(i + p, p)
            spread(NT - 1, 1)

        @block.scalar
        def _(act):
            for dst, src in ((bqc[:, :], bq.rearrange("(p a) -> p a", a=1)), (bkc[:, :], bk.rearrange("(p a) -> p a", a=1)),
                             (bvr[:, :], bv.rearrange("(a n) -> a n", a=1).broadcast_to([P, P])),
                             (bor[:, :], bo.rearrange("(a n) -> a n", a=1).broadcast_to([P, D]))):
                act.dma_start(dst, src).then_inc(const_in, 16)
            wo_v = Wo.rearrange("(j t d) n -> t j d n", j=8, t=2)
            for t in range(2):
                act.dma_start(wo2[:, t, :], wo_v[t]).then_inc(const_in, 16)
            act.preload_act_table_set("natural_log_exp_and_others")
            for dst, src in later:
                act.dma_start(dst, src).then_inc(wts["loaded"], 16)

            def exp(i, u):
                n = NU * i + u
                act.wait_ge(s["dif_ready"], n + 1)
                if from_(i, 1):
                    act.wait_ge(s["pt_ready"], n - 3)
                nc.scalar.activation(prob[:, u, :], dif[:, u, :], ACT.Exp).then_inc(s["prob_ready"], 1)

            def evacuate(i, u):
                n = NU * i + u
                act.wait_ge(s["pt_ready"], n + 1)
                if from_(i, 1):
                    act.wait_ge(s["pv_ready"], n - 3)
                nc.scalar.activation(pts[:, u, :], PT[u % 2][:, :], ACT.Copy).then_inc(s["pt_out"], 1)

            def turned_out(i, p):
                act.wait_ge(s["turned"], i + 1)
                if from_(i, 2):
                    act.wait_ge(s["q_ready"], i - 1)
                nc.scalar.activation(xt[:, p, :], TB[:, 0:384], ACT.Copy).then_inc(s["turned_out"], 1)

            def k_out(i, p):
                act.wait_ge(s["kv_ready"], i + 1)
                if from_(i, 2):
                    act.wait_ge(s["logits_ready"], NU * (i - 1))
                nc.scalar.activation(kt[:, p, :], KO[:, 0:256], ACT.Identity, bias=bkc[:, :]).then_inc(s["k_out"], 1)

            def q_out(i, p):
                act.wait_ge(s["q_ready"], i + 1)
                if from_(i, 2):
                    act.wait_ge(s["q_spread"], 2 * (i - 1))
                nc.scalar.activation(qt[:, p, :], TB[:, 384:512], ACT.Identity, bias=bqc[:, :]).then_inc(s["q_out"], 1)

            def ot_out(i):
                act.wait_ge(s["ot_ready"], i + 1)
                if from_(i, 1):
                    act.wait_ge(s["y_ready"], i)
                nc.scalar.activation(ot[:, :, :, :], KO[0:64, 256:512].rearrange("p (b t q) -> p t b q", b=2, t=2),
                                     ACT.Copy).then_inc(s["ot_out"], 1)

            def step(i, p):
                exp(i, 0)
                if from_(i, 2):
                    ot_out(i - 2)
                if from_(i, 1):
                    evacuate(i - 1, 2)
                if has(i, 1):
                    turned_out(i + 1, 1 - p)
                exp(i, 1)
                if has(i, 1):
                    q_out(i + 1, 1 - p)
                if from_(i, 1):
                    evacuate(i - 1, 3)
                if has(i, 1):
                    k_out(i + 1, 1 - p)
                exp(i, 2)
                evacuate(i, 0)
                exp(i, 3)
                evacuate(i, 1)

            def tail(i):
                evacuate(i - 1, 2)
                ot_out(i - 2)
                evacuate(i - 1, 3)
                ot_out(i - 1)

            turned_out(0, 0)
            k_out(0, 0)
            q_out(0, 0)
            run(act, step, tail)

        @block.vector
        def _(dve):
            def unit(i, u):
                n = NU * i + u
                lg = S[u % 2][:, :].rearrange("p (c k) -> p c k", k=SK)
                dve.wait_ge(s["logits_ready"], n + 1)
                nc.vector.tensor_reduce(mx[:, u % 2, :], lg, AX.X, ALU.max).then_inc(s["max_ready"], 1)
                dve.wait_ge(s["max_ready"], n + 1)
                if from_(i, 1):
                    dve.wait_ge(s["prob_ready"], n - 3)
                nc.vector.tensor_tensor(dif[:, u, :].rearrange("p (c k) -> p c k", k=SK), lg,
                                        mx[:, u % 2, :].rearrange("p (c a) -> p c a", a=1).broadcast_to([P, 4, SK]),
                                        ALU.subtract).then_inc(s["dif_ready"], 1)

            def norm(i, p):
                dve.wait_ge(tile_in[p], 48 * (half(i, p) + 1))
                xin = xres[:, bass.ds(i, 1), :]
                nc.vector.bn_stats(stats[:, p, :], xin.rearrange("p n d -> p (n d)")).then_inc(s["stats_ready"], 1)
                dve.wait_ge(s["stats_ready"], i + 1)

            def aggregate(i, p):
                nc.vector.bn_aggr(aggr[:, p, :], stats[:, p, :]).then_inc(s["aggr_ready"], 1)
                dve.wait_ge(s["aggr_ready"], i + 1)
                nc.vector.tensor_scalar(veps[:, p:p + 1], aggr[:, p, 1:2], EPS, None, ALU.add).then_inc(s["veps_ready"], 1)

            def scale(i, p):
                dve.wait_ge(s["rstd_ready"], i + 1)
                if from_(i, 2):
                    dve.wait_ge(s["turned"], i - 1)
                nc.vector.tensor_scalar(xn[:, p, :].rearrange("p (n d) -> p n d", n=1), xres[:, bass.ds(i, 1), :],
                                        aggr[:, p, 0:1], rstd[:, p:p + 1], ALU.subtract, ALU.mult).then_inc(s["xn_ready"], 1)

            def kv_out(i, p):
                dve.wait_ge(s["kv_ready"], i + 1)
                if from_(i, 2):
                    dve.wait_ge(s["pv_ready"], NU * (i - 1))
                for b in range(2):
                    nc.vector.tensor_tensor(vx[:, p, b, :, 0:16],
                                            VY[:, P * b:P * b + P].rearrange("p (j w) -> p j w", j=8),
                                            bvr[:, :].rearrange("p (j w) -> p j w", j=8), ALU.add).then_inc(s["kv_out"], 1)

            def divide(i):
                dve.wait_ge(s["pv_ready"], NU * (i + 1))
                if from_(i, 1):
                    dve.wait_ge(s["ot_ready"], i)
                nc.vector.reciprocal(rc[:, :].rearrange("p (b j a) -> p b j a", b=2, j=8), o_ps[:, :, :, 16:17]).then_inc(s["rc_ready"], 1)
                dve.wait_ge(s["rc_ready"], i + 1)
                for t in range(2):
                    r = slice(64 * t, 64 * t + 64)
                    nc.vector.tensor_tensor(on[r, :, :].rearrange("p b (j d) -> p b j d", j=8), o_ps[r, :, :, 8 * t:8 * t + 8],
                                            rc[r, :].rearrange("p (b j a) -> p b j a", b=2, j=8).broadcast_to([64, 2, 8, 8]),
                                            ALU.mult).then_inc(s["on_ready"], 1)

            def add(i):
                dve.wait_ge(s["y_ready"], i + 1)
                dve.wait_ge(s["residual_ready"], i + 1)
                nc.vector.tensor_tensor(xres[:, bass.ds(i, 1), :], VY[:, 256:384].rearrange("p (n d) -> p n d", n=1),
                                        xres[:, bass.ds(i, 1), :], ALU.add).then_inc(s["x1_ready"], 1)

            def step(i, p):
                unit(i, 0)
                unit(i, 1)
                if from_(i, 2):
                    add(i - 2)
                if has(i, 2):
                    norm(i + 2, p)
                unit(i, 2)
                if has(i, 2):
                    aggregate(i + 2, p)
                if from_(i, 1):
                    divide(i - 1)
                if has(i, 1):
                    kv_out(i + 1, 1 - p)
                if has(i, 2):
                    scale(i + 2, p)
                unit(i, 3)

            def tail(i):
                add(i - 2)
                divide(i - 1)
                add(i - 1)

            dve.wait_ge(const_in, 16 * NCONST)
            dve.wait_ge(ones_set, 4)
            for i in range(2):
                norm(i, i)
                aggregate(i, i)
                scale(i, i)
            kv_out(0, 0)
            run(dve, step, tail)

        @block.tensor
        def _(pe):
            def logits(i, u, p):
                n = NU * i + u
                if u == 0:
                    pe.wait_ge(s["q_spread"], 2 * (i + 1))
                    pe.wait_ge(s["k_out"], i + 1)
                    pe.wait_ge(s["mask_ready"], i + 1)
                if from_(i, 1) or u >= 2:
                    pe.wait_ge(s["dif_ready"], n - 1)
                nc.tensor.matmul(S[u % 2][:, :], onesb[:, :],
                                 mkb[:, p, :].rearrange("p (b a k) -> p b a k", b=2, a=1).broadcast_to([P, 2, 2, SK]),
                                 start=True, stop=False)
                for b in range(2):
                    for jj in range(2):
                        c = (2 * b + jj) * SK
                        last = nc.tensor.matmul(S[u % 2][:, c:c + SK],
                                                qm[:, p, b, 4 * u + 2 * jj:4 * u + 2 * jj + 2, :].rearrange("p c q -> p (c q)"),
                                                kt[:, p, SK * b:SK * b + SK], start=False, stop=(b == 1 and jj == 1))
                last.then_inc(s["logits_ready"], 1)

            def turn_prob(i, u):
                n = NU * i + u
                pe.wait_ge(s["prob_ready"], n + 1)
                if from_(i, 1) or u >= 2:
                    pe.wait_ge(s["pt_out"], n - 1)
                for c in range(4):
                    last = nc.tensor.transpose(PT[u % 2][:, c * P:c * P + P], prob[:, u, c * P:c * P + P], ident[:, :])
                last.then_inc(s["pt_ready"], 1)

            def values(i, u, p):
                n = NU * i + u
                pe.wait_ge(s["pt_out"], n + 1)
                if u == 0:
                    pe.wait_ge(s["kv_out"], 2 * (i + 1))
                if u == 0 and from_(i, 1):
                    pe.wait_ge(s["on_ready"], 2 * i)
                for b in range(2):
                    for jj in range(2):
                        last = nc.tensor.matmul(o_ps[:, b, 2 * u + jj, :], pts[:, u, (2 * b + jj) * P:(2 * b + jj + 1) * P],
                                                vx[:, p, b, 2 * u + jj, :], start=True, stop=True)
                last.then_inc(s["pv_ready"], 1)

            def turn(i, p):
                pe.wait_ge(s["xn_ready"], i + 1)
                pe.wait_ge(tile_in[p], 48 * (half(i, p) + 1))
                if from_(i, 1):
                    pe.wait_ge(s["q_out"], i)
                for b in range(2):
                    nc.tensor.transpose(TB[:, b * P:b * P + P], cin[:, p, b, :], ident[:, :])
                nc.tensor.transpose(TB[:, 256:384], xn[:, p, :], ident[:, :]).then_inc(s["turned"], 1)

            def keys_values(i, p):
                pe.wait_ge(s["turned_out"], i + 1)
                if from_(i, 1):
                    pe.wait_ge(s["kv_out"], 2 * i)
                    pe.wait_ge(s["k_out"], i)
                if from_(i, 3):
                    pe.wait_ge(s["ot_out"], i - 2)
                    pe.wait_ge(s["x1_ready"], i - 2)
                nc.tensor.matmul(KO[:, 0:256], wk[:, :], xt[:, p, 0:256], start=True, stop=True)
                for b in range(2):
                    last = nc.tensor.matmul(VY[:, b * P:b * P + P], xt[:, p, b * P:b * P + P], wv[:, :],
                                            start=True, stop=True)
                last.then_inc(s["kv_ready"], 1)

            def queries(i, p):
                pe.wait_ge(s["turned_out"], i + 1)
                nc.tensor.matmul(TB[:, 384:512], wq[:, :], xt[:, p, 256:384], start=True, stop=True).then_inc(s["q_ready"], 1)

            def output_divided(i):
                pe.wait_ge(s["on_ready"], 2 * (i + 1))
                pe.wait_ge(s["k_out"], (i + 3) if has(i, 2) else NT)

            def turn_output(i):
                for b in range(2):
                    last = nc.tensor.transpose(KO[0:64, 256 + b * P:384 + b * P], on[:, b, :], ident[:, :])
                last.then_inc(s["ot_ready"], 1)

            def project(i):
                pe.wait_ge(s["ot_out"], i + 1)
                pe.wait_ge(s["kv_out"], 2 * (i + 3) if has(i, 2) else 2 * NT)
                for t in range(2):
                    last = nc.tensor.matmul(VY[:, 256:384], ot[:, t, :, :].rearrange("p b q -> p (b q)"), wo2[:, t, :],
                                            start=(t == 0), stop=(t == 1))
                last.then_inc(s["y_ready"], 1)

            def step(i, p):
                if from_(i, 2):
                    output_divided(i - 2)
                logits(i, 0, p)
                if from_(i, 2):
                    turn_output(i - 2)
                if from_(i, 1):
                    turn_prob(i - 1, 2)
                    values(i - 1, 1, 1 - p)
                if has(i, 1):
                    turn(i + 1, 1 - p)
                logits(i, 1, p)
                if has(i, 1):
                    queries(i + 1, 1 - p)
                if from_(i, 2):
                    project(i - 2)
                if from_(i, 1):
                    turn_prob(i - 1, 3)
                    values(i - 1, 2, 1 - p)
                if has(i, 1):
                    keys_values(i + 1, 1 - p)
                logits(i, 2, p)
                turn_prob(i, 0)
                if from_(i, 1):
                    values(i - 1, 3, 1 - p)
                logits(i, 3, p)
                turn_prob(i, 1)
                values(i, 0, p)

            def tail(i):
                turn_prob(i - 1, 2)
                values(i - 1, 1, 1)
                output_divided(i - 2)
                turn_output(i - 2)
                turn_prob(i - 1, 3)
                values(i - 1, 2, 1)
                project(i - 2)
                values(i - 1, 3, 1)
                output_divided(i - 1)
                turn_output(i - 1)
                project(i - 1)

            pe.wait_ge(const_in, 16 * NCONST)
            pe.wait_ge(ones_set, 4)
            turn(0, 0)
            keys_values(0, 0)
            queries(0, 0)
            run(pe, step, tail)


def linear_attention(nc, xres, ident, wts):
    HG, DK, DV, LR = 4, 128, 32, 16
    NB = B * SQ // 512
    T4 = 512 // P
    with ExitStack() as ctx:
        def sb(name, shape, dt=F32):
            return ctx.enter_context(nc.sbuf_tensor(name, shape, dt))

        def psum(name):
            return ctx.enter_context(nc.psum_tensor(name, [P, 512], F32))

        def sem(name):
            return ctx.enter_context(nc.semaphore(name))

        xt = sb("g_xt", [D, NB, 512])
        xs = sb("g_xs", [D, 512])
        low = sb("g_low", [LR + 1, NB, 512])
        val = sb("g_val", [P, NB, T4, P])
        silu = sb("g_silu", [P, NB, 512])
        stats, aggr = sb("g_stats", [P, T4, 6]), sb("g_aggr", [P, T4, 2])
        veps, rstd = sb("g_veps", [P, T4]), sb("g_rstd", [P, T4])
        xn = sb("g_xn", [P, T4, D])
        reset = sb("g_reset", [P, 512])
        neg, mag = (sb("g_" + n, [P, 2, 512]) for n in ("neg", "mag"))
        cum, grow, decay = (sb("g_" + n, [P, 2, 512]) for n in ("cum", "grow", "decay"))
        qg, ki, am = (sb("g_" + n, [P, 2, 512]) for n in ("qg", "ki", "am"))
        gneg, gmag = sb("g_gneg", [P, 512]), sb("g_gmag", [P, 512])
        sq, on, og = sb("g_sq", [P, 512]), sb("g_on", [P, 512]), sb("g_og", [P, 512])
        ms, meps, rms = sb("g_ms", [P, 16]), sb("g_meps", [P, 16]), sb("g_rms", [P, 16])
        halfs = sb("g_halfs", [P, 16])

        Z = [psum("gZ0"), psum("gZ1")]
        Q, K, A, O, T, V = (psum("g" + n) for n in "QKAOTV")

        s = {n: sem("g_" + n) for n in (
            "set_up", "x_kept", "stats_ready", "aggr_ready", "veps_ready", "rstd_ready", "xn_ready", "turned", "turned_out", "low_ready",
            "low_out", "v_ready", "v_out", "gate_ready", "gmag_ready", "gexp_ready", "glog_ready", "gsum_ready", "gsig_ready",
            "silu_ready", "z_ready", "mag_ready", "exp_ready", "log_ready", "tot_ready", "cum_ready", "grow_ready",
            "decay_ready", "q_ready", "k_ready", "qg_ready", "ki_ready", "a_ready", "am_ready", "o_ready", "sq_ready",
            "ms_ready", "meps_ready", "rms_ready", "on_ready", "ot_ready", "og_ready", "y_ready", "x2_ready")}
        NSET = 7
        block = ctx.enter_context(nc.Block())

        def run(eng, step, tail):
            step(0)
            step(1)
            with eng.Fori(2, NB - 2, 1) as c:
                step(c)
            step(NB - 2)
            step(NB - 1)
            tail(NB)

        def from_(c, k):
            return c >= k if isinstance(c, int) else k <= 2

        def has(c, k):
            return c + k < NB if isinstance(c, int) else k <= 2

        def cols(t, c):
            return t[:, bass.ds(c, 1), :].rearrange("p a n -> p (a n)")

        @block.gpsimd
        def _(pool):
            nc.gpsimd.memset(halfs[:, :], -0.5).then_inc(s["set_up"], 1)
            nc.gpsimd.memset(low[:, :, :], 1.0).then_inc(s["set_up"], 1)
            nc.gpsimd.memset(am[:, :, :], 0.0).then_inc(s["set_up"], 1)
            nc.gpsimd.memset(reset[:, :], 1.0).then_inc(s["set_up"], 1)
            pool.wait_ge(s["set_up"], 4)
            nc.gpsimd.memset(reset[:, 0:512:SQ], 0.0).then_inc(s["set_up"], 3)

            def keep(c):
                pool.wait_ge(s["turned_out"], c + 1)
                nc.gpsimd.tensor_copy(cols(xt, c), xs[:, :]).then_inc(s["x_kept"], 1)

            def power(c):
                pool.wait_ge(s["veps_ready"], c + 1)
                nc.gpsimd.tensor_tensor(rstd[:, :], veps[:, :], halfs[:, 0:T4], ALU.pow).then_inc(s["rstd_ready"], 1)

            def total(n, par):
                pool.wait_ge(s["log_ready"], n + 1)
                nc.gpsimd.tensor_tensor(neg[:, par, :], neg[:, par, :], mag[:, par, :], ALU.add).then_inc(s["tot_ready"], 1)

            def gate_total(c):
                pool.wait_ge(s["glog_ready"], c + 1)
                nc.gpsimd.tensor_tensor(gneg[:, :], gneg[:, :], gmag[:, :], ALU.add).then_inc(s["gsum_ready"], 1)

            def rms_power(c):
                pool.wait_ge(s["meps_ready"], c + 1)
                nc.gpsimd.tensor_tensor(rms[:, :], meps[:, :], halfs[:, :], ALU.pow).then_inc(s["rms_ready"], 1)

            def step(c):
                for h in range(HG):
                    if h < 2 or has(c, 1):
                        total(HG * c + h + 2, h % 2)
                    if h == 0 and has(c, 1):
                        keep(c + 1)
                    if h == 1 and has(c, 2):
                        power(c + 2)
                    if h == 2:
                        if from_(c, 1):
                            rms_power(c - 1)
                        if has(c, 1):
                            gate_total(c + 1)

            def tail(c):
                rms_power(c - 1)

            power(0)
            keep(0)
            gate_total(0)
            total(0, 0)
            total(1, 1)
            power(1)
            run(pool, step, tail)

        @block.scalar
        def _(act):
            def turned_out(c):
                act.wait_ge(s["turned"], c + 1)
                if from_(c, 1):
                    act.wait_ge(s["v_ready"], c)
                    act.wait_ge(s["x_kept"], c)
                nc.scalar.activation(xs[:, :], T[:, :], ACT.Copy).then_inc(s["turned_out"], 1)

            def low_out(c):
                act.wait_ge(s["low_ready"], c + 1)
                nc.scalar.activation(low[0:LR, bass.ds(c, 1), :].rearrange("p a n -> p (a n)"), T[0:LR, :], ACT.Copy).then_inc(s["low_out"], 1)

            def v_out(c):
                act.wait_ge(s["v_ready"], c + 1)
                nc.scalar.activation(val[:, bass.ds(c, 1), :, :].rearrange("p a t n -> p (a t n)"), V[:, :], ACT.Copy).then_inc(s["v_out"], 1)

            def front(n, par):
                act.wait_ge(s["z_ready"], n + 1)
                if not isinstance(n, int) or n >= 2:
                    act.wait_ge(s["cum_ready"], n - 1)
                nc.scalar.activation(neg[:, par, :], Z[par][:, :], ACT.Relu, scale=-1.0)
                nc.scalar.activation(mag[:, par, :], Z[par][:, :], ACT.Abs).then_inc(s["mag_ready"], 1)
                act.wait_ge(s["mag_ready"], n + 1)
                nc.scalar.activation(mag[:, par, :], mag[:, par, :], ACT.Exp, scale=-1.0).then_inc(s["exp_ready"], 1)
                act.wait_ge(s["exp_ready"], n + 1)
                nc.scalar.activation(mag[:, par, :], mag[:, par, :], ACT.Ln, bias=1.0).then_inc(s["log_ready"], 1)

            def back(n, par):
                act.wait_ge(s["cum_ready"], n + 1)
                if not isinstance(n, int) or n >= 2:
                    act.wait_ge(s["ki_ready"], n - 1)
                nc.scalar.activation(decay[:, par, :], cum[:, par, :], ACT.Exp, scale=-1.0 / 16).then_inc(s["decay_ready"], 1)
                nc.scalar.activation(grow[:, par, :], cum[:, par, :], ACT.Exp, scale=1.0 / 16).then_inc(s["grow_ready"], 1)

            def gate_front(c):
                act.wait_ge(s["gate_ready"], c + 1)
                if from_(c, 1):
                    act.wait_ge(s["silu_ready"], c)
                nc.scalar.activation(gneg[:, :], T[:, :], ACT.Relu, scale=-1.0)
                nc.scalar.activation(gmag[:, :], T[:, :], ACT.Abs).then_inc(s["gmag_ready"], 1)
                act.wait_ge(s["gmag_ready"], c + 1)
                nc.scalar.activation(gmag[:, :], gmag[:, :], ACT.Exp, scale=-1.0).then_inc(s["gexp_ready"], 1)
                act.wait_ge(s["gexp_ready"], c + 1)
                nc.scalar.activation(gmag[:, :], gmag[:, :], ACT.Ln, bias=1.0).then_inc(s["glog_ready"], 1)

            def gate_sigmoid(c):
                act.wait_ge(s["gsum_ready"], c + 1)
                nc.scalar.activation(gneg[:, :], gneg[:, :], ACT.Exp, scale=-1.0).then_inc(s["gsig_ready"], 1)

            def square(c):
                act.wait_ge(s["o_ready"], HG * (c + 1))
                if from_(c, 1):
                    act.wait_ge(s["ms_ready"], c)
                nc.scalar.activation(sq[:, :], O[:, :], ACT.Square).then_inc(s["sq_ready"], 1)

            def step(c):
                for h in range(HG):
                    n = HG * c + h
                    if h < 2 or has(c, 1):
                        front(n + 2, h % 2)
                    if h == 1 and from_(c, 1):
                        square(c - 1)
                    if h < 3 or has(c, 1):
                        back(n + 1, (h + 1) % 2)
                    if has(c, 1):
                        if h == 0:
                            turned_out(c + 1)
                        if h == 1:
                            low_out(c + 1)
                        if h == 2:
                            gate_front(c + 1)
                        if h == 3:
                            v_out(c + 1)
                            gate_sigmoid(c + 1)

            def tail(c):
                square(c - 1)

            turned_out(0)
            low_out(0)
            gate_front(0)
            v_out(0)
            gate_sigmoid(0)
            front(0, 0)
            front(1, 1)
            back(0, 0)
            run(act, step, tail)

        @block.vector
        def _(dve):
            def norm(c):
                for t in range(T4):
                    last = nc.vector.bn_stats(stats[:, t, :], xres[:, bass.ds(c * T4 + t, 1), :].rearrange("p n d -> p (n d)"))
                last.then_inc(s["stats_ready"], 1)
                dve.wait_ge(s["stats_ready"], c + 1)

            def aggregate(c):
                for t in range(T4):
                    last = nc.vector.bn_aggr(aggr[:, t, :], stats[:, t, :])
                last.then_inc(s["aggr_ready"], 1)
                dve.wait_ge(s["aggr_ready"], c + 1)
                nc.vector.tensor_scalar(veps[:, :], aggr[:, :, 1], EPS, None, ALU.add).then_inc(s["veps_ready"], 1)

            def unit(n, par, c):
                dve.wait_ge(s["decay_ready"], n + 1)
                dve.wait_ge(s["q_ready"], n + 1)
                if not isinstance(n, int) or n >= 2:
                    dve.wait_ge(s["a_ready"], n - 1)
                nc.vector.scalar_tensor_tensor(out=qg[:, par, :], in0=Q[:, :], scalar=DK ** -0.5, in1=decay[:, par, :],
                                               op0=ALU.mult, op1=ALU.mult).then_inc(s["qg_ready"], 1)
                dve.wait_ge(s["grow_ready"], n + 1)
                dve.wait_ge(s["k_ready"], n + 1)
                nc.vector.tensor_tensor(ki[:, par, :], K[:, :], grow[:, par, :], ALU.mult).then_inc(s["ki_ready"], 1)

            def scan(n, par):
                dve.wait_ge(s["tot_ready"], n + 1)
                if not isinstance(n, int) or n >= 2:
                    dve.wait_ge(s["grow_ready"], n - 1)
                nc.vector.tensor_tensor_scan(cum[:, par, :], reset[:, :], neg[:, par, :], 0.0, ALU.mult, ALU.add).then_inc(s["cum_ready"], 1)

            def mask_waits(n):
                dve.wait_ge(s["a_ready"], n + 1)
                if not isinstance(n, int) or n >= 2:
                    dve.wait_ge(s["o_ready"], n - 1)

            def mask(n, par):
                nc.vector.copy_predicated(am[:, par, :].rearrange("p (t i) -> p t i", t=T4),
                                          wts["causal"][:, :].rearrange("p (a i) -> p a i", a=1).broadcast_to([P, T4, P]),
                                          A[:, :].rearrange("p (t i) -> p t i", t=T4)).then_inc(s["am_ready"], 1)

            def make_silu(c):
                dve.wait_ge(s["gsig_ready"], c + 1)
                nc.vector.tensor_tensor(cols(silu, c), T[:, :], gneg[:, :], ALU.mult).then_inc(s["silu_ready"], 1)

            def mean_square(c):
                dve.wait_ge(s["sq_ready"], c + 1)
                nc.vector.tensor_reduce(ms[:, :], sq[:, :].rearrange("p (a v) -> p a v", v=DV), AX.X, ALU.add).then_inc(s["ms_ready"], 1)
                dve.wait_ge(s["ms_ready"], c + 1)
                nc.vector.tensor_scalar(meps[:, :], ms[:, :], 1.0 / DV, EPS, ALU.mult, ALU.add).then_inc(s["meps_ready"], 1)

            def over_rms(c):
                dve.wait_ge(s["rms_ready"], c + 1)
                if from_(c, 1):
                    dve.wait_ge(s["ot_ready"], c)
                nc.vector.tensor_tensor(on[:, :].rearrange("p (a v) -> p a v", v=DV), O[:, :].rearrange("p (a v) -> p a v", v=DV),
                                        rms[:, :].rearrange("p (a b) -> p a b", b=1).broadcast_to([P, 16, DV]),
                                        ALU.mult).then_inc(s["on_ready"], 1)

            def gate(c):
                dve.wait_ge(s["ot_ready"], c + 1)
                dve.wait_ge(s["silu_ready"], c + 1)
                if from_(c, 1):
                    dve.wait_ge(s["y_ready"], c)
                nc.vector.scalar_tensor_tensor(out=og[:, :], in0=T[:, :], scalar=wts["gnw"][:, :], in1=cols(silu, c),
                                               op0=ALU.mult, op1=ALU.mult).then_inc(s["og_ready"], 1)

            def add(c):
                dve.wait_ge(s["y_ready"], c + 1)
                xb = xres[:, bass.ds(c * T4, T4), :]
                nc.vector.tensor_tensor(xb, V[:, :].rearrange("p (t n) -> p t n", t=T4), xb, ALU.add).then_inc(s["x2_ready"], 1)

            def scale(c):
                dve.wait_ge(s["rstd_ready"], c + 1)
                if from_(c, 1):
                    dve.wait_ge(s["turned"], c)
                for t in range(T4):
                    last = nc.vector.tensor_scalar(xn[:, t:t + 1, :], xres[:, bass.ds(c * T4 + t, 1), :],
                                                   aggr[:, t, 0:1], rstd[:, t:t + 1], ALU.subtract, ALU.mult)
                last.then_inc(s["xn_ready"], 1)

            def step(c):
                for h in range(HG):
                    n = HG * c + h
                    unit(n, h % 2, c)
                    if h > 0 or from_(c, 1):
                        mask_waits(n - 1)
                    if h < 3 or has(c, 1):
                        scan(n + 1, (h + 1) % 2)
                    if h > 0 or from_(c, 1):
                        mask(n - 1, (h + 1) % 2)
                    if h == 1 and from_(c, 2):
                        add(c - 2)
                    if h == 2 and from_(c, 1):
                        mean_square(c - 1)
                        over_rms(c - 1)
                    if h == 3:
                        if has(c, 1):
                            make_silu(c + 1)
                        if from_(c, 1):
                            gate(c - 1)
                    if h == 0 and has(c, 2):
                        norm(c + 2)
                    if h == 1 and has(c, 2):
                        aggregate(c + 2)
                    if h == 2 and has(c, 2):
                        scale(c + 2)

            def tail(c):
                mask_waits(HG * c - 1)
                mask(HG * c - 1, 1)
                add(c - 2)
                mean_square(c - 1)
                over_rms(c - 1)
                gate(c - 1)
                add(c - 1)

            dve.wait_ge(s["set_up"], NSET)
            dve.wait_ge(wts["loaded"], wts["nload"])
            for c in range(2):
                norm(c)
                aggregate(c)
                scale(c)
            make_silu(0)
            scan(0, 0)
            run(dve, step, tail)

        @block.tensor
        def _(pe):
            def turn(c):
                pe.wait_ge(s["xn_ready"], c + 1)
                if from_(c, 3) or not isinstance(c, int):
                    pe.wait_ge(s["og_ready"], c - 2)
                elif from_(c, 1):
                    pe.wait_ge(s["silu_ready"], c)
                for t in range(T4):
                    last = nc.tensor.transpose(T[:, t * P:t * P + P], xn[:, t, :], ident[:, :])
                last.then_inc(s["turned"], 1)

            def gate_low_rank(c):
                pe.wait_ge(s["turned_out"], c + 1)
                nc.tensor.matmul(T[0:LR, :], wts["wgk1"][:, :], xs[:, :], start=True, stop=True).then_inc(s["low_ready"], 1)

            def gate_values(c):
                pe.wait_ge(s["low_out"], c + 1)
                nc.tensor.matmul(T[:, :], wts["wg"][:, :], xs[:, :], start=True, stop=True).then_inc(s["gate_ready"], 1)
                if from_(c, 3) or not isinstance(c, int):
                    pe.wait_ge(s["x2_ready"], c - 2)
                elif from_(c, 1):
                    pe.wait_ge(s["v_out"], c)
                for t in range(T4):
                    last = nc.tensor.matmul(V[:, t * P:t * P + P], xs[:, t * P:t * P + P], wts["wv"][:, :], start=True, stop=True)
                last.then_inc(s["v_ready"], 1)

            def log_gates(n, par, c, h):
                nc.tensor.matmul(Z[par][:, :], wts["wgk2"][:, h * P:h * P + P], cols(low, c), start=True, stop=True).then_inc(s["z_ready"], 1)

            def queries_keys(n, c, h):
                if h == 0:
                    pe.wait_ge(s["x_kept"], c + 1)
                if not isinstance(n, int) or n >= 1:
                    pe.wait_ge(s["qg_ready"], n)
                nc.tensor.matmul(Q[:, :], wts["wq"][:, h * P:h * P + P], cols(xt, c), start=True, stop=True).then_inc(s["q_ready"], 1)
                if not isinstance(n, int) or n >= 1:
                    pe.wait_ge(s["ki_ready"], n)
                if h < 2 or has(c, 1):
                    pe.wait_ge(s["mag_ready"], n + 1)
                    if h == 2:
                        pe.wait_ge(s["low_out"], c + 2)
                nc.tensor.matmul(K[:, :], wts["wk"][:, h * P:h * P + P], cols(xt, c), start=True, stop=True).then_inc(s["k_ready"], 1)

            def products(n, par):
                pe.wait_ge(s["ki_ready"], n + 1)
                if not isinstance(n, int) or n >= 1:
                    pe.wait_ge(s["am_ready"], n)
                for t in range(T4):
                    r = slice(t * P, t * P + P)
                    last = nc.tensor.matmul(A[:, r], ki[:, par, r], qg[:, par, r], start=True, stop=True)
                last.then_inc(s["a_ready"], 1)

            def outputs(n, par, c, h):
                pe.wait_ge(s["am_ready"], n + 1)
                if h == 0 and from_(c, 1):
                    pe.wait_ge(s["on_ready"], c)
                for t in range(T4):
                    last = nc.tensor.matmul(O[:, t * P + h * DV:t * P + h * DV + DV], am[:, par, t * P:t * P + P],
                                            val[:, bass.ds(c, 1), t, h * DV:h * DV + DV].rearrange("p a v -> p (a v)"),
                                            start=True, stop=True)
                last.then_inc(s["o_ready"], 1)

            def turn_output(c):
                pe.wait_ge(s["on_ready"], c + 1)
                pe.wait_ge(s["silu_ready"], c + 3 if has(c, 2) else NB)
                if isinstance(c, int) and c == NB - 1:
                    pe.wait_ge(s["og_ready"], c)
                for t in range(T4):
                    last = nc.tensor.transpose(T[:, t * P:t * P + P], on[:, t * P:t * P + P], ident[:, :])
                last.then_inc(s["ot_ready"], 1)

            def project(c):
                pe.wait_ge(s["og_ready"], c + 1)
                pe.wait_ge(s["v_out"], c + 3 if has(c, 2) else NB)
                if isinstance(c, int) and c == NB - 1:
                    pe.wait_ge(s["x2_ready"], c)
                for t in range(T4):
                    last = nc.tensor.matmul(V[:, t * P:t * P + P], og[:, t * P:t * P + P], wts["wo"][:, :], start=True, stop=True)
                last.then_inc(s["y_ready"], 1)

            def step(c):
                for h in range(HG):
                    n = HG * c + h
                    queries_keys(n, c, h)
                    if h < 2:
                        log_gates(n + 2, h % 2, c, h + 2)
                    elif has(c, 1):
                        log_gates(n + 2, h % 2, c + 1, h - 2)
                    if h > 0 or from_(c, 1):
                        products(n - 1, (h + 1) % 2)
                    if h > 1:
                        outputs(n - 2, h % 2, c, h - 2)
                    elif from_(c, 1):
                        outputs(n - 2, h % 2, c - 1, h + 2)
                    if h == 0:
                        if from_(c, 2):
                            project(c - 2)
                        if has(c, 1):
                            turn(c + 1)
                    if h == 1 and has(c, 1):
                        gate_low_rank(c + 1)
                    if h == 2 and has(c, 1):
                        gate_values(c + 1)
                    if h == 3 and from_(c, 1):
                        turn_output(c - 1)

            def tail(c):
                products(HG * c - 1, 1)
                outputs(HG * c - 2, 0, c - 1, 2)
                project(c - 2)
                outputs(HG * c - 1, 1, c - 1, 3)
                turn_output(c - 1)
                project(c - 1)

            pe.wait_ge(s["set_up"], NSET)
            pe.wait_ge(wts["loaded"], wts["nload"])
            turn(0)
            gate_low_rank(0)
            gate_values(0)
            pe.wait_ge(s["low_out"], 1)
            log_gates(0, 0, 0, 0)
            log_gates(1, 1, 0, 1)
            run(pe, step, tail)


def experts(nc, rows, xres, ident, wts, slots, out):
    NE, F = 8, 512
    NS = (B * SQ + NE * (P - 1)) // P
    FC = F // P
    NB, T4 = NT // 4, 4
    out_rows = out.rearrange("b s d -> (b s) d")
    slot_rows = slots.rearrange("(n p) w -> n p w", p=P)
    with ExitStack() as ctx:
        def sb(name, shape, dt=F32):
            return ctx.enter_context(nc.sbuf_tensor(name, shape, dt))

        def psum(name):
            return ctx.enter_context(nc.psum_tensor(name, [P, 512], F32))

        def sem(name):
            return ctx.enter_context(nc.semaphore(name))

        stats, aggr = sb("e_stats", [P, T4, 6]), sb("e_aggr", [P, T4, 2])
        veps, rstd, halfs = sb("e_veps", [P, T4]), sb("e_rstd", [P, T4]), sb("e_halfs", [P, T4])
        xt = sb("e_xt", [D, 512])
        lg, dif, ex, eq, hot = (sb("e_" + n, [P, NT, NE]) for n in ("lg", "dif", "ex", "eq", "hot"))
        mx, ssum, first, pos = (sb("e_" + n, [P, NT]) for n in ("mx", "ssum", "first", "pos"))
        posi = sb("e_posi", [P, NT], I32)
        cnt, inc = sb("e_cnt", [P, NE, NT]), sb("e_inc", [P, NE, NT])
        num, base = sb("e_num", [P, NE]), sb("e_base", [P, NE])
        numi = sb("e_numi", [P, NE], I32)
        ends, ones = sb("e_ends", [P, NE]), sb("e_ones", [P, NE])
        start = sb("e_start", [P, NT, NE])
        below = sb("e_below", [P, NS, NE])
        who, whoi = sb("e_who", [P, NS]), sb("e_whoi", [P, NS], I32)
        sx, sr = sb("e_sx", [P, 2, D]), sb("e_sr", [P, 2, D + 2])
        sxt = sb("e_sxt", [D, 2, P])
        act_a, act_h, act_t = sb("e_a", [P, 2, F]), sb("e_h", [P, 2, F]), sb("e_t", [P, 2, FC, P])
        fin = sb("e_fin", [P, 2, D])

        XT, AT, Y, LG = psum("eXT"), psum("eAT"), psum("eY"), psum("eLG")
        HA, HG = [psum("eHA0"), psum("eHA1")], [psum("eHG0"), psum("eHG1")]

        s = {n: sem("e_" + n) for n in (
            "set_up", "stats_ready", "aggr_ready", "veps_ready", "rstd_ready", "xn_ready", "turned", "turned_out",
            "logits_ready", "route", "exp_ready", "ranks_ready", "chain", "sorted", "scattered", "rest_in", "who_ready",
            "sx_turned", "sx_out", "h_ready", "silu_ready", "act_ready", "at_ready", "at_out", "y_ready", "fin_ready",
            "stored", "passed")}
        sx_in, sr_in = [sem("e_sx_in0"), sem("e_sx_in1")], [sem("e_sr_in0"), sem("e_sr_in1")]
        block = ctx.enter_context(nc.Block())

        def run(eng, step, tail):
            for j in range(3):
                step(j, j % 2)
            with eng.Fori(3, NS - 2, 2) as j:
                step(j, 1)
                step(j + 1, 0)
            for j in range(NS - 2, NS):
                step(j, j % 2)
            tail(NS)

        def from_(j, k):
            return j >= k if isinstance(j, int) else True

        def has(j, k):
            return j + k < NS if isinstance(j, int) else True

        def half(j, p):
            return j // 2 if isinstance(j, int) else (j - p) // 2

        @block.sync
        def _(sp):
            def load(j, p):
                if from_(j, 2):
                    sp.wait_ge(s["sx_turned"], j - 1)
                sp.dma_start(sx[:, p, :], slot_rows[bass.ds(j, 1), :, 0:D].rearrange("n p w -> (n p) w")).then_inc(sx_in[p], 16)

            def load_rest(j, p):
                if from_(j, 2):
                    sp.wait_ge(s["stored"], 16 * (j - 1))
                sp.dma_start(sr[:, p, :], slot_rows[bass.ds(j, 1), :, D:2 * D + 2].rearrange("n p w -> (n p) w")).then_inc(sr_in[p], 16)

            def step(j, p):
                load(j, p)
                if from_(j, 1):
                    load_rest(j - 1, 1 - p)

            sp.wait_ge(s["scattered"], 16 * NT)
            run(sp, step, lambda j: load_rest(j - 1, (NS - 1) % 2))

        @block.gpsimd
        def _(pool):
            nc.gpsimd.memset(halfs[:, :], -0.5).then_inc(s["set_up"], 1)
            nc.gpsimd.memset(ones[:, :], 1.0).then_inc(s["set_up"], 1)
            pool.wait_ge(s["set_up"], 2)
            for c in range(NB):
                pool.wait_ge(s["veps_ready"], c + 1)
                nc.gpsimd.tensor_tensor(rstd[:, :], veps[:, :], halfs[:, :], ALU.pow).then_inc(s["rstd_ready"], 1)
            nc.gpsimd.tensor_copy(rows[:, :, 2 * D:2 * D + 1].bitcast(I32).rearrange("p t a -> p (t a)"), wts["token"][:, :]).then_inc(s["set_up"], 1)
            pool.wait_ge(s["set_up"], 3)
            pool.wait_ge(wts["cleared"], 16)
            pool.wait_ge(s["sorted"], 1)
            for t in range(NT):
                nc.gpsimd.indirect_dma_start(out=slots, out_offset=bass.IndirectOffsetOnAxis(ap=posi[:, t:t + 1], axis=0),
                                             in_=rows[:, t, :], in_offset=None).then_inc(s["scattered"], 16)

            held = pool.alloc_register("last_token")
            pool.reg_mov(held, B * SQ - 1)
            last_token = pool.snap(held, min_val=0, max_val=B * SQ - 1)

            def store(j, p):
                pool.wait_ge(s["fin_ready"], j + 1)
                if from_(j, 1):
                    pool.wait_ge(s["stored"], 16 * j)
                pool.sem_inc(s["passed"], 1)
                nc.gpsimd.indirect_dma_start(
                    out=out_rows, out_offset=bass.IndirectOffsetOnAxis(ap=sr[:, p, D:D + 1].bitcast(I32), axis=0),
                    in_=fin[:, p, :], in_offset=None, bounds_check=last_token, oob_is_err=False).then_inc(s["stored"], 16)

            run(pool, store, lambda j: pool.wait_ge(s["stored"], 16 * NS))

        @block.scalar
        def _(act):
            for c in range(NB):
                act.wait_ge(s["turned"], c + 1)
                if c:
                    act.wait_ge(s["logits_ready"], c)
                nc.scalar.activation(xt[:, :], XT[:, :], ACT.Copy).then_inc(s["turned_out"], 1)
            act.wait_ge(s["route"], 3)
            nc.scalar.activation(ex[:, :, :], dif[:, :, :], ACT.Exp).then_inc(s["exp_ready"], 1)
            act.preload_act_table_set("silu_and_others")

            def step(j, p):
                act.wait_ge(s["sx_turned"], j + 1)
                if from_(j, 2):
                    act.wait_ge(s["h_ready"], j - 1)
                nc.scalar.activation(sxt[:, p, :], XT[:, 0:P], ACT.Copy).then_inc(s["sx_out"], 1)
                if from_(j, 1):
                    silu(j - 1, 1 - p)

            def silu(j, p):
                act.wait_ge(s["h_ready"], j + 1)
                if from_(j, 2):
                    act.wait_ge(s["act_ready"], j - 1)
                nc.scalar.activation(act_a[:, p, :], HA[p][:, :], ACT.Silu).then_inc(s["silu_ready"], 1)
                if from_(j, 1):
                    at_out(j - 1, 1 - p)

            def at_out(j, p):
                act.wait_ge(s["at_ready"], j + 1)
                if from_(j, 2):
                    act.wait_ge(s["y_ready"], j - 1)
                nc.scalar.activation(act_t[:, p, :, :], AT[:, :].rearrange("p (c k) -> p c k", c=FC), ACT.Copy).then_inc(s["at_out"], 1)

            def tail(j):
                silu(j - 1, (NS - 1) % 2)
                at_out(j - 1, (NS - 1) % 2)

            run(act, step, tail)

        @block.vector
        def _(dve):
            for c in range(NB):
                for t in range(T4):
                    last = nc.vector.bn_stats(stats[:, t, :], xres[:, c * T4 + t, :])
                last.then_inc(s["stats_ready"], 1)
                dve.wait_ge(s["stats_ready"], c + 1)
                for t in range(T4):
                    last = nc.vector.bn_aggr(aggr[:, t, :], stats[:, t, :])
                last.then_inc(s["aggr_ready"], 1)
                dve.wait_ge(s["aggr_ready"], c + 1)
                nc.vector.tensor_scalar(veps[:, :], aggr[:, :, 1], EPS, None, ALU.add).then_inc(s["veps_ready"], 1)
                dve.wait_ge(s["rstd_ready"], c + 1)
                for t in range(T4):
                    last = nc.vector.tensor_scalar(rows[:, c * T4 + t, 0:D], xres[:, c * T4 + t, :], aggr[:, t, 0:1],
                                                   rstd[:, t:t + 1], ALU.subtract, ALU.mult)
                last.then_inc(s["xn_ready"], 1)

            done = [0]

            def then(ins):
                done[0] += 1
                ins.then_inc(s["chain"], 1)
                dve.wait_ge(s["chain"], done[0])

            def over(ap, shape):
                return ap.broadcast_to(shape)

            dve.wait_ge(s["logits_ready"], NB)
            then(nc.vector.tensor_tensor(lg[:, :, :], LG[:, 0:NT * NE].rearrange("p (t e) -> p t e", e=NE),
                                         over(wts["rb"][:, :].rearrange("p (a e) -> p a e", a=1), [P, NT, NE]), ALU.add))
            then(nc.vector.tensor_reduce(mx[:, :], lg[:, :, :], AX.X, ALU.max))
            nc.vector.tensor_tensor(dif[:, :, :], lg[:, :, :], over(mx[:, :].rearrange("p (t a) -> p t a", a=1), [P, NT, NE]),
                                    ALU.subtract).then_inc(s["route"], 3)
            dve.wait_ge(s["route"], 3)
            then(nc.vector.scalar_tensor_tensor(out=eq[:, :, :], in0=dif[:, :, :], scalar=0.0,
                                                in1=over(wts["order"][:, :].rearrange("p (a e) -> p a e", a=1), [P, NT, NE]),
                                                op0=ALU.is_equal, op1=ALU.mult))
            then(nc.vector.tensor_reduce(first[:, :], eq[:, :, :], AX.X, ALU.min))
            nc.vector.tensor_tensor(hot[:, :, :], over(first[:, :].rearrange("p (t a) -> p t a", a=1), [P, NT, NE]),
                                    over(wts["order"][:, :].rearrange("p (a e) -> p a e", a=1), [P, NT, NE]),
                                    ALU.is_equal).then_inc(s["route"], 1)
            dve.wait_ge(s["exp_ready"], 1)
            then(nc.vector.tensor_reduce(ssum[:, :], ex[:, :, :], AX.X, ALU.add))
            then(nc.vector.reciprocal(rows[:, :, 2 * D + 1], ssum[:, :]))
            dve.wait_ge(s["ranks_ready"], 1)
            then(nc.vector.tensor_copy(cnt[:, :, :], LG[:, 256:512].rearrange("p (t e) -> p e t", e=NE)))
            then(nc.vector.tensor_tensor_scan(inc[:, :, :].rearrange("p e t -> p (e t)"), wts["again"][:, :],
                                              cnt[:, :, :].rearrange("p e t -> p (e t)"), 0.0, ALU.mult, ALU.add))
            then(nc.vector.tensor_scalar(numi[:, :], inc[:, :, NT - 1], float(P - 1), None, ALU.add))
            then(nc.vector.tensor_scalar(numi[:, :], numi[:, :], 7, None, ALU.arith_shift_right))
            then(nc.vector.tensor_copy(num[:, :], numi[:, :]))
            then(nc.vector.tensor_tensor_scan(ends[:, :], ones[:, :], num[:, :], 0.0, ALU.mult, ALU.add))
            then(nc.vector.tensor_tensor(base[:, :], ends[:, :], num[:, :], ALU.subtract))
            then(nc.vector.tensor_tensor(start[:, :, :].rearrange("p t e -> p e t"), inc[:, :, :], cnt[:, :, :], ALU.subtract))
            then(nc.vector.scalar_tensor_tensor(out=start[:, :, :], in0=over(base[:, :].rearrange("p (a e) -> p a e", a=1), [P, NT, NE]),
                                                scalar=float(P), in1=start[:, :, :], op0=ALU.mult, op1=ALU.add))
            then(nc.vector.tensor_tensor(start[:, :, :], LG[:, 0:256].rearrange("p (t e) -> p t e", e=NE), start[:, :, :], ALU.add))
            then(nc.vector.tensor_tensor(start[:, :, :], start[:, :, :], hot[:, :, :], ALU.mult))
            then(nc.vector.tensor_reduce(pos[:, :], start[:, :, :], AX.X, ALU.add))
            nc.vector.tensor_copy(posi[:, :], pos[:, :]).then_inc(s["sorted"], 1)
            then(nc.vector.tensor_tensor(below[:, :, :], over(ends[:, :].rearrange("p (a e) -> p a e", a=1), [P, NS, NE]),
                                         over(wts["tiles"][:, :].rearrange("p (j a) -> p j a", a=1), [P, NS, NE]), ALU.is_le))
            then(nc.vector.tensor_reduce(who[:, :], below[:, :, :], AX.X, ALU.add))
            nc.vector.tensor_scalar(whoi[:, :], who[:, :], float(NE - 1), None, ALU.min).then_inc(s["who_ready"], 1)

            def gate(j, p):
                dve.wait_ge(s["silu_ready"], j + 1)
                if from_(j, 2):
                    dve.wait_ge(s["at_ready"], j - 1)
                nc.vector.tensor_tensor(act_h[:, p, :], HG[p][:, :], act_a[:, p, :], ALU.mult).then_inc(s["act_ready"], 1)

            def finish(j, p):
                dve.wait_ge(s["y_ready"], j + 1)
                dve.wait_ge(sr_in[p], 16 * (half(j, p) + 1))
                if from_(j, 2):
                    dve.wait_ge(s["stored"], 16 * (j - 1))
                nc.vector.scalar_tensor_tensor(out=fin[:, p, :], in0=Y[:, 0:D], scalar=sr[:, p, D + 1:D + 2],
                                               in1=sr[:, p, 0:D], op0=ALU.mult, op1=ALU.add).then_inc(s["fin_ready"], 1)

            def step(j, p):
                gate(j, p)
                if from_(j, 2):
                    finish(j - 2, p)

            def tail(j):
                finish(j - 2, (NS - 2) % 2)
                finish(j - 1, (NS - 1) % 2)

            run(dve, step, tail)

        @block.tensor
        def _(pe):
            for c in range(NB + 1):
                if c < NB:
                    pe.wait_ge(s["xn_ready"], c + 1)
                    if c:
                        pe.wait_ge(s["turned_out"], c)
                    for t in range(T4):
                        last = nc.tensor.transpose(XT[:, t * P:t * P + P], rows[:, c * T4 + t, 0:D], ident[:, :])
                    last.then_inc(s["turned"], 1)
                if c < NB:
                    pe.wait_ge(s["turned_out"], c + 1)
                    for t in range(T4):
                        last = nc.tensor.matmul(LG[:, (c * T4 + t) * NE:(c * T4 + t + 1) * NE], xt[:, t * P:t * P + P],
                                                wts["rw"][:, :], start=True, stop=True)
                    last.then_inc(s["logits_ready"], 1)
            pe.wait_ge(s["route"], 4)
            nc.tensor.matmul(LG[:, 0:256], wts["before"][:, :], hot[:, :, :].rearrange("p t e -> p (t e)"), start=True, stop=True)
            nc.tensor.matmul(LG[:, 256:512], wts["all"][:, :], hot[:, :, :].rearrange("p t e -> p (t e)"),
                             start=True, stop=True).then_inc(s["ranks_ready"], 1)
            pe.wait_ge(s["who_ready"], 1)

            def turn(j, p):
                pe.wait_ge(sx_in[p], 16 * (half(j, p) + 1))
                if from_(j, 1):
                    pe.wait_ge(s["sx_out"], j)
                nc.tensor.transpose(XT[:, 0:P], sx[:, p, :], ident[:, :]).then_inc(s["sx_turned"], 1)

            def up(j, p):
                e = pe.value_load(whoi[0:1, bass.ds(j, 1)], min_val=0, max_val=NE - 1)
                pe.wait_ge(s["sx_out"], j + 1)
                if from_(j, 2):
                    pe.wait_ge(s["act_ready"], j - 1)
                nc.tensor.matmul(HA[p][:, :], sxt[:, p, :], wts["w1"][:, bass.ds(e, 1), 0:F].rearrange("p a f -> p (a f)"),
                                 start=True, stop=True)
                nc.tensor.matmul(HG[p][:, :], sxt[:, p, :], wts["w1"][:, bass.ds(e, 1), F:2 * F].rearrange("p a f -> p (a f)"),
                                 start=True, stop=True).then_inc(s["h_ready"], 1)

            def turn_act(j, p):
                pe.wait_ge(s["act_ready"], j + 1)
                if from_(j, 1):
                    pe.wait_ge(s["at_out"], j)
                for f in range(FC):
                    last = nc.tensor.transpose(AT[:, f * P:f * P + P], act_h[:, p, f * P:f * P + P], ident[:, :])
                last.then_inc(s["at_ready"], 1)

            def down(j, p):
                e = pe.value_load(whoi[0:1, bass.ds(j, 1)], min_val=0, max_val=NE - 1)
                pe.wait_ge(s["at_out"], j + 1)
                if from_(j, 1):
                    pe.wait_ge(s["fin_ready"], j)
                for f in range(FC):
                    last = nc.tensor.matmul(Y[:, 0:D], act_t[:, p, f, :], wts["w2"][:, bass.ds(e, 1), f, :].rearrange("p a n -> p (a n)"),
                                            start=(f == 0), stop=(f == FC - 1))
                last.then_inc(s["y_ready"], 1)

            def step(j, p):
                if has(j, 1):
                    turn(j + 1, 1 - p)
                up(j, p)
                if from_(j, 1):
                    turn_act(j - 1, 1 - p)
                if from_(j, 2):
                    down(j - 2, p)

            def tail(j):
                turn_act(j - 1, (NS - 1) % 2)
                down(j - 2, (NS - 2) % 2)
                down(j - 1, (NS - 1) % 2)

            turn(0, 0)
            run(pe, step, tail)


def layer(nc, t, out):
    NE, F = 8, 512
    NS = (B * SQ + NE * (P - 1)) // P
    slots = nc.dram_tensor("slots", (NS * P, ROW), F32).ap()
    with ExitStack() as ctx:
        def sb(name, shape, dt=F32):
            return ctx.enter_context(nc.sbuf_tensor(name, shape, dt))

        rows = sb("rows", [P, NT, ROW])
        xres = rows[:, :, D:2 * D]
        ident = sb("ident", [P, P])
        wts = {"wq": sb("a_wq", [D, 512]), "wk": sb("a_wk", [D, 512]), "wv": sb("a_wv", [D, P]), "wg": sb("a_wg", [D, P]),
               "wo": sb("a_wo", [P, D]), "wgk1": sb("a_wgk1", [D, 16]), "wgk2": sb("a_wgk2", [17, 512]), "gnw": sb("a_gnw", [P, 1]),
               "causal": sb("causal", [P, P], I32), "w1": sb("w1", [D, NE, 2 * F]), "w2": sb("w2", [P, NE, F // P, D]),
               "rw": sb("rw", [D, NE]), "rb": sb("rb", [P, NE]), "order": sb("order", [P, NE]), "again": sb("again", [P, NE * NT]),
               "before": sb("before", [P, P]), "all": sb("all", [P, P]), "tiles": sb("tiles", [P, NS]),
               "token": sb("token", [P, NT], I32)}
        later = [(wts[k][:, :], t["L0_attn_" + n]) for k, n in (("wq", "Wq"), ("wk", "Wk"), ("wv", "Wv"), ("wg", "Wg"), ("wo", "Wo"), ("wgk1", "Wgk1"))]
        later += [(wts["wgk2"][0:16, :], t["L0_attn_Wgk2"]), (wts["wgk2"][16:17, :], t["L0_attn_bgk2"].rearrange("(a n) -> a n", a=1))]
        later += [(wts["gnw"][32 * h:32 * h + 32, :], t["L0_attn_gnw"].rearrange("(p a) -> p a", a=1)) for h in range(4)]
        later += [(wts["rw"][:, :], t["L0_ffn_router_w"]), (wts["rb"][:, :], t["L0_ffn_router_b"].rearrange("(a n) -> a n", a=1).broadcast_to([P, NE]))]
        later += [(wts[k][:, :], t[k]) for k in ("causal", "order", "again", "before", "all", "tiles", "token")]
        later += [(wts["w1"][:, 2 * e:2 * e + 2, :], t["L0_ffn_w1"][2 * e:2 * e + 2].rearrange("e d f -> d e f")) for e in range(NE // 2)]
        later += [(wts["w2"][:, 4 * e:4 * e + 4, :, :].rearrange("p e c n -> p (e c) n"),
                   t["L0_ffn_w2"][4 * e:4 * e + 4].rearrange("e (c p) n -> p (e c) n", p=P)) for e in range(NE // 4)]
        wts["loaded"] = ctx.enter_context(nc.semaphore("weights_loaded"))
        wts["cleared"] = ctx.enter_context(nc.semaphore("slots_cleared"))
        wts["nload"] = 16 * len(later)
        cross_attention(nc, rows, xres, ident, wts, slots, later, t["x"], t["ctx_1024"], t["mask_Bx1x1xS2_ik0"],
                        *(t["L0_xattn_" + n] for n in ("Wq", "bq", "Wk", "bk", "Wv", "bv", "Wo", "bo")), t["ident"], t["heads"])
        linear_attention(nc, xres, ident, wts)
        experts(nc, rows, xres, ident, wts, slots, out)


def kernel(**inputs):
    import numpy as np
    import concourse.bacc as bacc
    from concourse.bass_utils import run_bass_kernel_spmd as launch

    f = np.float32
    p, q, e = np.arange(P)[:, None], np.arange(P)[None, :], np.arange(8)[None, :]
    ns = (B * SQ + 8 * (P - 1)) // P
    arrays = {n: np.ascontiguousarray(a) for n, a in inputs.items()}
    arrays["ident"] = np.eye(P, dtype=f)
    arrays["heads"] = ((p // DH == np.arange(H)[None, :]) * f(SCALE)).astype(f)
    arrays["causal"] = ((p // SQ == q // SQ) & (q >= p)).astype(np.int32)
    arrays["order"] = np.ascontiguousarray(np.broadcast_to(e - 8, (P, 8))).astype(f)
    arrays["again"] = np.ascontiguousarray(np.broadcast_to(np.arange(8 * NT)[None, :] % NT != 0, (P, 8 * NT))).astype(f)
    arrays["before"] = (p < q).astype(f)
    arrays["all"] = np.ones((P, P), f)
    arrays["tiles"] = np.ascontiguousarray(np.broadcast_to(np.arange(ns)[None, :], (P, ns))).astype(f)
    arrays["token"] = (p + P * np.arange(NT)[None, :]).astype(np.int32)
    nc = bacc.Bacc("TRN2", target_bir_lowering=False, num_devices=1)
    t, feeds = {}, {}
    for n, a in arrays.items():
        feeds[f"in_{n}_dram"] = a
        t[n] = nc.dram_tensor(f"in_{n}_dram", a.shape, mybir.dt.from_np(a.dtype), kind="ExternalInput").ap()
    out = nc.dram_tensor("out_0_dram", (B, SQ, D), F32, kind="ExternalOutput").ap()
    layer(nc, t, out)
    return launch(nc, [feeds], core_ids=[0]).results[0]["out_0_dram"]
```

```python
from contextlib import ExitStack

import concourse.bass as bass
from concourse import mybir

F32 = mybir.dt.float32
BF16 = mybir.dt.bfloat16
I32 = mybir.dt.int32
ALU = mybir.AluOpType
ACT = mybir.ActivationFunctionType
AX = mybir.AxisListType

P = 128
B, SQ, D = 64, 64, 128
SK = 128
H, DH = 16, 8
EPS = 1e-5
SCALE = DH ** -0.5
MASKED = -1000000000.0
NT = B * SQ // P
NU = 4
ROW = 2 * D + 2
VW = 32


def cross_attention(nc, rows, xres, ident, wts, slots, later, x, ctx_in, mask, Wq, bq, Wk, bk, Wv, bv, Wo, bo, ident_in, heads_in):
    x_t = x.rearrange("(n b) s d -> n (b s) d", b=2)
    ctx_t = ctx_in.rearrange("(n b) k d -> n k b d", b=2)
    mask_t = mask.rearrange("(n b) a c k -> n (a c) (b k)", b=2)

    with ExitStack() as ctx:
        def sb(name, shape, dt=F32):
            return ctx.enter_context(nc.sbuf_tensor(name, shape, dt))

        def psum(name):
            return ctx.enter_context(nc.psum_tensor(name, [P, 512], F32))

        def sem(name):
            return ctx.enter_context(nc.semaphore(name))

        pad = sb("pad", [P, ROW])
        heads = sb("heads", [P, H])
        qt = sb("qt", [P, 2, P])
        wq, wk, wv = sb("wq", [D, P]), sb("wk", [D, P]), sb("wv", [D, P])
        wo2 = sb("wo2", [64, 2, D])
        bqc, bkc = sb("bqc", [P, 1]), sb("bkc", [P, 1])
        bvr, bor = sb("bvr", [P, P]), sb("bor", [P, D])
        onesb = sb("onesb", [P, P], BF16)
        halfs = sb("halfs", [P, 1])
        cin = sb("cin", [P, 2, 2, D])
        mki = sb("mki", [P, 2, 2 * SK], I32)
        mkb = sb("mkb", [P, 2, 2 * SK], BF16)
        stats, aggr, veps, rstd = sb("stats", [P, 2, 6]), sb("aggr", [P, 2, 2]), sb("veps", [P, 2]), sb("rstd", [P, 2])
        xn = sb("xn", [P, 2, D])
        xt = sb("xt", [P, 2, 384])
        kt = sb("kt", [P, 2, 2 * SK])
        vx = sb("vx", [P, 2, 2, 8, VW])
        qm = sb("qm", [P, 2, 2, H, SQ])
        mx = sb("mx", [P, 2, 4])
        dif, prob, pts = sb("dif", [P, NU, 512]), sb("prob", [P, NU, 512]), sb("pts", [P, NU, 512])
        rc = sb("rc", [P, 16])
        osum = sb("osum", [P, 512])
        on = sb("on", [P, 2, 64])
        ot = sb("ot", [64, 2, 2, SQ])

        S = [psum("S0"), psum("S1")]
        PT = [psum("PT0"), psum("PT1")]
        TB = psum("TB")
        KO = psum("KO")
        VY = psum("VY")
        OB = psum("OB")
        o_ps = OB[:, :].rearrange("p (u b j w) -> p b u j w", u=NU, b=2, j=2)

        const_in, ones_set = sem("const_in"), sem("ones_set")
        tile_in = [sem("tile_in0"), sem("tile_in1")]
        s = {n: sem(n) for n in (
            "stats_ready", "aggr_ready", "veps_ready", "rstd_ready", "xn_ready", "turned", "turned_out",
            "kv_ready", "kv_out", "q_ready", "q_out", "k_out", "q_spread", "mask_ready", "residual_ready", "logits_ready", "max_ready",
            "dif_ready", "prob_ready", "pt_ready", "pt_out", "pv_ready", "osum_ready", "o_turned", "rc_ready", "on_ready", "ot_ready",
            "ot_out", "y_ready", "x1_ready")}
        NCONST = 11
        block = ctx.enter_context(nc.Block())

        def run(eng, step, tail):
            for i in range(3):
                step(i, i % 2)
            with eng.Fori(3, NT - 3, 2) as i:
                step(i, 1)
                step(i + 1, 0)
            for i in range(NT - 3, NT):
                step(i, i % 2)
            tail(NT)

        def from_(i, k):
            return not isinstance(i, int) or i >= k

        def has(i, k):
            return not isinstance(i, int) or i + k < NT

        def half(i, p):
            return i // 2 if isinstance(i, int) else (i - p) // 2

        @block.sync
        def _(sp):
            for dst, src in ((ident[:, :], ident_in), (heads[:, :], heads_in), (wq[:, :], Wq), (wk[:, :], Wk),
                             (wv[:, :], Wv)):
                sp.dma_start(dst, src).then_inc(const_in, 16)

            def load(i, p):
                sp.dma_start(xres[:, bass.ds(i, 1), :], x_t[bass.ds(i, 1)].rearrange("n p d -> p n d")).then_inc(tile_in[p], 16)
                sp.dma_start(cin[:, p], ctx_t[bass.ds(i, 1)].rearrange("n k b d -> k (n b) d")).then_inc(tile_in[p], 16)
                if True:
                    sp.dma_start(mki[0:1, p, :], mask_t[bass.ds(i, 1)].rearrange("n a c -> (n a) c")).then_inc(tile_in[p], 16)

            sp.wait_ge(ones_set, 4)
            load(0, 0)
            load(1, 1)
            with sp.Fori(2, NT - 1, 2) as i:
                for p in range(2):
                    sp.wait_ge(s["turned"], i + p - 1)
                    sp.wait_ge(s["mask_ready"], i + p - 1)
                    load(i + p, p)

        @block.gpsimd
        def _(pool):
            nc.gpsimd.memset(onesb[:, :], 1.0).then_inc(ones_set, 1)
            nc.gpsimd.memset(halfs[:, :], -0.5).then_inc(ones_set, 1)
            nc.gpsimd.memset(mki[:, :, :], 0).then_inc(ones_set, 1)
            nc.gpsimd.memset(vx[:, :, :, :, :], 1.0).then_inc(ones_set, 1)
            pool.wait_ge(ones_set, 4)
            nc.gpsimd.memset(pad[:, :], 0.0).then_inc(ones_set, 1)
            pool.wait_ge(ones_set, 5)
            nc.gpsimd.memset(pad[:, 2 * D:2 * D + 1].bitcast(I32), 1 << 20).then_inc(ones_set, 1)
            pool.wait_ge(ones_set, 6)
            pool.dma_start(slots.rearrange("(n p) w -> p n w", p=P),
                           pad[:, :].rearrange("p (a w) -> p a w", a=1).broadcast_to([P, slots.shape[0] // P, ROW])).then_inc(wts["cleared"], 16)
            pool.wait_ge(const_in, 16 * NCONST)

            def power(i, p):
                pool.wait_ge(s["veps_ready"], i + 1)
                nc.gpsimd.tensor_tensor(rstd[:, p:p + 1], veps[:, p:p + 1], halfs[:, :], ALU.pow).then_inc(s["rstd_ready"], 1)

            def prepare(i, p):
                pool.wait_ge(tile_in[p], 48 * (half(i, p) + 1))
                if from_(i, 2):
                    pool.wait_ge(s["logits_ready"], NU * (i - 1))
                pool.wait_ge(s["stats_ready"], i + 1)
                pool.wait_ge(s["xn_ready"], i + 1)
                nc.gpsimd.tensor_tensor(xres[:, bass.ds(i, 1), :], xres[:, bass.ds(i, 1), :],
                                        bor[:, :].rearrange("p (n d) -> p n d", n=1), ALU.add).then_inc(s["residual_ready"], 1)
                nc.gpsimd.tensor_scalar(mkb[:, p, :], mki[:, p, :], MASKED, None, ALU.mult).then_inc(s["mask_ready"], 1)

            def spread(i, p):
                pool.wait_ge(s["q_out"], i + 1)
                if from_(i, 2):
                    pool.wait_ge(s["logits_ready"], NU * (i - 1))
                for b in range(2):
                    if b and from_(i, 1) and has(i, 1):
                        power(i + 1, 1 - p)
                    nc.gpsimd.tensor_tensor(
                        qm[:, p, b, :, :],
                        qt[:, p, SQ * b:SQ * b + SQ].rearrange("p (a c) -> p a c", a=1).broadcast_to([P, H, SQ]),
                        heads[:, :].rearrange("p (c a) -> p c a", a=1).broadcast_to([P, H, SQ]),
                        ALU.mult).then_inc(s["q_spread"], 1)

            power(0, 0)
            power(1, 1)
            prepare(0, 0)
            prepare(1, 1)
            spread(0, 0)
            for i in range(2, 4):
                spread(i - 1, 1 - i % 2)
                prepare(i, i % 2)
            with pool.Fori(4, NT - 1, 2) as i:
                for p in range(2):
                    spread(i + p - 1, 1 - p)
                    prepare(i + p, p)
            spread(NT - 1, 1)

        @block.scalar
        def _(act):
            for dst, src in ((bqc[:, :], bq.rearrange("(p a) -> p a", a=1)), (bkc[:, :], bk.rearrange("(p a) -> p a", a=1)),
                             (bvr[:, :], bv.rearrange("(a n) -> a n", a=1).broadcast_to([P, P])),
                             (bor[:, :], bo.rearrange("(a n) -> a n", a=1).broadcast_to([P, D]))):
                act.dma_start(dst, src).then_inc(const_in, 16)
            wo_v = Wo.rearrange("(j t d) n -> t j d n", j=8, t=2)
            for t in range(2):
                act.dma_start(wo2[:, t, :], wo_v[t]).then_inc(const_in, 16)
            act.preload_act_table_set("natural_log_exp_and_others")
            for dst, src in later:
                act.dma_start(dst, src).then_inc(wts["loaded"], 16)

            def exp(i, u):
                n = NU * i + u
                act.wait_ge(s["dif_ready"], n + 1)
                if from_(i, 1):
                    act.wait_ge(s["pt_ready"], n - 3)
                nc.scalar.activation(prob[:, u, :], dif[:, u, :], ACT.Exp).then_inc(s["prob_ready"], 1)

            def evacuate(i, u):
                n = NU * i + u
                act.wait_ge(s["pt_ready"], n + 1)
                if from_(i, 1):
                    act.wait_ge(s["pv_ready"], n - 3)
                nc.scalar.activation(pts[:, u, :], PT[u % 2][:, :], ACT.Copy).then_inc(s["pt_out"], 1)

            def turned_out(i, p):
                act.wait_ge(s["turned"], i + 1)
                if from_(i, 2):
                    act.wait_ge(s["q_ready"], i - 1)
                nc.scalar.activation(xt[:, p, :], TB[:, 0:384], ACT.Copy).then_inc(s["turned_out"], 1)

            def k_out(i, p):
                act.wait_ge(s["kv_ready"], i + 1)
                if from_(i, 2):
                    act.wait_ge(s["logits_ready"], NU * (i - 1))
                nc.scalar.activation(kt[:, p, :], KO[:, 0:256], ACT.Identity, bias=bkc[:, :]).then_inc(s["k_out"], 1)

            def q_out(i, p):
                act.wait_ge(s["q_ready"], i + 1)
                if from_(i, 2):
                    act.wait_ge(s["q_spread"], 2 * (i - 1))
                nc.scalar.activation(qt[:, p, :], TB[:, 384:512], ACT.Identity, bias=bqc[:, :]).then_inc(s["q_out"], 1)

            def ot_out(i):
                act.wait_ge(s["ot_ready"], i + 1)
                if from_(i, 1):
                    act.wait_ge(s["y_ready"], i)
                nc.scalar.activation(ot[:, :, :, :], KO[0:64, 256:512].rearrange("p (b t q) -> p t b q", b=2, t=2),
                                     ACT.Copy).then_inc(s["ot_out"], 1)

            def o_out(i):
                act.wait_ge(s["pv_ready"], NU * (i + 1))
                if from_(i, 1):
                    act.wait_ge(s["o_turned"], i)
                nc.scalar.activation(osum[:, :], OB[:, :], ACT.Copy).then_inc(s["osum_ready"], 1)

            def step(i, p):
                if from_(i, 1):
                    exp(i - 1, 3)
                    evacuate(i - 1, 2)
                if has(i, 1):
                    turned_out(i + 1, 1 - p)
                exp(i, 0)
                if from_(i, 2):
                    ot_out(i - 2)
                if from_(i, 1):
                    evacuate(i - 1, 3)
                if has(i, 1):
                    q_out(i + 1, 1 - p)
                exp(i, 1)
                if has(i, 1):
                    k_out(i + 1, 1 - p)
                if from_(i, 1):
                    o_out(i - 1)
                evacuate(i, 0)
                exp(i, 2)
                evacuate(i, 1)

            def tail(i):
                exp(i - 1, 3)
                evacuate(i - 1, 2)
                ot_out(i - 2)
                evacuate(i - 1, 3)
                o_out(i - 1)
                ot_out(i - 1)

            turned_out(0, 0)
            k_out(0, 0)
            q_out(0, 0)
            run(act, step, tail)

        @block.vector
        def _(dve):
            def unit(i, u):
                n = NU * i + u
                lg = S[u % 2][:, :].rearrange("p (c k) -> p c k", k=SK)
                dve.wait_ge(s["logits_ready"], n + 1)
                nc.vector.tensor_reduce(mx[:, u % 2, :], lg, AX.X, ALU.max).then_inc(s["max_ready"], 1)
                dve.wait_ge(s["max_ready"], n + 1)
                if from_(i, 1):
                    dve.wait_ge(s["prob_ready"], n - 3)
                nc.vector.tensor_tensor(dif[:, u, :].rearrange("p (c k) -> p c k", k=SK), lg,
                                        mx[:, u % 2, :].rearrange("p (c a) -> p c a", a=1).broadcast_to([P, 4, SK]),
                                        ALU.subtract).then_inc(s["dif_ready"], 1)

            def norm(i, p):
                dve.wait_ge(tile_in[p], 48 * (half(i, p) + 1))
                xin = xres[:, bass.ds(i, 1), :]
                nc.vector.bn_stats(stats[:, p, :], xin.rearrange("p n d -> p (n d)")).then_inc(s["stats_ready"], 1)
                dve.wait_ge(s["stats_ready"], i + 1)

            def aggregate(i, p):
                nc.vector.bn_aggr(aggr[:, p, :], stats[:, p, :]).then_inc(s["aggr_ready"], 1)
                dve.wait_ge(s["aggr_ready"], i + 1)
                nc.vector.tensor_scalar(veps[:, p:p + 1], aggr[:, p, 1:2], EPS, None, ALU.add).then_inc(s["veps_ready"], 1)

            def scale(i, p):
                dve.wait_ge(s["rstd_ready"], i + 1)
                if from_(i, 2):
                    dve.wait_ge(s["turned"], i - 1)
                nc.vector.tensor_scalar(xn[:, p, :].rearrange("p (n d) -> p n d", n=1), xres[:, bass.ds(i, 1), :],
                                        aggr[:, p, 0:1], rstd[:, p:p + 1], ALU.subtract, ALU.mult).then_inc(s["xn_ready"], 1)

            def kv_out(i, p):
                dve.wait_ge(s["kv_ready"], i + 1)
                if from_(i, 2):
                    dve.wait_ge(s["pv_ready"], NU * (i - 1))
                for b in range(2):
                    nc.vector.tensor_tensor(vx[:, p, b, :, 0:16],
                                            VY[:, P * b:P * b + P].rearrange("p (j w) -> p j w", j=8),
                                            bvr[:, :].rearrange("p (j w) -> p j w", j=8), ALU.add).then_inc(s["kv_out"], 1)

            def divide(i):
                dve.wait_ge(s["o_turned"], i + 1)
                if from_(i, 1):
                    dve.wait_ge(s["ot_ready"], i)
                nc.vector.reciprocal(rc[:, :].rearrange("p (b u j) -> p b u j", b=2, j=2), o_ps[:, :, :, :, 16]).then_inc(s["rc_ready"], 1)
                dve.wait_ge(s["rc_ready"], i + 1)
                for t in range(2):
                    r = slice(64 * t, 64 * t + 64)
                    for b in range(2):
                        nc.vector.tensor_tensor(on[r, b, :].rearrange("p (u j d) -> p u j d", u=NU, j=2), o_ps[r, b, :, :, 8 * t:8 * t + 8],
                                                rc[r, 8 * b:8 * b + 8].rearrange("p (u j a) -> p u j a", j=2, a=1).broadcast_to([64, NU, 2, 8]),
                                                ALU.mult).then_inc(s["on_ready"], 1)

            def add(i):
                dve.wait_ge(s["y_ready"], i + 1)
                dve.wait_ge(s["residual_ready"], i + 1)
                nc.vector.tensor_tensor(xres[:, bass.ds(i, 1), :], VY[:, 256:384].rearrange("p (n d) -> p n d", n=1),
                                        xres[:, bass.ds(i, 1), :], ALU.add).then_inc(s["x1_ready"], 1)

            def step(i, p):
                unit(i, 0)
                if has(i, 2):
                    norm(i + 2, p)
                unit(i, 1)
                if has(i, 2):
                    aggregate(i + 2, p)
                if has(i, 1):
                    kv_out(i + 1, 1 - p)
                unit(i, 2)
                if has(i, 2):
                    scale(i + 2, p)
                if from_(i, 1):
                    divide(i - 1)
                unit(i, 3)
                if from_(i, 2):
                    add(i - 2)

            def tail(i):
                add(i - 2)
                divide(i - 1)
                add(i - 1)

            dve.wait_ge(const_in, 16 * NCONST)
            dve.wait_ge(ones_set, 4)
            for i in range(2):
                norm(i, i)
                aggregate(i, i)
                scale(i, i)
            kv_out(0, 0)
            run(dve, step, tail)

        @block.tensor
        def _(pe):
            def logits(i, u, p):
                n = NU * i + u
                if u == 0:
                    pe.wait_ge(s["q_spread"], 2 * (i + 1))
                    pe.wait_ge(s["k_out"], i + 1)
                    pe.wait_ge(s["mask_ready"], i + 1)
                if from_(i, 1) or u >= 2:
                    pe.wait_ge(s["dif_ready"], n - 1)
                nc.tensor.matmul(S[u % 2][:, :], onesb[:, :],
                                 mkb[:, p, :].rearrange("p (b a k) -> p b a k", b=2, a=1).broadcast_to([P, 2, 2, SK]),
                                 start=True, stop=False)
                for b in range(2):
                    for jj in range(2):
                        c = (2 * b + jj) * SK
                        last = nc.tensor.matmul(S[u % 2][:, c:c + SK],
                                                qm[:, p, b, 4 * u + 2 * jj:4 * u + 2 * jj + 2, :].rearrange("p c q -> p (c q)"),
                                                kt[:, p, SK * b:SK * b + SK], start=False, stop=(b == 1 and jj == 1))
                last.then_inc(s["logits_ready"], 1)

            def turn_prob(i, u):
                n = NU * i + u
                pe.wait_ge(s["prob_ready"], n + 1)
                if from_(i, 1) or u >= 2:
                    pe.wait_ge(s["pt_out"], n - 1)
                for c in range(4):
                    last = nc.tensor.transpose(PT[u % 2][:, c * P:c * P + P], prob[:, u, c * P:c * P + P], ident[:, :])
                last.then_inc(s["pt_ready"], 1)

            def values(i, u, p):
                n = NU * i + u
                pe.wait_ge(s["pt_out"], n + 1)
                if u == 0:
                    pe.wait_ge(s["kv_out"], 2 * (i + 1))
                if u == 0 and from_(i, 1):
                    pe.wait_ge(s["on_ready"], 4 * i)
                for b in range(2):
                    for jj in range(2):
                        k = 2 * b + jj
                        last = nc.tensor.matmul(OB[32 * k:32 * k + 32, u * P:u * P + P], vx[:, p, b, 2 * u + jj, :],
                                                pts[:, u, k * P:k * P + P], start=True, stop=True, tile_position=(0, 32 * k))
                last.then_inc(s["pv_ready"], 1)

            def turn_sums(i):
                pe.wait_ge(s["osum_ready"], i + 1)
                for u in range(NU):
                    last = nc.tensor.transpose(OB[:, u * P:u * P + P], osum[:, u * P:u * P + P], ident[:, :])
                last.then_inc(s["o_turned"], 1)

            def turn(i, p):
                pe.wait_ge(s["xn_ready"], i + 1)
                pe.wait_ge(tile_in[p], 48 * (half(i, p) + 1))
                if from_(i, 1):
                    pe.wait_ge(s["q_out"], i)
                for b in range(2):
                    nc.tensor.transpose(TB[:, b * P:b * P + P], cin[:, p, b, :], ident[:, :])
                nc.tensor.transpose(TB[:, 256:384], xn[:, p, :], ident[:, :]).then_inc(s["turned"], 1)

            def keys_values(i, p):
                pe.wait_ge(s["turned_out"], i + 1)
                if from_(i, 1):
                    pe.wait_ge(s["kv_out"], 2 * i)
                    pe.wait_ge(s["k_out"], i)
                if from_(i, 3):
                    pe.wait_ge(s["ot_out"], i - 2)
                if from_(i, 4):
                    pe.wait_ge(s["x1_ready"], i - 3)
                nc.tensor.matmul(KO[:, 0:256], wk[:, :], xt[:, p, 0:256], start=True, stop=True)
                for b in range(2):
                    last = nc.tensor.matmul(VY[:, b * P:b * P + P], xt[:, p, b * P:b * P + P], wv[:, :],
                                            start=True, stop=True)
                last.then_inc(s["kv_ready"], 1)

            def queries(i, p):
                pe.wait_ge(s["turned_out"], i + 1)
                nc.tensor.matmul(TB[:, 384:512], wq[:, :], xt[:, p, 256:384], start=True, stop=True).then_inc(s["q_ready"], 1)

            def output_divided(i):
                pe.wait_ge(s["on_ready"], 4 * (i + 1))
                pe.wait_ge(s["k_out"], (i + 3) if has(i, 2) else NT)

            def turn_output(i):
                for b in range(2):
                    last = nc.tensor.transpose(KO[0:64, 256 + b * P:384 + b * P], on[:, b, :], ident[:, :])
                last.then_inc(s["ot_ready"], 1)

            def project(i):
                pe.wait_ge(s["ot_out"], i + 1)
                pe.wait_ge(s["kv_out"], 2 * (i + 4) if has(i, 3) else 2 * NT)
                if not has(i, 2):
                    pe.wait_ge(s["x1_ready"], i)
                for t in range(2):
                    last = nc.tensor.matmul(VY[:, 256:384], ot[:, t, :, :].rearrange("p b q -> p (b q)"), wo2[:, t, :],
                                            start=(t == 0), stop=(t == 1))
                last.then_inc(s["y_ready"], 1)

            def step(i, p):
                logits(i, 0, p)
                if from_(i, 1):
                    turn_prob(i - 1, 2)
                    values(i - 1, 0, 1 - p)
                if has(i, 1):
                    turn(i + 1, 1 - p)
                if from_(i, 2):
                    output_divided(i - 2)
                logits(i, 1, p)
                if from_(i, 2):
                    turn_output(i - 2)
                if from_(i, 1):
                    turn_prob(i - 1, 3)
                    values(i - 1, 1, 1 - p)
                if has(i, 1):
                    queries(i + 1, 1 - p)
                    keys_values(i + 1, 1 - p)
                if from_(i, 1):
                    values(i - 1, 2, 1 - p)
                    values(i - 1, 3, 1 - p)
                logits(i, 2, p)
                turn_prob(i, 0)
                if from_(i, 1):
                    turn_sums(i - 1)
                logits(i, 3, p)
                if from_(i, 2):
                    project(i - 2)
                turn_prob(i, 1)

            def tail(i):
                output_divided(i - 2)
                turn_prob(i - 1, 2)
                turn_output(i - 2)
                values(i - 1, 0, 1)
                values(i - 1, 1, 1)
                turn_prob(i - 1, 3)
                values(i - 1, 2, 1)
                project(i - 2)
                values(i - 1, 3, 1)
                turn_sums(i - 1)
                output_divided(i - 1)
                turn_output(i - 1)
                project(i - 1)

            pe.wait_ge(const_in, 16 * NCONST)
            pe.wait_ge(ones_set, 4)
            turn(0, 0)
            keys_values(0, 0)
            queries(0, 0)
            run(pe, step, tail)


def linear_attention(nc, xres, ident, wts):
    HG, DK, DV, LR = 4, 128, 32, 16
    NB = B * SQ // 512
    T4 = 512 // P
    with ExitStack() as ctx:
        def sb(name, shape, dt=F32):
            return ctx.enter_context(nc.sbuf_tensor(name, shape, dt))

        def psum(name):
            return ctx.enter_context(nc.psum_tensor(name, [P, 512], F32))

        def sem(name):
            return ctx.enter_context(nc.semaphore(name))

        xt = sb("g_xt", [D, NB, 512])
        xs = sb("g_xs", [D, 512])
        low = sb("g_low", [LR + 1, NB, 512])
        val = sb("g_val", [P, NB, T4, P])
        silu = sb("g_silu", [P, NB, 512])
        stats, aggr = sb("g_stats", [P, T4, 6]), sb("g_aggr", [P, T4, 2])
        veps, rstd = sb("g_veps", [P, T4]), sb("g_rstd", [P, T4])
        xn = sb("g_xn", [P, T4, D])
        reset = sb("g_reset", [P, 512])
        neg, mag = (sb("g_" + n, [P, 2, 512]) for n in ("neg", "mag"))
        cum, grow, decay = (sb("g_" + n, [P, 2, 512]) for n in ("cum", "grow", "decay"))
        qg, ki, am = (sb("g_" + n, [P, 2, 512]) for n in ("qg", "ki", "am"))
        gneg, gmag = sb("g_gneg", [P, 512]), sb("g_gmag", [P, 512])
        sq, on, og = sb("g_sq", [P, 512]), sb("g_on", [P, 512]), sb("g_og", [P, 512])
        ms, meps, rms = sb("g_ms", [P, 16]), sb("g_meps", [P, 16]), sb("g_rms", [P, 16])
        halfs = sb("g_halfs", [P, 16])

        Z, Q, K, A, O, T, U, V = (psum("g" + n) for n in "ZQKAOTUV")

        s = {n: sem("g_" + n) for n in (
            "set_up", "x_kept", "stats_ready", "aggr_ready", "veps_ready", "rstd_ready", "xn_ready", "turned", "turned_out", "low_ready",
            "low_out", "v_ready", "v_out", "gate_ready", "gmag_ready", "gexp_ready", "glog_ready", "gsum_ready", "gsig_ready",
            "silu_ready", "z_ready", "mag_ready", "exp_ready", "log_ready", "tot_ready", "cum_ready", "grow_ready",
            "decay_ready", "q_ready", "k_ready", "qg_ready", "ki_ready", "a_ready", "am_ready", "o_ready", "o_out", "sq_ready",
            "ms_ready", "meps_ready", "rms_ready", "on_ready", "ot_ready", "og_ready", "y_ready", "x2_ready")}
        NSET = 7
        block = ctx.enter_context(nc.Block())

        def run(eng, step, tail):
            for c in range(3):
                step(c)
            with eng.Fori(3, NB - 2, 1) as c:
                step(c)
            step(NB - 2)
            step(NB - 1)
            tail(NB)

        def from_(c, k):
            return c >= k if isinstance(c, int) else k <= 3

        def has(c, k):
            return c + k < NB if isinstance(c, int) else k <= 2

        def cols(t, c):
            return t[:, bass.ds(c, 1), :].rearrange("p a n -> p (a n)")

        @block.gpsimd
        def _(pool):
            nc.gpsimd.memset(halfs[:, :], -0.5).then_inc(s["set_up"], 1)
            nc.gpsimd.memset(low[:, :, :], 1.0).then_inc(s["set_up"], 1)
            nc.gpsimd.memset(am[:, :, :], 0.0).then_inc(s["set_up"], 1)
            nc.gpsimd.memset(reset[:, :], 1.0).then_inc(s["set_up"], 1)
            pool.wait_ge(s["set_up"], 4)
            nc.gpsimd.memset(reset[:, 0:512:SQ], 0.0).then_inc(s["set_up"], 3)

            def keep(c):
                pool.wait_ge(s["turned_out"], c + 1)
                nc.gpsimd.tensor_copy(cols(xt, c), xs[:, :]).then_inc(s["x_kept"], 1)

            def power(c):
                pool.wait_ge(s["veps_ready"], c + 1)
                nc.gpsimd.tensor_tensor(rstd[:, :], veps[:, :], halfs[:, 0:T4], ALU.pow).then_inc(s["rstd_ready"], 1)

            def total(n, par):
                pool.wait_ge(s["log_ready"], n + 1)
                nc.gpsimd.tensor_tensor(neg[:, par, :], neg[:, par, :], mag[:, par, :], ALU.add).then_inc(s["tot_ready"], 1)

            def gate_total(c):
                pool.wait_ge(s["glog_ready"], c + 1)
                nc.gpsimd.tensor_tensor(gneg[:, :], gneg[:, :], gmag[:, :], ALU.add).then_inc(s["gsum_ready"], 1)

            def rms_power(c):
                pool.wait_ge(s["meps_ready"], c + 1)
                nc.gpsimd.tensor_tensor(rms[:, :], meps[:, :], halfs[:, :], ALU.pow).then_inc(s["rms_ready"], 1)

            def step(c):
                for h in range(HG):
                    if h == 3 and from_(c, 1):
                        rms_power(c - 1)
                    if h == 0 or has(c, 1):
                        total(HG * c + h + 3, (h + 1) % 2)
                    if h == 0 and has(c, 1):
                        keep(c + 1)
                    if h == 1 and has(c, 2):
                        power(c + 2)
                    if h == 2 and has(c, 1):
                        gate_total(c + 1)

            power(0)
            power(1)
            keep(0)
            gate_total(0)
            for n in range(3):
                total(n, n % 2)
            run(pool, step, lambda c: rms_power(c - 1))

        @block.scalar
        def _(act):
            def turned_out(c):
                act.wait_ge(s["turned"], c + 1)
                if from_(c, 1):
                    act.wait_ge(s["v_ready"], c)
                    act.wait_ge(s["x_kept"], c)
                nc.scalar.activation(xs[:, :], T[:, :], ACT.Copy).then_inc(s["turned_out"], 1)

            def low_out(c):
                act.wait_ge(s["low_ready"], c + 1)
                nc.scalar.activation(low[0:LR, bass.ds(c, 1), :].rearrange("p a n -> p (a n)"), T[0:LR, :], ACT.Copy).then_inc(s["low_out"], 1)

            def v_out(c):
                act.wait_ge(s["v_ready"], c + 1)
                nc.scalar.activation(val[:, bass.ds(c, 1), :, :].rearrange("p a t n -> p (a t n)"), V[:, :], ACT.Copy).then_inc(s["v_out"], 1)

            def front(n, par):
                act.wait_ge(s["z_ready"], n + 1)
                if not isinstance(n, int) or n >= 2:
                    act.wait_ge(s["cum_ready"], n - 1)
                nc.scalar.activation(neg[:, par, :], Z[:, :], ACT.Relu, scale=-1.0)
                nc.scalar.activation(mag[:, par, :], Z[:, :], ACT.Abs).then_inc(s["mag_ready"], 1)
                act.wait_ge(s["mag_ready"], n + 1)
                nc.scalar.activation(mag[:, par, :], mag[:, par, :], ACT.Exp, scale=-1.0).then_inc(s["exp_ready"], 1)
                act.wait_ge(s["exp_ready"], n + 1)
                nc.scalar.activation(mag[:, par, :], mag[:, par, :], ACT.Ln, bias=1.0).then_inc(s["log_ready"], 1)

            def back(n, par):
                act.wait_ge(s["cum_ready"], n + 1)
                if not isinstance(n, int) or n >= 2:
                    act.wait_ge(s["ki_ready"], n - 1)
                nc.scalar.activation(decay[:, par, :], cum[:, par, :], ACT.Exp, scale=-1.0 / 16).then_inc(s["decay_ready"], 1)
                nc.scalar.activation(grow[:, par, :], cum[:, par, :], ACT.Exp, scale=1.0 / 16).then_inc(s["grow_ready"], 1)

            def gate_front(c):
                act.wait_ge(s["gate_ready"], c + 1)
                if from_(c, 1):
                    act.wait_ge(s["silu_ready"], c)
                nc.scalar.activation(gneg[:, :], T[:, :], ACT.Relu, scale=-1.0)
                nc.scalar.activation(gmag[:, :], T[:, :], ACT.Abs).then_inc(s["gmag_ready"], 1)
                act.wait_ge(s["gmag_ready"], c + 1)
                nc.scalar.activation(gmag[:, :], gmag[:, :], ACT.Exp, scale=-1.0).then_inc(s["gexp_ready"], 1)
                act.wait_ge(s["gexp_ready"], c + 1)
                nc.scalar.activation(gmag[:, :], gmag[:, :], ACT.Ln, bias=1.0).then_inc(s["glog_ready"], 1)

            def gate_sigmoid(c):
                act.wait_ge(s["gsum_ready"], c + 1)
                nc.scalar.activation(gneg[:, :], gneg[:, :], ACT.Exp, scale=-1.0).then_inc(s["gsig_ready"], 1)

            def o_out(c):
                act.wait_ge(s["o_ready"], HG * (c + 1))
                if from_(c, 1):
                    act.wait_ge(s["ot_ready"], c)
                    act.wait_ge(s["ms_ready"], c)
                nc.scalar.activation(on[:, :], O[:, :], ACT.Copy).then_inc(s["o_out"], 1)
                act.wait_ge(s["o_out"], c + 1)
                nc.scalar.activation(sq[:, :], on[:, :], ACT.Square).then_inc(s["sq_ready"], 1)

            def step(c):
                for h in range(HG):
                    n = HG * c + h
                    if h == 1 and has(c, 1):
                        low_out(c + 1)
                    if h == 3 and has(c, 1):
                        v_out(c + 1)
                    if h < 3 or has(c, 1):
                        back(n + 1, (h + 1) % 2)
                    if h == 0 and has(c, 1):
                        turned_out(c + 1)
                    if h == 2 and from_(c, 1):
                        o_out(c - 1)
                    if h == 0 or has(c, 1):
                        front(n + 3, (h + 1) % 2)
                    if h == 2 and has(c, 1):
                        gate_front(c + 1)
                    if h == 3 and has(c, 1):
                        gate_sigmoid(c + 1)

            turned_out(0)
            low_out(0)
            front(0, 0)
            gate_front(0)
            v_out(0)
            gate_sigmoid(0)
            front(1, 1)
            back(0, 0)
            front(2, 0)
            run(act, step, lambda c: o_out(c - 1))

        @block.vector
        def _(dve):
            def norm(c):
                for t in range(T4):
                    last = nc.vector.bn_stats(stats[:, t, :], xres[:, bass.ds(c * T4 + t, 1), :].rearrange("p n d -> p (n d)"))
                last.then_inc(s["stats_ready"], 1)
                dve.wait_ge(s["stats_ready"], c + 1)

            def aggregate(c):
                for t in range(T4):
                    last = nc.vector.bn_aggr(aggr[:, t, :], stats[:, t, :])
                last.then_inc(s["aggr_ready"], 1)
                dve.wait_ge(s["aggr_ready"], c + 1)
                nc.vector.tensor_scalar(veps[:, :], aggr[:, :, 1], EPS, None, ALU.add).then_inc(s["veps_ready"], 1)

            def unit(n, par, c):
                dve.wait_ge(s["decay_ready"], n + 1)
                dve.wait_ge(s["q_ready"], n + 1)
                if not isinstance(n, int) or n >= 2:
                    dve.wait_ge(s["a_ready"], n - 1)
                nc.vector.scalar_tensor_tensor(out=qg[:, par, :], in0=Q[:, :], scalar=DK ** -0.5, in1=decay[:, par, :],
                                               op0=ALU.mult, op1=ALU.mult).then_inc(s["qg_ready"], 1)
                dve.wait_ge(s["grow_ready"], n + 1)
                dve.wait_ge(s["k_ready"], n + 1)
                if not isinstance(n, int) or n >= 1:
                    dve.wait_ge(s["a_ready"], n)
                if not isinstance(n, int) or n >= 3:
                    dve.wait_ge(s["o_ready"], n - 2)
                nc.vector.tensor_tensor(ki[:, par, :], K[:, :], grow[:, par, :], ALU.mult).then_inc(s["ki_ready"], 1)

            def scan(n, par):
                dve.wait_ge(s["tot_ready"], n + 1)
                if not isinstance(n, int) or n >= 2:
                    dve.wait_ge(s["grow_ready"], n - 1)
                nc.vector.tensor_tensor_scan(cum[:, par, :], reset[:, :], neg[:, par, :], 0.0, ALU.mult, ALU.add).then_inc(s["cum_ready"], 1)

            def mask(n, par):
                nc.vector.copy_predicated(am[:, par, :].rearrange("p (t i) -> p t i", t=T4),
                                          wts["causal"][:, :].rearrange("p (a i) -> p a i", a=1).broadcast_to([P, T4, P]),
                                          A[:, :].rearrange("p (t i) -> p t i", t=T4)).then_inc(s["am_ready"], 1)

            def make_silu(c):
                dve.wait_ge(s["gsig_ready"], c + 1)
                nc.vector.tensor_tensor(cols(silu, c), T[:, :], gneg[:, :], ALU.mult).then_inc(s["silu_ready"], 1)

            def mean_square(c):
                dve.wait_ge(s["sq_ready"], c + 1)
                nc.vector.tensor_reduce(ms[:, :], sq[:, :].rearrange("p (a v) -> p a v", v=DV), AX.X, ALU.add).then_inc(s["ms_ready"], 1)
                dve.wait_ge(s["ms_ready"], c + 1)
                nc.vector.tensor_scalar(meps[:, :], ms[:, :], 1.0 / DV, EPS, ALU.mult, ALU.add).then_inc(s["meps_ready"], 1)

            def over_rms(c):
                dve.wait_ge(s["rms_ready"], c + 1)
                nc.vector.tensor_tensor(on[:, :].rearrange("p (a v) -> p a v", v=DV), on[:, :].rearrange("p (a v) -> p a v", v=DV),
                                        rms[:, :].rearrange("p (a b) -> p a b", b=1).broadcast_to([P, 16, DV]),
                                        ALU.mult).then_inc(s["on_ready"], 1)

            def gate(c):
                dve.wait_ge(s["ot_ready"], c + 1)
                dve.wait_ge(s["silu_ready"], c + 1)
                if from_(c, 1):
                    dve.wait_ge(s["y_ready"], c)
                nc.vector.scalar_tensor_tensor(out=og[:, :], in0=U[:, :], scalar=wts["gnw"][:, :], in1=cols(silu, c),
                                               op0=ALU.mult, op1=ALU.mult).then_inc(s["og_ready"], 1)

            def add(c):
                dve.wait_ge(s["y_ready"], c + 1)
                xb = xres[:, bass.ds(c * T4, T4), :]
                nc.vector.tensor_tensor(xb, V[:, :].rearrange("p (t n) -> p t n", t=T4), xb, ALU.add).then_inc(s["x2_ready"], 1)

            def scale(c):
                dve.wait_ge(s["rstd_ready"], c + 1)
                if from_(c, 1):
                    dve.wait_ge(s["turned"], c)
                for t in range(T4):
                    last = nc.vector.tensor_scalar(xn[:, t:t + 1, :], xres[:, bass.ds(c * T4 + t, 1), :],
                                                   aggr[:, t, 0:1], rstd[:, t:t + 1], ALU.subtract, ALU.mult)
                last.then_inc(s["xn_ready"], 1)

            def step(c):
                for h in range(HG):
                    n = HG * c + h
                    if h < 3 or has(c, 1):
                        scan(n + 1, (h + 1) % 2)
                    unit(n, h % 2, c)
                    if h > 0 or from_(c, 1):
                        mask(n - 1, (h + 1) % 2)
                    if h == 0 and from_(c, 2):
                        over_rms(c - 2)
                    if h == 2 and from_(c, 2):
                        gate(c - 2)
                    if h == 0 and has(c, 2):
                        norm(c + 2)
                    if h == 1 and has(c, 2):
                        aggregate(c + 2)
                    if h == 2:
                        if has(c, 2):
                            scale(c + 2)
                        if from_(c, 1):
                            mean_square(c - 1)
                    if h == 3:
                        if has(c, 1):
                            make_silu(c + 1)
                        if from_(c, 2):
                            add(c - 2)

            def tail(c):
                dve.wait_ge(s["a_ready"], HG * c)
                dve.wait_ge(s["o_ready"], HG * c - 2)
                mask(HG * c - 1, 1)
                over_rms(c - 2)
                gate(c - 2)
                mean_square(c - 1)
                add(c - 2)
                over_rms(c - 1)
                gate(c - 1)
                add(c - 1)

            dve.wait_ge(s["set_up"], NSET)
            dve.wait_ge(wts["loaded"], wts["nload"])
            for c in range(2):
                norm(c)
                aggregate(c)
                scale(c)
            make_silu(0)
            scan(0, 0)
            run(dve, step, tail)

        @block.tensor
        def _(pe):
            def turn(c):
                pe.wait_ge(s["xn_ready"], c + 1)
                if from_(c, 1):
                    pe.wait_ge(s["silu_ready"], c)
                for t in range(T4):
                    last = nc.tensor.transpose(T[:, t * P:t * P + P], xn[:, t, :], ident[:, :])
                last.then_inc(s["turned"], 1)

            def gate_low_rank(c):
                pe.wait_ge(s["turned_out"], c + 1)
                nc.tensor.matmul(T[0:LR, :], wts["wgk1"][:, :], xs[:, :], start=True, stop=True).then_inc(s["low_ready"], 1)

            def gate_values(c):
                pe.wait_ge(s["low_out"], c + 1)
                nc.tensor.matmul(T[:, :], wts["wg"][:, :], xs[:, :], start=True, stop=True).then_inc(s["gate_ready"], 1)
                if from_(c, 4) or not isinstance(c, int):
                    pe.wait_ge(s["x2_ready"], c - 3)
                if from_(c, 1):
                    pe.wait_ge(s["v_out"], c)
                for t in range(T4):
                    last = nc.tensor.matmul(V[:, t * P:t * P + P], xs[:, t * P:t * P + P], wts["wv"][:, :], start=True, stop=True)
                last.then_inc(s["v_ready"], 1)

            def log_gates(c, h):
                nc.tensor.matmul(Z[:, :], wts["wgk2"][:, h * P:h * P + P], cols(low, c), start=True, stop=True).then_inc(s["z_ready"], 1)

            def queries(n, c, h):
                if h == 0:
                    pe.wait_ge(s["x_kept"], c + 1)
                if not isinstance(n, int) or n >= 1:
                    pe.wait_ge(s["qg_ready"], n)
                nc.tensor.matmul(Q[:, :], wts["wq"][:, h * P:h * P + P], cols(xt, c), start=True, stop=True).then_inc(s["q_ready"], 1)

            def keys(n, c, h):
                if not isinstance(n, int) or n >= 1:
                    pe.wait_ge(s["ki_ready"], n)
                if h == 0 or has(c, 1):
                    pe.wait_ge(s["mag_ready"], n + 3)
                    if h == 1:
                        pe.wait_ge(s["low_out"], c + 2)
                nc.tensor.matmul(K[:, :], wts["wk"][:, h * P:h * P + P], cols(xt, c), start=True, stop=True).then_inc(s["k_ready"], 1)

            def products(n, par):
                pe.wait_ge(s["ki_ready"], n + 1)
                if not isinstance(n, int) or n >= 1:
                    pe.wait_ge(s["am_ready"], n)
                for t in range(T4):
                    r = slice(t * P, t * P + P)
                    last = nc.tensor.matmul(A[:, r], ki[:, par, r], qg[:, par, r], start=True, stop=True)
                last.then_inc(s["a_ready"], 1)

            def outputs(n, par, c, h):
                pe.wait_ge(s["am_ready"], n + 1)
                if h == 0 and from_(c, 1):
                    pe.wait_ge(s["o_out"], c)
                for t in range(T4):
                    last = nc.tensor.matmul(O[:, t * P + h * DV:t * P + h * DV + DV], am[:, par, t * P:t * P + P],
                                            val[:, bass.ds(c, 1), t, h * DV:h * DV + DV].rearrange("p a v -> p (a v)"),
                                            start=True, stop=True)
                last.then_inc(s["o_ready"], 1)

            def turn_output(c):
                pe.wait_ge(s["on_ready"], c + 1)
                if from_(c, 1):
                    pe.wait_ge(s["og_ready"], c)
                for t in range(T4):
                    last = nc.tensor.transpose(U[:, t * P:t * P + P], on[:, t * P:t * P + P], ident[:, :])
                last.then_inc(s["ot_ready"], 1)

            def project(c):
                pe.wait_ge(s["og_ready"], c + 1)
                pe.wait_ge(s["v_out"], c + 4 if not isinstance(c, int) or c + 4 < NB else NB)
                if isinstance(c, int) and c >= NB - 2:
                    pe.wait_ge(s["x2_ready"], c)
                for t in range(T4):
                    last = nc.tensor.matmul(V[:, t * P:t * P + P], og[:, t * P:t * P + P], wts["wo"][:, :], start=True, stop=True)
                last.then_inc(s["y_ready"], 1)

            def step(c):
                for h in range(HG):
                    n = HG * c + h
                    queries(n, c, h)
                    if h > 0 or from_(c, 1):
                        products(n - 1, (h + 1) % 2)
                    if h == 0 and has(c, 1):
                        turn(c + 1)
                    keys(n, c, h)
                    if h == 0:
                        log_gates(c, 3)
                    elif has(c, 1):
                        log_gates(c + 1, h - 1)
                    if h > 1:
                        outputs(n - 2, h % 2, c, h - 2)
                    elif from_(c, 1):
                        outputs(n - 2, h % 2, c - 1, h + 2)
                    if h == 0 and has(c, 1):
                        gate_low_rank(c + 1)
                    if h == 1 and has(c, 1):
                        gate_values(c + 1)
                    if h == 3 and from_(c, 2):
                        project(c - 2)
                    if h == 1 and from_(c, 2):
                        turn_output(c - 2)

            def tail(c):
                products(HG * c - 1, 1)
                outputs(HG * c - 2, 0, c - 1, 2)
                outputs(HG * c - 1, 1, c - 1, 3)
                turn_output(c - 2)
                project(c - 2)
                turn_output(c - 1)
                project(c - 1)

            pe.wait_ge(s["set_up"], NSET)
            pe.wait_ge(wts["loaded"], wts["nload"])
            turn(0)
            gate_low_rank(0)
            pe.wait_ge(s["low_out"], 1)
            log_gates(0, 0)
            gate_values(0)
            pe.wait_ge(s["mag_ready"], 1)
            log_gates(0, 1)
            pe.wait_ge(s["mag_ready"], 2)
            log_gates(0, 2)
            run(pe, step, tail)


def experts(nc, rows, xres, ident, wts, slots, out):
    NE, F = 8, 512
    NS = (B * SQ + NE * (P - 1)) // P
    FC = F // P
    DEEP = 6
    NB, T4 = NT // 4, 4
    out_rows = out.rearrange("b s d -> (b s) d")
    slot_rows = slots.rearrange("(n p) w -> n p w", p=P)
    with ExitStack() as ctx:
        def sb(name, shape, dt=F32):
            return ctx.enter_context(nc.sbuf_tensor(name, shape, dt))

        def psum(name):
            return ctx.enter_context(nc.psum_tensor(name, [P, 512], F32))

        def sem(name):
            return ctx.enter_context(nc.semaphore(name))

        stats, aggr = sb("e_stats", [P, T4, 6]), sb("e_aggr", [P, T4, 2])
        veps, rstd, halfs = sb("e_veps", [P, T4]), sb("e_rstd", [P, T4]), sb("e_halfs", [P, T4])
        xt = sb("e_xt", [D, 512])
        lg, dif, ex, eq, hot = (sb("e_" + n, [P, NT, NE]) for n in ("lg", "dif", "ex", "eq", "hot"))
        mx, ssum, first, pos = (sb("e_" + n, [P, NT]) for n in ("mx", "ssum", "first", "pos"))
        posi = sb("e_posi", [P, NT], I32)
        cnt, inc = sb("e_cnt", [P, NE, NT]), sb("e_inc", [P, NE, NT])
        num, base = sb("e_num", [P, NE]), sb("e_base", [P, NE])
        numi = sb("e_numi", [P, NE], I32)
        ends, ones = sb("e_ends", [P, NE]), sb("e_ones", [P, NE])
        start = sb("e_start", [P, NT, NE])
        below = sb("e_below", [P, NS, NE])
        who, whoi = sb("e_who", [P, NS]), sb("e_whoi", [P, NS], I32)
        sx = sb("e_sx", [P, DEEP, ROW])
        sxt = sb("e_sxt", [D, 2, P])
        act_a, act_h, act_t = sb("e_a", [P, 2, F]), sb("e_h", [P, 2, F]), sb("e_t", [P, 2, FC, P])
        fin = sb("e_fin", [P, DEEP, D])

        XT, AT, Y, LG = psum("eXT"), psum("eAT"), psum("eY"), psum("eLG")
        HA, HG = [psum("eHA0"), psum("eHA1")], [psum("eHG0"), psum("eHG1")]

        s = {n: sem("e_" + n) for n in (
            "set_up", "stats_ready", "aggr_ready", "veps_ready", "rstd_ready", "xn_ready", "turned", "turned_out",
            "logits_ready", "route", "exp_ready", "ranks_ready", "chain", "sorted", "scattered", "rest_in", "who_ready",
            "sx_turned", "sx_out", "h_ready", "silu_ready", "act_ready", "at_ready", "at_out", "y_ready", "fin_ready",
            "passed")}
        sx_in, stored = ([sem(f"e_{n}{b}") for b in range(DEEP)] for n in ("sx_in", "stored"))
        block = ctx.enter_context(nc.Block())

        def run(eng, step, tail):
            for j in range(DEEP):
                step(j, j, 0)
            with eng.Fori(1, (NS - 1) // DEEP, 1) as r:
                for b in range(DEEP):
                    step(r * DEEP + b, b, r)
            for j in range(NS - (NS - 1) % DEEP - 1, NS):
                step(j, j % DEEP, j // DEEP)
            tail(NS)

        def from_(j, k):
            return j >= k if isinstance(j, int) else True

        def has(j, k):
            return j + k < NS if isinstance(j, int) else True

        @block.sync
        def _(sp):
            def load(j, b, r):
                if from_(j, DEEP):
                    sp.wait_ge(stored[b], 16 * r)
                sp.dma_start(sx[:, b, :], slot_rows[bass.ds(j, 1)].rearrange("n p w -> (n p) w")).then_inc(sx_in[b], 16)

            sp.wait_ge(s["scattered"], 16 * NT)
            run(sp, load, lambda j: None)

        @block.gpsimd
        def _(pool):
            nc.gpsimd.memset(halfs[:, :], -0.5).then_inc(s["set_up"], 1)
            nc.gpsimd.memset(ones[:, :], 1.0).then_inc(s["set_up"], 1)
            pool.wait_ge(s["set_up"], 2)
            for c in range(NB):
                pool.wait_ge(s["veps_ready"], c + 1)
                nc.gpsimd.tensor_tensor(rstd[:, :], veps[:, :], halfs[:, :], ALU.pow).then_inc(s["rstd_ready"], 1)
            nc.gpsimd.tensor_copy(rows[:, :, 2 * D:2 * D + 1].bitcast(I32).rearrange("p t a -> p (t a)"), wts["token"][:, :]).then_inc(s["set_up"], 1)
            pool.wait_ge(s["set_up"], 3)
            pool.wait_ge(wts["cleared"], 16)
            pool.wait_ge(s["sorted"], 1)
            for t in range(NT):
                nc.gpsimd.indirect_dma_start(out=slots, out_offset=bass.IndirectOffsetOnAxis(ap=posi[:, t:t + 1], axis=0),
                                             in_=rows[:, t, :], in_offset=None).then_inc(s["scattered"], 16)

            held = pool.alloc_register("last_token")
            pool.reg_mov(held, B * SQ - 1)
            last_token = pool.snap(held, min_val=0, max_val=B * SQ - 1)

            def store(j, b, r):
                pool.wait_ge(s["fin_ready"], j + 1)
                pool.sem_inc(s["passed"], 1)
                nc.gpsimd.indirect_dma_start(
                    out=out_rows, out_offset=bass.IndirectOffsetOnAxis(ap=sx[:, b, 2 * D:2 * D + 1].bitcast(I32), axis=0),
                    in_=fin[:, b, :], in_offset=None, bounds_check=last_token, oob_is_err=False).then_inc(stored[b], 16)

            def all_stored(j):
                for b in range(DEEP):
                    pool.wait_ge(stored[b], 16 * ((NS - b + DEEP - 1) // DEEP))

            run(pool, store, all_stored)

        @block.scalar
        def _(act):
            for c in range(NB):
                act.wait_ge(s["turned"], c + 1)
                if c:
                    act.wait_ge(s["logits_ready"], c)
                nc.scalar.activation(xt[:, :], XT[:, :], ACT.Copy).then_inc(s["turned_out"], 1)
            act.wait_ge(s["route"], 3)
            nc.scalar.activation(ex[:, :, :], dif[:, :, :], ACT.Exp).then_inc(s["exp_ready"], 1)
            act.preload_act_table_set("silu_and_others")

            def turned_out(j, p):
                act.wait_ge(s["sx_turned"], j + 1)
                if from_(j, 2):
                    act.wait_ge(s["h_ready"], j - 1)
                nc.scalar.activation(sxt[:, p, :], XT[:, 0:P], ACT.Copy).then_inc(s["sx_out"], 1)

            def silu(j, p):
                act.wait_ge(s["h_ready"], j + 1)
                if from_(j, 2):
                    act.wait_ge(s["act_ready"], j - 1)
                nc.scalar.activation(act_a[:, p, :], HA[p][:, :], ACT.Silu).then_inc(s["silu_ready"], 1)

            def at_out(j, p):
                act.wait_ge(s["at_ready"], j + 1)
                if from_(j, 2):
                    act.wait_ge(s["y_ready"], j - 1)
                nc.scalar.activation(act_t[:, p, :, :], AT[:, :].rearrange("p (c k) -> p c k", c=FC), ACT.Copy).then_inc(s["at_out"], 1)

            def step(j, b, r):
                p = b % 2
                if has(j, 1):
                    turned_out(j + 1, 1 - p)
                if from_(j, 1):
                    at_out(j - 1, 1 - p)
                silu(j, p)

            turned_out(0, 0)
            run(act, step, lambda j: at_out(j - 1, (NS - 1) % 2))

        @block.vector
        def _(dve):
            for c in range(NB):
                for t in range(T4):
                    last = nc.vector.bn_stats(stats[:, t, :], xres[:, c * T4 + t, :])
                last.then_inc(s["stats_ready"], 1)
                dve.wait_ge(s["stats_ready"], c + 1)
                for t in range(T4):
                    last = nc.vector.bn_aggr(aggr[:, t, :], stats[:, t, :])
                last.then_inc(s["aggr_ready"], 1)
                dve.wait_ge(s["aggr_ready"], c + 1)
                nc.vector.tensor_scalar(veps[:, :], aggr[:, :, 1], EPS, None, ALU.add).then_inc(s["veps_ready"], 1)
                dve.wait_ge(s["rstd_ready"], c + 1)
                for t in range(T4):
                    last = nc.vector.tensor_scalar(rows[:, c * T4 + t, 0:D], xres[:, c * T4 + t, :], aggr[:, t, 0:1],
                                                   rstd[:, t:t + 1], ALU.subtract, ALU.mult)
                last.then_inc(s["xn_ready"], 1)

            done = [0]

            def then(ins):
                done[0] += 1
                ins.then_inc(s["chain"], 1)
                dve.wait_ge(s["chain"], done[0])

            def over(ap, shape):
                return ap.broadcast_to(shape)

            dve.wait_ge(s["logits_ready"], NB)
            then(nc.vector.tensor_tensor(lg[:, :, :], LG[:, 0:NT * NE].rearrange("p (t e) -> p t e", e=NE),
                                         over(wts["rb"][:, :].rearrange("p (a e) -> p a e", a=1), [P, NT, NE]), ALU.add))
            then(nc.vector.tensor_reduce(mx[:, :], lg[:, :, :], AX.X, ALU.max))
            nc.vector.tensor_tensor(dif[:, :, :], lg[:, :, :], over(mx[:, :].rearrange("p (t a) -> p t a", a=1), [P, NT, NE]),
                                    ALU.subtract).then_inc(s["route"], 3)
            dve.wait_ge(s["route"], 3)
            then(nc.vector.scalar_tensor_tensor(out=eq[:, :, :], in0=dif[:, :, :], scalar=0.0,
                                                in1=over(wts["order"][:, :].rearrange("p (a e) -> p a e", a=1), [P, NT, NE]),
                                                op0=ALU.is_equal, op1=ALU.mult))
            then(nc.vector.tensor_reduce(first[:, :], eq[:, :, :], AX.X, ALU.min))
            nc.vector.tensor_tensor(hot[:, :, :], over(first[:, :].rearrange("p (t a) -> p t a", a=1), [P, NT, NE]),
                                    over(wts["order"][:, :].rearrange("p (a e) -> p a e", a=1), [P, NT, NE]),
                                    ALU.is_equal).then_inc(s["route"], 1)
            dve.wait_ge(s["exp_ready"], 1)
            then(nc.vector.tensor_reduce(ssum[:, :], ex[:, :, :], AX.X, ALU.add))
            then(nc.vector.reciprocal(rows[:, :, 2 * D + 1], ssum[:, :]))
            dve.wait_ge(s["ranks_ready"], 1)
            then(nc.vector.tensor_copy(cnt[:, :, :], LG[:, 256:512].rearrange("p (t e) -> p e t", e=NE)))
            then(nc.vector.tensor_tensor_scan(inc[:, :, :].rearrange("p e t -> p (e t)"), wts["again"][:, :],
                                              cnt[:, :, :].rearrange("p e t -> p (e t)"), 0.0, ALU.mult, ALU.add))
            then(nc.vector.tensor_scalar(numi[:, :], inc[:, :, NT - 1], float(P - 1), None, ALU.add))
            then(nc.vector.tensor_scalar(numi[:, :], numi[:, :], 7, None, ALU.arith_shift_right))
            then(nc.vector.tensor_copy(num[:, :], numi[:, :]))
            then(nc.vector.tensor_tensor_scan(ends[:, :], ones[:, :], num[:, :], 0.0, ALU.mult, ALU.add))
            then(nc.vector.tensor_tensor(base[:, :], ends[:, :], num[:, :], ALU.subtract))
            then(nc.vector.tensor_tensor(start[:, :, :].rearrange("p t e -> p e t"), inc[:, :, :], cnt[:, :, :], ALU.subtract))
            then(nc.vector.scalar_tensor_tensor(out=start[:, :, :], in0=over(base[:, :].rearrange("p (a e) -> p a e", a=1), [P, NT, NE]),
                                                scalar=float(P), in1=start[:, :, :], op0=ALU.mult, op1=ALU.add))
            then(nc.vector.tensor_tensor(start[:, :, :], LG[:, 0:256].rearrange("p (t e) -> p t e", e=NE), start[:, :, :], ALU.add))
            then(nc.vector.tensor_tensor(start[:, :, :], start[:, :, :], hot[:, :, :], ALU.mult))
            then(nc.vector.tensor_reduce(pos[:, :], start[:, :, :], AX.X, ALU.add))
            nc.vector.tensor_copy(posi[:, :], pos[:, :]).then_inc(s["sorted"], 1)
            then(nc.vector.tensor_tensor(below[:, :, :], over(ends[:, :].rearrange("p (a e) -> p a e", a=1), [P, NS, NE]),
                                         over(wts["tiles"][:, :].rearrange("p (j a) -> p j a", a=1), [P, NS, NE]), ALU.is_le))
            then(nc.vector.tensor_reduce(who[:, :], below[:, :, :], AX.X, ALU.add))
            nc.vector.tensor_scalar(whoi[:, :], who[:, :], float(NE - 1), None, ALU.min).then_inc(s["who_ready"], 1)

            def gate(j, p):
                dve.wait_ge(s["silu_ready"], j + 1)
                if from_(j, 2):
                    dve.wait_ge(s["at_ready"], j - 1)
                nc.vector.tensor_tensor(act_h[:, p, :], HG[p][:, :], act_a[:, p, :], ALU.mult).then_inc(s["act_ready"], 1)

            def finish(j, b, r):
                dve.wait_ge(s["y_ready"], j + 1)
                dve.wait_ge(sx_in[b], 16 * (r + 1))
                if from_(j, DEEP):
                    dve.wait_ge(stored[b], 16 * r)
                nc.vector.scalar_tensor_tensor(out=fin[:, b, :], in0=Y[:, 0:D], scalar=sx[:, b, 2 * D + 1:2 * D + 2],
                                               in1=sx[:, b, D:2 * D], op0=ALU.mult, op1=ALU.add).then_inc(s["fin_ready"], 1)

            def step(j, b, r):
                if from_(j, 2):
                    finish(j - 2, (b - 2) % DEEP, r if b >= 2 else r - 1)
                gate(j, b % 2)

            def tail(j):
                finish(j - 2, (NS - 2) % DEEP, (NS - 2) // DEEP)
                finish(j - 1, (NS - 1) % DEEP, (NS - 1) // DEEP)

            run(dve, step, tail)

        @block.tensor
        def _(pe):
            for c in range(NB + 1):
                if c < NB:
                    pe.wait_ge(s["xn_ready"], c + 1)
                    if c:
                        pe.wait_ge(s["turned_out"], c)
                    for t in range(T4):
                        last = nc.tensor.transpose(XT[:, t * P:t * P + P], rows[:, c * T4 + t, 0:D], ident[:, :])
                    last.then_inc(s["turned"], 1)
                if c < NB:
                    pe.wait_ge(s["turned_out"], c + 1)
                    for t in range(T4):
                        last = nc.tensor.matmul(LG[:, (c * T4 + t) * NE:(c * T4 + t + 1) * NE], xt[:, t * P:t * P + P],
                                                wts["rw"][:, :], start=True, stop=True)
                    last.then_inc(s["logits_ready"], 1)
            pe.wait_ge(s["route"], 4)
            nc.tensor.matmul(LG[:, 0:256], wts["before"][:, :], hot[:, :, :].rearrange("p t e -> p (t e)"), start=True, stop=True)
            nc.tensor.matmul(LG[:, 256:512], wts["all"][:, :], hot[:, :, :].rearrange("p t e -> p (t e)"),
                             start=True, stop=True).then_inc(s["ranks_ready"], 1)
            pe.wait_ge(s["who_ready"], 1)

            def turn(j, b, r):
                pe.wait_ge(sx_in[b], 16 * (r + 1))
                if from_(j, 1):
                    pe.wait_ge(s["sx_out"], j)
                nc.tensor.transpose(XT[:, 0:P], sx[:, b, 0:D], ident[:, :]).then_inc(s["sx_turned"], 1)

            def up(j, p):
                e = pe.value_load(whoi[0:1, bass.ds(j, 1)], min_val=0, max_val=NE - 1)
                pe.wait_ge(s["sx_out"], j + 1)
                if from_(j, 2):
                    pe.wait_ge(s["act_ready"], j - 1)
                nc.tensor.matmul(HA[p][:, :], sxt[:, p, :], wts["w1"][:, bass.ds(e, 1), 0:F].rearrange("p a f -> p (a f)"),
                                 start=True, stop=True)
                nc.tensor.matmul(HG[p][:, :], sxt[:, p, :], wts["w1"][:, bass.ds(e, 1), F:2 * F].rearrange("p a f -> p (a f)"),
                                 start=True, stop=True).then_inc(s["h_ready"], 1)

            def turn_act(j, p):
                pe.wait_ge(s["act_ready"], j + 1)
                if from_(j, 1):
                    pe.wait_ge(s["at_out"], j)
                for f in range(FC):
                    last = nc.tensor.transpose(AT[:, f * P:f * P + P], act_h[:, p, f * P:f * P + P], ident[:, :])
                last.then_inc(s["at_ready"], 1)

            def down(j, p):
                e = pe.value_load(whoi[0:1, bass.ds(j, 1)], min_val=0, max_val=NE - 1)
                pe.wait_ge(s["at_out"], j + 1)
                if from_(j, 1):
                    pe.wait_ge(s["fin_ready"], j)
                for f in range(FC):
                    last = nc.tensor.matmul(Y[:, 0:D], act_t[:, p, f, :], wts["w2"][:, bass.ds(e, 1), f, :].rearrange("p a n -> p (a n)"),
                                            start=(f == 0), stop=(f == FC - 1))
                last.then_inc(s["y_ready"], 1)

            def step(j, b, r):
                p = b % 2
                if has(j, 1):
                    turn(j + 1, (b + 1) % DEEP, r if b < DEEP - 1 else r + 1)
                up(j, p)
                if from_(j, 1):
                    turn_act(j - 1, 1 - p)
                if from_(j, 2):
                    down(j - 2, p)

            def tail(j):
                down(j - 2, (NS - 2) % 2)
                turn_act(j - 1, (NS - 1) % 2)
                down(j - 1, (NS - 1) % 2)

            turn(0, 0, 0)
            run(pe, step, tail)


def layer(nc, t, out):
    NE, F = 8, 512
    NS = (B * SQ + NE * (P - 1)) // P
    slots = nc.dram_tensor("slots", (NS * P, ROW), F32).ap()
    with ExitStack() as ctx:
        def sb(name, shape, dt=F32):
            return ctx.enter_context(nc.sbuf_tensor(name, shape, dt))

        rows = sb("rows", [P, NT, ROW])
        xres = rows[:, :, D:2 * D]
        ident = sb("ident", [P, P])
        wts = {"wq": sb("a_wq", [D, 512]), "wk": sb("a_wk", [D, 512]), "wv": sb("a_wv", [D, P]), "wg": sb("a_wg", [D, P]),
               "wo": sb("a_wo", [P, D]), "wgk1": sb("a_wgk1", [D, 16]), "wgk2": sb("a_wgk2", [17, 512]), "gnw": sb("a_gnw", [P, 1]),
               "causal": sb("causal", [P, P], I32), "w1": sb("w1", [D, NE, 2 * F]), "w2": sb("w2", [P, NE, F // P, D]),
               "rw": sb("rw", [D, NE]), "rb": sb("rb", [P, NE]), "order": sb("order", [P, NE]), "again": sb("again", [P, NE * NT]),
               "before": sb("before", [P, P]), "all": sb("all", [P, P]), "tiles": sb("tiles", [P, NS]),
               "token": sb("token", [P, NT], I32)}
        later = [(wts[k][:, :], t["L0_attn_" + n]) for k, n in (("wq", "Wq"), ("wk", "Wk"), ("wv", "Wv"), ("wg", "Wg"), ("wo", "Wo"), ("wgk1", "Wgk1"))]
        later += [(wts["wgk2"][0:16, :], t["L0_attn_Wgk2"]), (wts["wgk2"][16:17, :], t["L0_attn_bgk2"].rearrange("(a n) -> a n", a=1))]
        later += [(wts["gnw"][32 * h:32 * h + 32, :], t["L0_attn_gnw"].rearrange("(p a) -> p a", a=1)) for h in range(4)]
        later += [(wts["rw"][:, :], t["L0_ffn_router_w"]), (wts["rb"][:, :], t["L0_ffn_router_b"].rearrange("(a n) -> a n", a=1).broadcast_to([P, NE]))]
        later += [(wts[k][:, :], t[k]) for k in ("causal", "order", "again", "before", "all", "tiles", "token")]
        later += [(wts["w1"][:, 2 * e:2 * e + 2, :], t["L0_ffn_w1"][2 * e:2 * e + 2].rearrange("e d f -> d e f")) for e in range(NE // 2)]
        later += [(wts["w2"][:, 4 * e:4 * e + 4, :, :].rearrange("p e c n -> p (e c) n"),
                   t["L0_ffn_w2"][4 * e:4 * e + 4].rearrange("e (c p) n -> p (e c) n", p=P)) for e in range(NE // 4)]
        wts["loaded"] = ctx.enter_context(nc.semaphore("weights_loaded"))
        wts["cleared"] = ctx.enter_context(nc.semaphore("slots_cleared"))
        wts["nload"] = 16 * len(later)
        cross_attention(nc, rows, xres, ident, wts, slots, later, t["x"], t["ctx_1024"], t["mask_Bx1x1xS2_ik0"],
                        *(t["L0_xattn_" + n] for n in ("Wq", "bq", "Wk", "bk", "Wv", "bv", "Wo", "bo")), t["ident"], t["heads"])
        linear_attention(nc, xres, ident, wts)
        experts(nc, rows, xres, ident, wts, slots, out)


def kernel(**inputs):
    import numpy as np
    import concourse.bacc as bacc
    from concourse.bass_utils import run_bass_kernel_spmd as launch

    f = np.float32
    p, q, e = np.arange(P)[:, None], np.arange(P)[None, :], np.arange(8)[None, :]
    ns = (B * SQ + 8 * (P - 1)) // P
    arrays = {n: np.ascontiguousarray(a) for n, a in inputs.items()}
    arrays["ident"] = np.eye(P, dtype=f)
    arrays["heads"] = ((p // DH == np.arange(H)[None, :]) * f(SCALE)).astype(f)
    arrays["causal"] = ((p // SQ == q // SQ) & (q >= p)).astype(np.int32)
    arrays["order"] = np.ascontiguousarray(np.broadcast_to(e - 8, (P, 8))).astype(f)
    arrays["again"] = np.ascontiguousarray(np.broadcast_to(np.arange(8 * NT)[None, :] % NT != 0, (P, 8 * NT))).astype(f)
    arrays["before"] = (p < q).astype(f)
    arrays["all"] = np.ones((P, P), f)
    arrays["tiles"] = np.ascontiguousarray(np.broadcast_to(np.arange(ns)[None, :], (P, ns))).astype(f)
    arrays["token"] = (p + P * np.arange(NT)[None, :]).astype(np.int32)
    nc = bacc.Bacc("TRN2", target_bir_lowering=False, num_devices=1)
    t, feeds = {}, {}
    for n, a in arrays.items():
        feeds[f"in_{n}_dram"] = a
        t[n] = nc.dram_tensor(f"in_{n}_dram", a.shape, mybir.dt.from_np(a.dtype), kind="ExternalInput").ap()
    out = nc.dram_tensor("out_0_dram", (B, SQ, D), F32, kind="ExternalOutput").ap()
    layer(nc, t, out)
    return launch(nc, [feeds], core_ids=[0]).results[0]["out_0_dram"]
```

```python
from contextlib import ExitStack

import concourse.bass as bass
from concourse import mybir

F32 = mybir.dt.float32
BF16 = mybir.dt.bfloat16
I32 = mybir.dt.int32
ALU = mybir.AluOpType
ACT = mybir.ActivationFunctionType
AX = mybir.AxisListType

P = 128
B, SQ, D = 64, 64, 128
SK = 128
H, DH = 16, 8
EPS = 1e-5
SCALE = DH ** -0.5
MASKED = -1000000000.0
NT = B * SQ // P
NU = 4
ROW = 2 * D + 2
VW = 32


def cross_attention(nc, rows, xres, ident, wts, slots, x, ctx_in, mask, Wq, bq, Wk, bk, Wv, bv, Wo, bo, ident_in, heads_in):
    x_t = x.rearrange("(n b) s d -> n (b s) d", b=2)
    ctx_t = ctx_in.rearrange("(n b) k d -> n k b d", b=2)
    mask_t = mask.rearrange("(n b) a c k -> n (a c) (b k)", b=2)

    with ExitStack() as ctx:
        def sb(name, shape, dt=F32):
            return ctx.enter_context(nc.sbuf_tensor(name, shape, dt))

        def psum(name):
            return ctx.enter_context(nc.psum_tensor(name, [P, 512], F32))

        def sem(name):
            return ctx.enter_context(nc.semaphore(name))

        heads = sb("heads", [P, H])
        qt = sb("qt", [P, 2, P])
        wq, wk, wv = sb("wq", [D, P]), sb("wk", [D, P]), sb("wv", [D, P])
        wo2 = sb("wo2", [64, 2, D])
        bqc, bkc = sb("bqc", [P, 1]), sb("bkc", [P, 1])
        bvr, bor = sb("bvr", [P, P]), sb("bor", [P, D])
        onesb = sb("onesb", [P, P], BF16)
        halfs = sb("halfs", [P, 1])
        cin = sb("cin", [P, 2, 2, D])
        mki = sb("mki", [P, 2, 2 * SK], I32)
        mkb = sb("mkb", [P, 2, 2 * SK], BF16)
        stats, aggr, veps, rstd = sb("stats", [P, 2, 6]), sb("aggr", [P, 2, 2]), sb("veps", [P, 2]), sb("rstd", [P, 2])
        xn = sb("xn", [P, 2, D])
        xt = sb("xt", [P, 2, 384])
        kt = sb("kt", [P, 2, 2 * SK])
        vx = sb("vx", [P, 2, 2, 8, VW])
        qm = sb("qm", [P, 2, 2, H, SQ])
        mx = sb("mx", [P, 2, 4])
        dif, prob, pts = sb("dif", [P, NU, 512]), sb("prob", [P, NU, 512]), sb("pts", [P, NU, 512])
        rc = sb("rc", [P, 16])
        osum = sb("osum", [P, 512])
        on = sb("on", [P, 2, 64])
        ot = sb("ot", [64, 2, 2, SQ])

        S = [psum("S0"), psum("S1")]
        PT = [psum("PT0"), psum("PT1")]
        TB = psum("TB")
        KO = psum("KO")
        VY = psum("VY")
        OB = psum("OB")
        o_ps = OB[:, :].rearrange("p (u b j w) -> p b u j w", u=NU, b=2, j=2)

        const_in, ones_set = sem("const_in"), sem("ones_set")
        tile_in = [sem("tile_in0"), sem("tile_in1")]
        s = {n: sem(n) for n in (
            "stats_ready", "aggr_ready", "veps_ready", "rstd_ready", "xn_ready", "turned", "turned_out",
            "kv_ready", "kv_out", "q_ready", "q_out", "k_out", "q_spread", "mask_ready", "residual_ready", "logits_ready", "max_ready",
            "dif_ready", "prob_ready", "pt_ready", "pt_out", "pv_ready", "osum_ready", "o_turned", "rc_ready", "on_ready", "ot_ready",
            "ot_out", "y_ready", "x1_ready")}
        NCONST = 11
        block = ctx.enter_context(nc.Block())

        def run(eng, step, tail):
            for i in range(3):
                step(i, i % 2)
            with eng.Fori(3, NT - 3, 2) as i:
                step(i, 1)
                step(i + 1, 0)
            for i in range(NT - 3, NT):
                step(i, i % 2)
            tail(NT)

        def from_(i, k):
            return not isinstance(i, int) or i >= k

        def has(i, k):
            return not isinstance(i, int) or i + k < NT

        def half(i, p):
            return i // 2 if isinstance(i, int) else (i - p) // 2

        @block.sync
        def _(sp):
            def load(i, p):
                sp.dma_start(xres[:, bass.ds(i, 1), :], x_t[bass.ds(i, 1)].rearrange("n p d -> p n d")).then_inc(tile_in[p], 16)
                sp.dma_start(cin[:, p], ctx_t[bass.ds(i, 1)].rearrange("n k b d -> k (n b) d")).then_inc(tile_in[p], 16)
                sp.dma_start(mki[0:1, p, :], mask_t[bass.ds(i, 1)].rearrange("n a c -> (n a) c")).then_inc(tile_in[p], 16)

            sp.wait_ge(ones_set, 1)
            load(0, 0)
            for dst, src in ((ident[:, :], ident_in), (wk[:, :], Wk), (wv[:, :], Wv), (wq[:, :], Wq), (heads[:, :], heads_in)):
                sp.dma_start(dst, src).then_inc(const_in, 16)
            load(1, 1)
            with sp.Fori(2, NT - 1, 2) as i:
                for p in range(2):
                    sp.wait_ge(s["turned"], i + p - 1)
                    sp.wait_ge(s["mask_ready"], i + p - 1)
                    load(i + p, p)
            for dst, src in wts["attn_weights"]:
                sp.dma_start(dst, src).then_inc(wts["attn_loaded"], 16)
            for dst, src in wts["ffn_weights"]:
                sp.dma_start(dst, src).then_inc(wts["ffn_loaded"], 16)
            sp.wait_ge(ones_set, 6)
            sp.dma_start(slots.rearrange("(n p) w -> p n w", p=P),
                         wts["pad"][:, :].rearrange("p (a w) -> p a w", a=1).broadcast_to([P, slots.shape[0] // P, ROW])).then_inc(wts["cleared"], 16)

        @block.gpsimd
        def _(pool):
            nc.gpsimd.memset(mki[:, :, :], 0).then_inc(ones_set, 1)
            nc.gpsimd.memset(halfs[:, :], -0.5).then_inc(ones_set, 1)
            nc.gpsimd.memset(onesb[:, :], 1.0).then_inc(ones_set, 1)
            nc.gpsimd.memset(vx[:, :, :, :, :], 1.0).then_inc(ones_set, 1)
            pool.wait_ge(ones_set, 4)

            def power(i, p):
                pool.wait_ge(s["veps_ready"], i + 1)
                nc.gpsimd.tensor_tensor(rstd[:, p:p + 1], veps[:, p:p + 1], halfs[:, :], ALU.pow).then_inc(s["rstd_ready"], 1)

            def prepare(i, p):
                pool.wait_ge(tile_in[p], 48 * (half(i, p) + 1))
                if from_(i, 2):
                    pool.wait_ge(s["logits_ready"], NU * (i - 1))
                pool.wait_ge(s["stats_ready"], i + 1)
                pool.wait_ge(s["xn_ready"], i + 1)
                nc.gpsimd.tensor_tensor(xres[:, bass.ds(i, 1), :], xres[:, bass.ds(i, 1), :],
                                        bor[:, :].rearrange("p (n d) -> p n d", n=1), ALU.add).then_inc(s["residual_ready"], 1)
                nc.gpsimd.tensor_scalar(mkb[:, p, :], mki[:, p, :], MASKED, None, ALU.mult).then_inc(s["mask_ready"], 1)

            def spread(i, p):
                pool.wait_ge(s["q_out"], i + 1)
                if from_(i, 2):
                    pool.wait_ge(s["logits_ready"], NU * (i - 1))
                for b in range(2):
                    if b and from_(i, 1) and has(i, 1):
                        power(i + 1, 1 - p)
                    nc.gpsimd.tensor_tensor(
                        qm[:, p, b, :, :],
                        qt[:, p, SQ * b:SQ * b + SQ].rearrange("p (a c) -> p a c", a=1).broadcast_to([P, H, SQ]),
                        heads[:, :].rearrange("p (c a) -> p c a", a=1).broadcast_to([P, H, SQ]),
                        ALU.mult).then_inc(s["q_spread"], 1)

            power(0, 0)
            power(1, 1)
            pool.wait_ge(const_in, 16 * NCONST)
            prepare(0, 0)
            spread(0, 0)
            prepare(1, 1)
            nc.gpsimd.memset(wts["pad"][:, :], 0.0).then_inc(ones_set, 1)
            pool.wait_ge(ones_set, 5)
            nc.gpsimd.memset(wts["pad"][:, 2 * D:2 * D + 1].bitcast(I32), 1 << 20).then_inc(ones_set, 1)
            for i in range(2, 4):
                spread(i - 1, 1 - i % 2)
                prepare(i, i % 2)
            with pool.Fori(4, NT - 1, 2) as i:
                for p in range(2):
                    spread(i + p - 1, 1 - p)
                    prepare(i + p, p)
            spread(NT - 1, 1)
            nc.gpsimd.memset(wts["halfs"][:, :], -0.5)
            nc.gpsimd.memset(wts["low"][:, :, :], 1.0)
            nc.gpsimd.memset(wts["am"][:, :, :], 0.0)
            nc.gpsimd.memset(wts["reset"][:, :], 1.0).then_inc(ones_set, 1)
            pool.wait_ge(ones_set, 7)
            nc.gpsimd.memset(wts["reset"][:, 0:512:SQ], 0.0)

        @block.scalar
        def _(act):
            for dst, src in ((bqc[:, :], bq.rearrange("(p a) -> p a", a=1)), (bkc[:, :], bk.rearrange("(p a) -> p a", a=1)),
                             (bvr[:, :], bv.rearrange("(a n) -> a n", a=1).broadcast_to([P, P])),
                             (bor[:, :], bo.rearrange("(a n) -> a n", a=1).broadcast_to([P, D]))):
                act.dma_start(dst, src).then_inc(const_in, 16)
            wo_v = Wo.rearrange("(j t d) n -> t j d n", j=8, t=2)
            for t in range(2):
                act.dma_start(wo2[:, t, :], wo_v[t]).then_inc(const_in, 16)
            act.preload_act_table_set("natural_log_exp_and_others")

            def exp(i, u):
                n = NU * i + u
                act.wait_ge(s["dif_ready"], n + 1)
                if from_(i, 1):
                    act.wait_ge(s["pt_ready"], n - 3)
                nc.scalar.activation(prob[:, u, :], dif[:, u, :], ACT.Exp).then_inc(s["prob_ready"], 1)

            def evacuate(i, u):
                n = NU * i + u
                act.wait_ge(s["pt_ready"], n + 1)
                if from_(i, 1):
                    act.wait_ge(s["pv_ready"], n - 3)
                nc.scalar.activation(pts[:, u, :], PT[u % 2][:, :], ACT.Copy).then_inc(s["pt_out"], 1)

            def turned_out(i, p):
                act.wait_ge(s["turned"], i + 1)
                if from_(i, 2):
                    act.wait_ge(s["q_ready"], i - 1)
                nc.scalar.activation(xt[:, p, :], TB[:, 0:384], ACT.Copy).then_inc(s["turned_out"], 1)

            def k_out(i, p):
                act.wait_ge(s["kv_ready"], i + 1)
                if from_(i, 2):
                    act.wait_ge(s["logits_ready"], NU * (i - 1))
                nc.scalar.activation(kt[:, p, :], KO[:, 0:256], ACT.Identity, bias=bkc[:, :]).then_inc(s["k_out"], 1)

            def q_out(i, p):
                act.wait_ge(s["q_ready"], i + 1)
                if from_(i, 2):
                    act.wait_ge(s["q_spread"], 2 * (i - 1))
                nc.scalar.activation(qt[:, p, :], TB[:, 384:512], ACT.Identity, bias=bqc[:, :]).then_inc(s["q_out"], 1)

            def ot_out(i):
                act.wait_ge(s["ot_ready"], i + 1)
                if from_(i, 1):
                    act.wait_ge(s["y_ready"], i)
                nc.scalar.activation(ot[:, :, :, :], KO[0:64, 256:512].rearrange("p (b t q) -> p t b q", b=2, t=2),
                                     ACT.Copy).then_inc(s["ot_out"], 1)

            def o_out(i):
                act.wait_ge(s["pv_ready"], NU * (i + 1))
                if from_(i, 1):
                    act.wait_ge(s["o_turned"], i)
                nc.scalar.activation(osum[:, :], OB[:, :], ACT.Copy).then_inc(s["osum_ready"], 1)

            def step(i, p):
                if from_(i, 1):
                    exp(i - 1, 3)
                    evacuate(i - 1, 2)
                if has(i, 1):
                    turned_out(i + 1, 1 - p)
                exp(i, 0)
                if from_(i, 2):
                    ot_out(i - 2)
                if from_(i, 1):
                    evacuate(i - 1, 3)
                if has(i, 1):
                    q_out(i + 1, 1 - p)
                exp(i, 1)
                if has(i, 1):
                    k_out(i + 1, 1 - p)
                if from_(i, 1):
                    o_out(i - 1)
                evacuate(i, 0)
                exp(i, 2)
                evacuate(i, 1)

            def tail(i):
                exp(i - 1, 3)
                evacuate(i - 1, 2)
                ot_out(i - 2)
                evacuate(i - 1, 3)
                o_out(i - 1)
                ot_out(i - 1)

            turned_out(0, 0)
            k_out(0, 0)
            q_out(0, 0)
            run(act, step, tail)

        @block.vector
        def _(dve):
            def unit(i, u):
                n = NU * i + u
                lg = S[u % 2][:, :].rearrange("p (c k) -> p c k", k=SK)
                dve.wait_ge(s["logits_ready"], n + 1)
                nc.vector.tensor_reduce(mx[:, u % 2, :], lg, AX.X, ALU.max).then_inc(s["max_ready"], 1)
                dve.wait_ge(s["max_ready"], n + 1)
                if from_(i, 1):
                    dve.wait_ge(s["prob_ready"], n - 3)
                nc.vector.tensor_tensor(dif[:, u, :].rearrange("p (c k) -> p c k", k=SK), lg,
                                        mx[:, u % 2, :].rearrange("p (c a) -> p c a", a=1).broadcast_to([P, 4, SK]),
                                        ALU.subtract).then_inc(s["dif_ready"], 1)

            def norm(i, p):
                dve.wait_ge(tile_in[p], 48 * (half(i, p) + 1))
                xin = xres[:, bass.ds(i, 1), :]
                nc.vector.bn_stats(stats[:, p, :], xin.rearrange("p n d -> p (n d)")).then_inc(s["stats_ready"], 1)
                dve.wait_ge(s["stats_ready"], i + 1)

            def aggregate(i, p):
                nc.vector.bn_aggr(aggr[:, p, :], stats[:, p, :]).then_inc(s["aggr_ready"], 1)
                dve.wait_ge(s["aggr_ready"], i + 1)
                nc.vector.tensor_scalar(veps[:, p:p + 1], aggr[:, p, 1:2], EPS, None, ALU.add).then_inc(s["veps_ready"], 1)

            def scale(i, p):
                dve.wait_ge(s["rstd_ready"], i + 1)
                if from_(i, 2):
                    dve.wait_ge(s["turned"], i - 1)
                nc.vector.tensor_scalar(xn[:, p, :].rearrange("p (n d) -> p n d", n=1), xres[:, bass.ds(i, 1), :],
                                        aggr[:, p, 0:1], rstd[:, p:p + 1], ALU.subtract, ALU.mult).then_inc(s["xn_ready"], 1)

            def kv_out(i, p):
                dve.wait_ge(s["kv_ready"], i + 1)
                if from_(i, 2):
                    dve.wait_ge(s["pv_ready"], NU * (i - 1))
                for b in range(2):
                    nc.vector.tensor_tensor(vx[:, p, b, :, 0:16],
                                            VY[:, P * b:P * b + P].rearrange("p (j w) -> p j w", j=8),
                                            bvr[:, :].rearrange("p (j w) -> p j w", j=8), ALU.add).then_inc(s["kv_out"], 1)

            def divide(i):
                dve.wait_ge(s["o_turned"], i + 1)
                if from_(i, 1):
                    dve.wait_ge(s["ot_ready"], i)
                nc.vector.reciprocal(rc[:, :].rearrange("p (b u j) -> p b u j", b=2, j=2), o_ps[:, :, :, :, 16]).then_inc(s["rc_ready"], 1)
                dve.wait_ge(s["rc_ready"], i + 1)
                for t in range(2):
                    r = slice(64 * t, 64 * t + 64)
                    for b in range(2):
                        nc.vector.tensor_tensor(on[r, b, :].rearrange("p (u j d) -> p u j d", u=NU, j=2), o_ps[r, b, :, :, 8 * t:8 * t + 8],
                                                rc[r, 8 * b:8 * b + 8].rearrange("p (u j a) -> p u j a", j=2, a=1).broadcast_to([64, NU, 2, 8]),
                                                ALU.mult).then_inc(s["on_ready"], 1)

            def add(i):
                dve.wait_ge(s["y_ready"], i + 1)
                dve.wait_ge(s["residual_ready"], i + 1)
                nc.vector.tensor_tensor(xres[:, bass.ds(i, 1), :], VY[:, 256:384].rearrange("p (n d) -> p n d", n=1),
                                        xres[:, bass.ds(i, 1), :], ALU.add).then_inc(s["x1_ready"], 1)

            def step(i, p):
                unit(i, 0)
                if has(i, 2):
                    norm(i + 2, p)
                unit(i, 1)
                if has(i, 2):
                    aggregate(i + 2, p)
                if has(i, 1):
                    kv_out(i + 1, 1 - p)
                unit(i, 2)
                if has(i, 2):
                    scale(i + 2, p)
                if from_(i, 1):
                    divide(i - 1)
                unit(i, 3)
                if from_(i, 2):
                    add(i - 2)

            def tail(i):
                add(i - 2)
                divide(i - 1)
                add(i - 1)

            dve.wait_ge(ones_set, 4)
            for i in range(2):
                norm(i, i)
                aggregate(i, i)
                scale(i, i)
            dve.wait_ge(const_in, 16 * NCONST)
            kv_out(0, 0)
            run(dve, step, tail)

        @block.tensor
        def _(pe):
            def logits(i, u, p):
                n = NU * i + u
                if u == 0:
                    pe.wait_ge(s["q_spread"], 2 * (i + 1))
                    pe.wait_ge(s["k_out"], i + 1)
                    pe.wait_ge(s["mask_ready"], i + 1)
                if from_(i, 1) or u >= 2:
                    pe.wait_ge(s["dif_ready"], n - 1)
                nc.tensor.matmul(S[u % 2][:, :], onesb[:, :],
                                 mkb[:, p, :].rearrange("p (b a k) -> p b a k", b=2, a=1).broadcast_to([P, 2, 2, SK]),
                                 start=True, stop=False)
                for b in range(2):
                    for jj in range(2):
                        c = (2 * b + jj) * SK
                        last = nc.tensor.matmul(S[u % 2][:, c:c + SK],
                                                qm[:, p, b, 4 * u + 2 * jj:4 * u + 2 * jj + 2, :].rearrange("p c q -> p (c q)"),
                                                kt[:, p, SK * b:SK * b + SK], start=False, stop=(b == 1 and jj == 1))
                last.then_inc(s["logits_ready"], 1)

            def turn_prob(i, u):
                n = NU * i + u
                pe.wait_ge(s["prob_ready"], n + 1)
                if from_(i, 1) or u >= 2:
                    pe.wait_ge(s["pt_out"], n - 1)
                for c in range(4):
                    last = nc.tensor.transpose(PT[u % 2][:, c * P:c * P + P], prob[:, u, c * P:c * P + P], ident[:, :])
                last.then_inc(s["pt_ready"], 1)

            def values(i, u, p):
                n = NU * i + u
                pe.wait_ge(s["pt_out"], n + 1)
                if u == 0:
                    pe.wait_ge(s["kv_out"], 2 * (i + 1))
                if u == 0 and from_(i, 1):
                    pe.wait_ge(s["on_ready"], 4 * i)
                for b in range(2):
                    for jj in range(2):
                        k = 2 * b + jj
                        last = nc.tensor.matmul(OB[32 * k:32 * k + 32, u * P:u * P + P], vx[:, p, b, 2 * u + jj, :],
                                                pts[:, u, k * P:k * P + P], start=True, stop=True, tile_position=(0, 32 * k))
                last.then_inc(s["pv_ready"], 1)

            def turn_sums(i):
                pe.wait_ge(s["osum_ready"], i + 1)
                for u in range(NU):
                    last = nc.tensor.transpose(OB[:, u * P:u * P + P], osum[:, u * P:u * P + P], ident[:, :])
                last.then_inc(s["o_turned"], 1)

            def turn(i, p):
                pe.wait_ge(s["xn_ready"], i + 1)
                pe.wait_ge(tile_in[p], 48 * (half(i, p) + 1))
                if from_(i, 1):
                    pe.wait_ge(s["q_out"], i)
                for b in range(2):
                    nc.tensor.transpose(TB[:, b * P:b * P + P], cin[:, p, b, :], ident[:, :])
                nc.tensor.transpose(TB[:, 256:384], xn[:, p, :], ident[:, :]).then_inc(s["turned"], 1)

            def keys_values(i, p):
                pe.wait_ge(s["turned_out"], i + 1)
                if from_(i, 1):
                    pe.wait_ge(s["kv_out"], 2 * i)
                    pe.wait_ge(s["k_out"], i)
                if from_(i, 3):
                    pe.wait_ge(s["ot_out"], i - 2)
                if from_(i, 4):
                    pe.wait_ge(s["x1_ready"], i - 3)
                nc.tensor.matmul(KO[:, 0:256], wk[:, :], xt[:, p, 0:256], start=True, stop=True)
                for b in range(2):
                    last = nc.tensor.matmul(VY[:, b * P:b * P + P], xt[:, p, b * P:b * P + P], wv[:, :],
                                            start=True, stop=True)
                last.then_inc(s["kv_ready"], 1)

            def queries(i, p):
                pe.wait_ge(s["turned_out"], i + 1)
                nc.tensor.matmul(TB[:, 384:512], wq[:, :], xt[:, p, 256:384], start=True, stop=True).then_inc(s["q_ready"], 1)

            def output_divided(i):
                pe.wait_ge(s["on_ready"], 4 * (i + 1))
                pe.wait_ge(s["k_out"], (i + 3) if has(i, 2) else NT)

            def turn_output(i):
                for b in range(2):
                    last = nc.tensor.transpose(KO[0:64, 256 + b * P:384 + b * P], on[:, b, :], ident[:, :])
                last.then_inc(s["ot_ready"], 1)

            def project(i):
                pe.wait_ge(s["ot_out"], i + 1)
                pe.wait_ge(s["kv_out"], 2 * (i + 4) if has(i, 3) else 2 * NT)
                if not has(i, 2):
                    pe.wait_ge(s["x1_ready"], i)
                for t in range(2):
                    last = nc.tensor.matmul(VY[:, 256:384], ot[:, t, :, :].rearrange("p b q -> p (b q)"), wo2[:, t, :],
                                            start=(t == 0), stop=(t == 1))
                last.then_inc(s["y_ready"], 1)

            def step(i, p):
                logits(i, 0, p)
                if from_(i, 1):
                    turn_prob(i - 1, 2)
                    values(i - 1, 0, 1 - p)
                if has(i, 1):
                    turn(i + 1, 1 - p)
                if from_(i, 2):
                    output_divided(i - 2)
                logits(i, 1, p)
                if from_(i, 2):
                    turn_output(i - 2)
                if from_(i, 1):
                    turn_prob(i - 1, 3)
                    values(i - 1, 1, 1 - p)
                if has(i, 1):
                    queries(i + 1, 1 - p)
                    keys_values(i + 1, 1 - p)
                if from_(i, 1):
                    values(i - 1, 2, 1 - p)
                    values(i - 1, 3, 1 - p)
                logits(i, 2, p)
                turn_prob(i, 0)
                if from_(i, 1):
                    turn_sums(i - 1)
                logits(i, 3, p)
                if from_(i, 2):
                    project(i - 2)
                turn_prob(i, 1)

            def tail(i):
                output_divided(i - 2)
                turn_prob(i - 1, 2)
                turn_output(i - 2)
                values(i - 1, 0, 1)
                values(i - 1, 1, 1)
                turn_prob(i - 1, 3)
                values(i - 1, 2, 1)
                project(i - 2)
                values(i - 1, 3, 1)
                turn_sums(i - 1)
                output_divided(i - 1)
                turn_output(i - 1)
                project(i - 1)

            pe.wait_ge(const_in, 16 * NCONST)
            pe.wait_ge(ones_set, 4)
            turn(0, 0)
            keys_values(0, 0)
            queries(0, 0)
            run(pe, step, tail)


def linear_attention(nc, rows, xres, ident, wts):
    HG, DK, DV, LR = 4, 128, 32, 16
    NB = B * SQ // 512
    T4 = 512 // P
    with ExitStack() as ctx:
        def sb(name, shape, dt=F32):
            return ctx.enter_context(nc.sbuf_tensor(name, shape, dt))

        def psum(name):
            return ctx.enter_context(nc.psum_tensor(name, [P, 512], F32))

        def sem(name):
            return ctx.enter_context(nc.semaphore(name))

        xt = sb("g_xt", [D, NB, 512])
        xs = sb("g_xs", [D, 512])
        low, am, reset, halfs = (wts[n] for n in ("low", "am", "reset", "halfs"))
        val = sb("g_val", [P, NB, T4, P])
        silu = sb("g_silu", [P, NB, 512])
        stats, aggr = sb("g_stats", [P, T4, 6]), sb("g_aggr", [P, T4, 2])
        veps, rstd = sb("g_veps", [P, T4]), sb("g_rstd", [P, T4])
        xn = sb("g_xn", [P, T4, D])
        n_stats, n_aggr = sb("n_stats", [P, T4, 6]), sb("n_aggr", [P, T4, 2])
        n_veps, n_rstd = sb("n_veps", [P, T4]), sb("n_rstd", [P, T4])
        neg, mag = (sb("g_" + n, [P, 2, 512]) for n in ("neg", "mag"))
        cum, grow, decay = (sb("g_" + n, [P, 2, 512]) for n in ("cum", "grow", "decay"))
        qg, ki = (sb("g_" + n, [P, 2, 512]) for n in ("qg", "ki"))
        gneg, gmag = sb("g_gneg", [P, 512]), sb("g_gmag", [P, 512])
        sq, on, og = sb("g_sq", [P, 512]), sb("g_on", [P, 512]), sb("g_og", [P, 512])
        ms, meps, rms = sb("g_ms", [P, 16]), sb("g_meps", [P, 16]), sb("g_rms", [P, 16])

        Z, Q, K, A, O, T, U, V = (psum("g" + n) for n in "ZQKAOTUV")

        s = {n: sem("g_" + n) for n in (
            "x_kept", "stats_ready", "aggr_ready", "veps_ready", "rstd_ready", "xn_ready", "turned", "turned_out", "low_ready",
            "low_out", "v_ready", "v_out", "gate_ready", "gmag_ready", "gexp_ready", "glog_ready", "gsum_ready", "gsig_ready",
            "silu_ready", "z_ready", "mag_ready", "exp_ready", "log_ready", "tot_ready", "cum_ready", "grow_ready",
            "decay_ready", "q_ready", "k_ready", "qg_ready", "ki_ready", "a_ready", "am_ready", "o_ready", "o_out", "sq_ready",
            "ms_ready", "meps_ready", "rms_ready", "on_ready", "ot_ready", "og_ready", "y_ready", "x2_ready",
            "n_stats_ready", "n_aggr_ready", "n_veps_ready", "n_rstd_ready")}
        block = ctx.enter_context(nc.Block())

        def run(eng, step, tail):
            for c in range(3):
                step(c)
            with eng.Fori(3, NB - 2, 1) as c:
                step(c)
            step(NB - 2)
            step(NB - 1)
            tail(NB)

        def from_(c, k):
            return c >= k if isinstance(c, int) else k <= 3

        def has(c, k):
            return c + k < NB if isinstance(c, int) else k <= 2

        def cols(t, c):
            return t[:, bass.ds(c, 1), :].rearrange("p a n -> p (a n)")

        @block.gpsimd
        def _(pool):
            def keep(c):
                pool.wait_ge(s["turned_out"], c + 1)
                nc.gpsimd.tensor_copy(cols(xt, c), xs[:, :]).then_inc(s["x_kept"], 1)

            def power(c):
                pool.wait_ge(s["veps_ready"], c + 1)
                nc.gpsimd.tensor_tensor(rstd[:, :], veps[:, :], halfs[:, 0:T4], ALU.pow).then_inc(s["rstd_ready"], 1)

            def total(n, par):
                pool.wait_ge(s["log_ready"], n + 1)
                nc.gpsimd.tensor_tensor(neg[:, par, :], neg[:, par, :], mag[:, par, :], ALU.add).then_inc(s["tot_ready"], 1)

            def gate_total(c):
                pool.wait_ge(s["glog_ready"], c + 1)
                nc.gpsimd.tensor_tensor(gneg[:, :], gneg[:, :], gmag[:, :], ALU.add).then_inc(s["gsum_ready"], 1)

            def rms_power(c):
                pool.wait_ge(s["meps_ready"], c + 1)
                nc.gpsimd.tensor_tensor(rms[:, :], meps[:, :], halfs[:, :], ALU.pow).then_inc(s["rms_ready"], 1)

            def over_rms(c):
                pool.wait_ge(s["rms_ready"], c + 1)
                nc.gpsimd.tensor_tensor(on[:, :].rearrange("p (a v) -> p a v", v=DV), on[:, :].rearrange("p (a v) -> p a v", v=DV),
                                        rms[:, :].rearrange("p (a b) -> p a b", b=1).broadcast_to([P, 16, DV]),
                                        ALU.mult).then_inc(s["on_ready"], 1)

            def next_power(c):
                pool.wait_ge(s["n_veps_ready"], c + 1)
                nc.gpsimd.tensor_tensor(n_rstd[:, :], n_veps[:, :], halfs[:, 0:T4], ALU.pow).then_inc(s["n_rstd_ready"], 1)

            def tail(c):
                over_rms(c - 2)
                next_power(c - 3)
                rms_power(c - 1)
                over_rms(c - 1)
                next_power(c - 2)

            def step(c):
                for h in range(HG):
                    if h == 2 and from_(c, 3):
                        next_power(c - 3)
                    if h == 2 and has(c, 1):
                        gate_total(c + 1)
                    if h == 0 or has(c, 1):
                        total(HG * c + h + 3, (h + 1) % 2)
                    if h == 0 and from_(c, 2):
                        over_rms(c - 2)
                    if h == 3 and from_(c, 1):
                        rms_power(c - 1)
                    if h == 0 and has(c, 1):
                        keep(c + 1)
                    if h == 1 and has(c, 2):
                        power(c + 2)

            power(0)
            power(1)
            keep(0)
            total(0, 0)
            total(1, 1)
            gate_total(0)
            total(2, 0)
            run(pool, step, tail)

        @block.scalar
        def _(act):
            def turned_out(c):
                act.wait_ge(s["turned"], c + 1)
                if from_(c, 1):
                    act.wait_ge(s["v_ready"], c)
                    act.wait_ge(s["x_kept"], c)
                nc.scalar.activation(xs[:, :], T[:, :], ACT.Copy).then_inc(s["turned_out"], 1)

            def low_out(c):
                act.wait_ge(s["low_ready"], c + 1)
                nc.scalar.activation(low[0:LR, bass.ds(c, 1), :].rearrange("p a n -> p (a n)"), T[0:LR, :], ACT.Copy).then_inc(s["low_out"], 1)

            def v_out(c):
                act.wait_ge(s["v_ready"], c + 1)
                nc.scalar.activation(val[:, bass.ds(c, 1), :, :].rearrange("p a t n -> p (a t n)"), V[:, :], ACT.Copy).then_inc(s["v_out"], 1)

            def front(n, par):
                act.wait_ge(s["z_ready"], n + 1)
                if not isinstance(n, int) or n >= 2:
                    act.wait_ge(s["cum_ready"], n - 1)
                nc.scalar.activation(neg[:, par, :], Z[:, :], ACT.Relu, scale=-1.0)
                nc.scalar.activation(mag[:, par, :], Z[:, :], ACT.Abs).then_inc(s["mag_ready"], 1)
                act.wait_ge(s["mag_ready"], n + 1)
                nc.scalar.activation(mag[:, par, :], mag[:, par, :], ACT.Exp, scale=-1.0).then_inc(s["exp_ready"], 1)
                act.wait_ge(s["exp_ready"], n + 1)
                nc.scalar.activation(mag[:, par, :], mag[:, par, :], ACT.Ln, bias=1.0).then_inc(s["log_ready"], 1)

            def back(n, par):
                act.wait_ge(s["cum_ready"], n + 1)
                if not isinstance(n, int) or n >= 2:
                    act.wait_ge(s["ki_ready"], n - 1)
                nc.scalar.activation(decay[:, par, :], cum[:, par, :], ACT.Exp, scale=-1.0 / 16).then_inc(s["decay_ready"], 1)
                nc.scalar.activation(grow[:, par, :], cum[:, par, :], ACT.Exp, scale=1.0 / 16).then_inc(s["grow_ready"], 1)

            def gate_front(c):
                act.wait_ge(s["gate_ready"], c + 1)
                if from_(c, 1):
                    act.wait_ge(s["silu_ready"], c)
                nc.scalar.activation(gneg[:, :], T[:, :], ACT.Relu, scale=-1.0)
                nc.scalar.activation(gmag[:, :], T[:, :], ACT.Abs).then_inc(s["gmag_ready"], 1)
                act.wait_ge(s["gmag_ready"], c + 1)
                nc.scalar.activation(gmag[:, :], gmag[:, :], ACT.Exp, scale=-1.0).then_inc(s["gexp_ready"], 1)
                act.wait_ge(s["gexp_ready"], c + 1)
                nc.scalar.activation(gmag[:, :], gmag[:, :], ACT.Ln, bias=1.0).then_inc(s["glog_ready"], 1)

            def gate_sigmoid(c):
                act.wait_ge(s["gsum_ready"], c + 1)
                nc.scalar.activation(gneg[:, :], gneg[:, :], ACT.Exp, scale=-1.0).then_inc(s["gsig_ready"], 1)

            def o_out(c):
                act.wait_ge(s["o_ready"], HG * (c + 1))
                if from_(c, 1):
                    act.wait_ge(s["ot_ready"], c)
                    act.wait_ge(s["ms_ready"], c)
                nc.scalar.activation(on[:, :], O[:, :], ACT.Copy).then_inc(s["o_out"], 1)
                act.wait_ge(s["o_out"], c + 1)
                nc.scalar.activation(sq[:, :], on[:, :], ACT.Square).then_inc(s["sq_ready"], 1)

            def step(c):
                for h in range(HG):
                    n = HG * c + h
                    if h == 1 and has(c, 1):
                        low_out(c + 1)
                    if h == 3 and has(c, 1):
                        v_out(c + 1)
                    if h < 3 or has(c, 1):
                        back(n + 1, (h + 1) % 2)
                    if h == 0 and has(c, 1):
                        turned_out(c + 1)
                    if h == 2 and from_(c, 1):
                        o_out(c - 1)
                    if h == 2 and has(c, 1):
                        gate_front(c + 1)
                    if h == 3 and has(c, 1):
                        gate_sigmoid(c + 1)
                    if h == 0 or has(c, 1):
                        front(n + 3, (h + 1) % 2)

            turned_out(0)
            low_out(0)
            front(0, 0)
            front(1, 1)
            gate_front(0)
            back(0, 0)
            gate_sigmoid(0)
            v_out(0)
            front(2, 0)
            run(act, step, lambda c: o_out(c - 1))

        @block.vector
        def _(dve):
            def norm(c):
                for t in range(T4):
                    last = nc.vector.bn_stats(stats[:, t, :], xres[:, bass.ds(c * T4 + t, 1), :].rearrange("p n d -> p (n d)"))
                last.then_inc(s["stats_ready"], 1)
                dve.wait_ge(s["stats_ready"], c + 1)

            def aggregate(c):
                for t in range(T4):
                    last = nc.vector.bn_aggr(aggr[:, t, :], stats[:, t, :])
                last.then_inc(s["aggr_ready"], 1)
                dve.wait_ge(s["aggr_ready"], c + 1)
                nc.vector.tensor_scalar(veps[:, :], aggr[:, :, 1], EPS, None, ALU.add).then_inc(s["veps_ready"], 1)

            def unit(n, par):
                dve.wait_ge(s["decay_ready"], n + 1)
                dve.wait_ge(s["q_ready"], n + 1)
                if not isinstance(n, int) or n >= 2:
                    dve.wait_ge(s["a_ready"], n - 1)
                nc.vector.scalar_tensor_tensor(out=qg[:, par, :], in0=Q[:, :], scalar=DK ** -0.5, in1=decay[:, par, :],
                                               op0=ALU.mult, op1=ALU.mult).then_inc(s["qg_ready"], 1)
                dve.wait_ge(s["grow_ready"], n + 1)
                dve.wait_ge(s["k_ready"], n + 1)
                if not isinstance(n, int) or n >= 1:
                    dve.wait_ge(s["a_ready"], n)
                if not isinstance(n, int) or n >= 3:
                    dve.wait_ge(s["o_ready"], n - 2)
                nc.vector.tensor_tensor(ki[:, par, :], K[:, :], grow[:, par, :], ALU.mult).then_inc(s["ki_ready"], 1)

            def scan(n, par):
                dve.wait_ge(s["tot_ready"], n + 1)
                if not isinstance(n, int) or n >= 2:
                    dve.wait_ge(s["grow_ready"], n - 1)
                nc.vector.tensor_tensor_scan(cum[:, par, :], reset[:, :], neg[:, par, :], 0.0, ALU.mult, ALU.add).then_inc(s["cum_ready"], 1)

            def mask(n, par):
                for b in range(2):
                    r = slice(b * SQ, b * SQ + SQ)
                    nc.vector.copy_predicated(am[r, par, :].rearrange("p (t i) -> p t i", t=T4)[:, :, r],
                                              wts["causal"][r, :].rearrange("p (a i) -> p a i", a=1).broadcast_to([SQ, T4, SQ]),
                                              A[r, 0:T4 * SQ].rearrange("p (t i) -> p t i", t=T4)).then_inc(s["am_ready"], 1)

            def make_silu(c):
                dve.wait_ge(s["gsig_ready"], c + 1)
                nc.vector.tensor_tensor(cols(silu, c), T[:, :], gneg[:, :], ALU.mult).then_inc(s["silu_ready"], 1)

            def mean_square(c):
                dve.wait_ge(s["sq_ready"], c + 1)
                nc.vector.tensor_reduce(ms[:, :], sq[:, :].rearrange("p (a v) -> p a v", v=DV), AX.X, ALU.add).then_inc(s["ms_ready"], 1)
                dve.wait_ge(s["ms_ready"], c + 1)
                nc.vector.tensor_scalar(meps[:, :], ms[:, :], 1.0 / DV, EPS, ALU.mult, ALU.add).then_inc(s["meps_ready"], 1)

            def gate(c):
                dve.wait_ge(s["ot_ready"], c + 1)
                dve.wait_ge(s["silu_ready"], c + 1)
                if from_(c, 1):
                    dve.wait_ge(s["y_ready"], c)
                nc.vector.scalar_tensor_tensor(out=og[:, :], in0=U[:, :], scalar=wts["gnw"][:, :], in1=cols(silu, c),
                                               op0=ALU.mult, op1=ALU.mult).then_inc(s["og_ready"], 1)

            def add(c):
                dve.wait_ge(s["y_ready"], c + 1)
                xb = xres[:, bass.ds(c * T4, T4), :]
                nc.vector.tensor_tensor(xb, V[:, :].rearrange("p (t n) -> p t n", t=T4), xb, ALU.add).then_inc(s["x2_ready"], 1)

            def next_norm(c):
                for t in range(T4):
                    last = nc.vector.bn_stats(n_stats[:, t, :], xres[:, bass.ds(c * T4 + t, 1), :].rearrange("p n d -> p (n d)"))
                last.then_inc(s["n_stats_ready"], 1)

            def next_aggregate(c):
                for t in range(T4):
                    last = nc.vector.bn_aggr(n_aggr[:, t, :], n_stats[:, t, :])
                last.then_inc(s["n_aggr_ready"], 1)
                dve.wait_ge(s["n_aggr_ready"], c + 1)
                nc.vector.tensor_scalar(n_veps[:, :], n_aggr[:, :, 1], EPS, None, ALU.add).then_inc(s["n_veps_ready"], 1)

            def next_scale(c):
                dve.wait_ge(s["n_rstd_ready"], c + 1)
                for t in range(T4):
                    nc.vector.tensor_scalar(rows[:, bass.ds(c * T4 + t, 1), 0:D], xres[:, bass.ds(c * T4 + t, 1), :],
                                                   n_aggr[:, t, 0:1], n_rstd[:, t:t + 1], ALU.subtract, ALU.mult)

            def scale(c):
                dve.wait_ge(s["rstd_ready"], c + 1)
                if from_(c, 1):
                    dve.wait_ge(s["turned"], c)
                for t in range(T4):
                    last = nc.vector.tensor_scalar(xn[:, t:t + 1, :], xres[:, bass.ds(c * T4 + t, 1), :],
                                                   aggr[:, t, 0:1], rstd[:, t:t + 1], ALU.subtract, ALU.mult)
                last.then_inc(s["xn_ready"], 1)

            def step(c):
                for h in range(HG):
                    n = HG * c + h
                    if h == 0 and from_(c, 3):
                        dve.wait_ge(s["x2_ready"], c - 2)
                    if h == 1 and from_(c, 3):
                        dve.wait_ge(s["n_stats_ready"], c - 2)
                    if h < 3 or has(c, 1):
                        scan(n + 1, (h + 1) % 2)
                    unit(n, h % 2)
                    if h > 0 or from_(c, 1):
                        mask(n - 1, (h + 1) % 2)
                    if h == 2 and from_(c, 2):
                        gate(c - 2)
                    if h == 0 and from_(c, 3):
                        next_norm(c - 3)
                    if h == 1 and from_(c, 3):
                        next_aggregate(c - 3)
                    if h == 0 and has(c, 2):
                        norm(c + 2)
                    if h == 1 and has(c, 2):
                        aggregate(c + 2)
                    if h == 2:
                        if has(c, 2):
                            scale(c + 2)
                        if from_(c, 1):
                            mean_square(c - 1)
                    if h == 3:
                        if from_(c, 3):
                            next_scale(c - 3)
                        if has(c, 1):
                            make_silu(c + 1)
                        if from_(c, 2):
                            add(c - 2)

            def tail(c):
                dve.wait_ge(s["a_ready"], HG * c)
                dve.wait_ge(s["o_ready"], HG * c - 2)
                mask(HG * c - 1, 1)
                dve.wait_ge(s["x2_ready"], c - 2)
                next_norm(c - 3)
                dve.wait_ge(s["n_stats_ready"], c - 2)
                next_aggregate(c - 3)
                gate(c - 2)
                mean_square(c - 1)
                next_scale(c - 3)
                add(c - 2)
                dve.wait_ge(s["x2_ready"], c - 1)
                next_norm(c - 2)
                dve.wait_ge(s["n_stats_ready"], c - 1)
                next_aggregate(c - 2)
                gate(c - 1)
                next_scale(c - 2)
                add(c - 1)

            dve.wait_ge(wts["attn_loaded"], 16 * len(wts["attn_weights"]))
            for c in range(2):
                norm(c)
                aggregate(c)
                scale(c)
            scan(0, 0)
            make_silu(0)
            run(dve, step, tail)

        @block.tensor
        def _(pe):
            def turn(c):
                pe.wait_ge(s["xn_ready"], c + 1)
                if from_(c, 1):
                    pe.wait_ge(s["silu_ready"], c)
                for t in range(T4):
                    last = nc.tensor.transpose(T[:, t * P:t * P + P], xn[:, t, :], ident[:, :])
                last.then_inc(s["turned"], 1)

            def gate_low_rank(c):
                pe.wait_ge(s["turned_out"], c + 1)
                nc.tensor.matmul(T[0:LR, :], wts["wgk1"][:, :], xs[:, :], start=True, stop=True).then_inc(s["low_ready"], 1)

            def gate_values(c):
                pe.wait_ge(s["low_out"], c + 1)
                nc.tensor.matmul(T[:, :], wts["wg"][:, :], xs[:, :], start=True, stop=True).then_inc(s["gate_ready"], 1)
                if not isinstance(c, int) or c >= 4:
                    pe.wait_ge(s["x2_ready"], c - 3)
                if from_(c, 1):
                    pe.wait_ge(s["v_out"], c)
                for t in range(T4):
                    last = nc.tensor.matmul(V[:, t * P:t * P + P], xs[:, t * P:t * P + P], wts["wv"][:, :], start=True, stop=True)
                last.then_inc(s["v_ready"], 1)

            def log_gates(c, h):
                nc.tensor.matmul(Z[:, :], wts["wgk2"][:, h * P:h * P + P], cols(low, c), start=True, stop=True).then_inc(s["z_ready"], 1)

            def queries(n, c, h):
                if h == 0:
                    pe.wait_ge(s["x_kept"], c + 1)
                if not isinstance(n, int) or n >= 1:
                    pe.wait_ge(s["qg_ready"], n)
                nc.tensor.matmul(Q[:, :], wts["wq"][:, h * P:h * P + P], cols(xt, c), start=True, stop=True).then_inc(s["q_ready"], 1)

            def keys(n, c, h):
                if not isinstance(n, int) or n >= 1:
                    pe.wait_ge(s["ki_ready"], n)
                if h == 0 or has(c, 1):
                    pe.wait_ge(s["mag_ready"], n + 3)
                    if h == 1:
                        pe.wait_ge(s["low_out"], c + 2)
                nc.tensor.matmul(K[:, :], wts["wk"][:, h * P:h * P + P], cols(xt, c), start=True, stop=True).then_inc(s["k_ready"], 1)

            def products(n, par):
                pe.wait_ge(s["ki_ready"], n + 1)
                if not isinstance(n, int) or n >= 1:
                    pe.wait_ge(s["am_ready"], 2 * n)
                for t in range(T4):
                    for b in range(2):
                        r = slice(t * P + b * SQ, t * P + b * SQ + SQ)
                        last = nc.tensor.matmul(A[b * SQ:b * SQ + SQ, t * SQ:t * SQ + SQ], ki[:, par, r], qg[:, par, r],
                                                start=True, stop=True, tile_position=(0, b * SQ))
                last.then_inc(s["a_ready"], 1)

            def outputs(n, par, c, h):
                pe.wait_ge(s["am_ready"], 2 * (n + 1))
                if h == 0 and from_(c, 1):
                    pe.wait_ge(s["o_out"], c)
                for t in range(T4):
                    last = nc.tensor.matmul(O[:, t * P + h * DV:t * P + h * DV + DV], am[:, par, t * P:t * P + P],
                                            val[:, bass.ds(c, 1), t, h * DV:h * DV + DV].rearrange("p a v -> p (a v)"),
                                            start=True, stop=True)
                last.then_inc(s["o_ready"], 1)

            def turn_output(c):
                pe.wait_ge(s["on_ready"], c + 1)
                if from_(c, 1):
                    pe.wait_ge(s["og_ready"], c)
                for t in range(T4):
                    last = nc.tensor.transpose(U[:, t * P:t * P + P], on[:, t * P:t * P + P], ident[:, :])
                last.then_inc(s["ot_ready"], 1)

            def project(c):
                pe.wait_ge(s["og_ready"], c + 1)
                pe.wait_ge(s["v_out"], c + 4 if not isinstance(c, int) or c + 4 < NB else NB)
                if isinstance(c, int) and c >= NB - 2:
                    pe.wait_ge(s["x2_ready"], c)
                for t in range(T4):
                    last = nc.tensor.matmul(V[:, t * P:t * P + P], og[:, t * P:t * P + P], wts["wo"][:, :], start=True, stop=True)
                last.then_inc(s["y_ready"], 1)

            def step(c):
                for h in range(HG):
                    n = HG * c + h
                    queries(n, c, h)
                    if h > 0 or from_(c, 1):
                        products(n - 1, (h + 1) % 2)
                    if h == 0 and has(c, 1):
                        turn(c + 1)
                    keys(n, c, h)
                    if h == 0:
                        log_gates(c, 3)
                    elif has(c, 1):
                        log_gates(c + 1, h - 1)
                    if h > 1:
                        outputs(n - 2, h % 2, c, h - 2)
                    elif from_(c, 1):
                        outputs(n - 2, h % 2, c - 1, h + 2)
                    if h == 0 and has(c, 1):
                        gate_low_rank(c + 1)
                    if h == 1 and has(c, 1):
                        gate_values(c + 1)
                    if h == 3 and from_(c, 2):
                        project(c - 2)
                    if h == 1 and from_(c, 2):
                        turn_output(c - 2)

            def tail(c):
                products(HG * c - 1, 1)
                outputs(HG * c - 2, 0, c - 1, 2)
                outputs(HG * c - 1, 1, c - 1, 3)
                turn_output(c - 2)
                project(c - 2)
                turn_output(c - 1)
                project(c - 1)

            pe.wait_ge(wts["attn_loaded"], 16 * len(wts["attn_weights"]))
            turn(0)
            gate_low_rank(0)
            pe.wait_ge(s["low_out"], 1)
            log_gates(0, 0)
            pe.wait_ge(s["mag_ready"], 1)
            log_gates(0, 1)
            gate_values(0)
            pe.wait_ge(s["mag_ready"], 2)
            log_gates(0, 2)
            run(pe, step, tail)


def experts(nc, rows, xres, ident, wts, slots, out):
    NE, F = 8, 512
    NS = (B * SQ + NE * (P - 1)) // P
    FC = F // P
    AHEAD = 7
    DEEP = 6
    NB, T4 = NT // 4, 4
    out_rows = out.rearrange("b s d -> (b s) d")
    slot_rows = slots.rearrange("(n p) w -> n p w", p=P)
    with ExitStack() as ctx:
        def sb(name, shape, dt=F32):
            return ctx.enter_context(nc.sbuf_tensor(name, shape, dt))

        def psum(name):
            return ctx.enter_context(nc.psum_tensor(name, [P, 512], F32))

        def sem(name):
            return ctx.enter_context(nc.semaphore(name))

        stats, aggr = sb("e_stats", [P, T4, 6]), sb("e_aggr", [P, T4, 2])
        veps, rstd = sb("e_veps", [P, T4]), sb("e_rstd", [P, T4])
        xt = sb("e_xt", [D, AHEAD, 512])
        lg, dif, ex, eq, hot = (sb("e_" + n, [P, NT, NE]) for n in ("lg", "dif", "ex", "eq", "hot"))
        mx, ssum, first, pos = (sb("e_" + n, [P, NT]) for n in ("mx", "ssum", "first", "pos"))
        posi = sb("e_posi", [P, NT], I32)
        cnt, inc = sb("e_cnt", [P, NE, NT]), sb("e_inc", [P, NE, NT])
        num, base = sb("e_num", [P, NE]), sb("e_base", [P, NE])
        numi = sb("e_numi", [P, NE], I32)
        ends, ones = sb("e_ends", [P, NE]), sb("e_ones", [P, NE])
        start = sb("e_start", [P, NT, NE])
        below = sb("e_below", [P, NS, NE])
        who, whoi = sb("e_who", [P, NS]), sb("e_whoi", [P, NS], I32)
        sx = sb("e_sx", [P, DEEP, ROW])
        sxt = sb("e_sxt", [D, 2, P])
        w1c = sb("e_w1c", [D, 2, 2 * F])
        act_a, act_h = sb("e_a", [P, 2, F]), sb("e_h", [P, 2, F])
        fin = sb("e_fin", [P, DEEP, D])

        XT, Y, LG = psum("eXT"), [psum("eY0"), psum("eY1")], psum("eLG")
        HA, HG = [psum("eHA0"), psum("eHA1")], [psum("eHG0"), psum("eHG1")]
        turned = (XT, *Y, *HA, *HG)

        s = {n: sem("e_" + n) for n in (
            "set_up", "stats_ready", "aggr_ready", "veps_ready", "rstd_ready", "xn_ready", "turned", "turned_out",
            "logits_ready", "route", "exp_ready", "ranks_ready", "chain", "sorted", "scattered", "who_ready",
            "sx_turned", "sx_out", "w1a_ready", "w1g_ready", "h_ready", "silu_ready", "act_ready", "y_ready", "fin_ready",
            "passed")}
        sx_in, stored = ([sem(f"e_{n}{b}") for b in range(DEEP)] for n in ("sx_in", "stored"))
        block = ctx.enter_context(nc.Block())

        def run(eng, step, tail):
            for j in range(DEEP):
                step(j, j, 0)
            with eng.Fori(1, (NS - 1) // DEEP, 1) as r:
                for b in range(DEEP):
                    step(r * DEEP + b, b, r)
            for j in range(NS - (NS - 1) % DEEP - 1, NS):
                step(j, j % DEEP, j // DEEP)
            tail(NS)

        def from_(j, k):
            return j >= k if isinstance(j, int) else True

        def has(j, k):
            return j + k < NS if isinstance(j, int) else True

        @block.sync
        def _(sp):
            def load(j, b, r):
                if from_(j, DEEP):
                    sp.wait_ge(stored[b], 16 * r)
                sp.dma_start(sx[:, b, :], slot_rows[bass.ds(j, 1)].rearrange("n p w -> (n p) w")).then_inc(sx_in[b], 16)

            sp.wait_ge(s["scattered"], 16 * NT)
            run(sp, load, lambda j: None)

        @block.gpsimd
        def _(pool):
            nc.gpsimd.memset(ones[:, :], 1.0).then_inc(s["set_up"], 1)
            pool.wait_ge(s["veps_ready"], 1)
            nc.gpsimd.tensor_tensor(rstd[:, :], veps[:, :], wts["halfs"][:, 0:T4], ALU.pow).then_inc(s["rstd_ready"], 1)
            pool.wait_ge(wts["ffn_loaded"], 16 * len(wts["ffn_weights"]))
            nc.gpsimd.tensor_copy(rows[:, :, 2 * D:2 * D + 1].bitcast(I32).rearrange("p t a -> p (t a)"), wts["token"][:, :]).then_inc(s["set_up"], 1)
            pool.wait_ge(s["set_up"], 2)
            pool.wait_ge(wts["cleared"], 16)
            pool.wait_ge(s["sorted"], 1)
            for t in range(NT):
                nc.gpsimd.indirect_dma_start(out=slots, out_offset=bass.IndirectOffsetOnAxis(ap=posi[:, t:t + 1], axis=0),
                                             in_=rows[:, t, :], in_offset=None).then_inc(s["scattered"], 16)

            held = pool.alloc_register("last_token")
            pool.reg_mov(held, B * SQ - 1)
            last_token = pool.snap(held, min_val=0, max_val=B * SQ - 1)

            def store(j, b, r):
                pool.wait_ge(s["fin_ready"], j + 1)
                pool.sem_inc(s["passed"], 1)
                nc.gpsimd.indirect_dma_start(
                    out=out_rows, out_offset=bass.IndirectOffsetOnAxis(ap=sx[:, b, 2 * D:2 * D + 1].bitcast(I32), axis=0),
                    in_=fin[:, b, :], in_offset=None, bounds_check=last_token, oob_is_err=False).then_inc(stored[b], 16)

            def all_stored(j):
                for b in range(DEEP):
                    pool.wait_ge(stored[b], 16 * ((NS - b + DEEP - 1) // DEEP))

            run(pool, store, all_stored)

        @block.scalar
        def _(act):
            for c in range(NB):
                act.wait_ge(s["turned"], c + 1)
                if c >= AHEAD:
                    act.wait_ge(s["logits_ready"], c - AHEAD + 1)
                nc.scalar.activation(xt[:, c % AHEAD, :], turned[c % AHEAD][:, :], ACT.Copy).then_inc(s["turned_out"], 1)
            act.wait_ge(s["route"], 3)
            nc.scalar.activation(ex[:, :, :], dif[:, :, :], ACT.Exp).then_inc(s["exp_ready"], 1)
            act.preload_act_table_set("silu_and_others")

            def turned_out(j, p):
                act.wait_ge(s["sx_turned"], j + 1)
                if from_(j, 2):
                    act.wait_ge(s["h_ready"], j - 1)
                nc.scalar.activation(sxt[:, p, :], XT[:, 0:P], ACT.Copy).then_inc(s["sx_out"], 1)

            def weights(j, p):
                e = act.value_load(whoi[0:1, bass.ds(j, 1)], min_val=0, max_val=NE - 1)
                nc.scalar.activation(w1c[:, p, 0:F], wts["w1"][:, bass.ds(e, 1), 0:F].rearrange("p a f -> p (a f)"), ACT.Copy).then_inc(s["w1a_ready"], 1)

            def silu(j, p):
                act.wait_ge(s["h_ready"], j + 1)
                if from_(j, 2):
                    act.wait_ge(s["act_ready"], j - 1)
                nc.scalar.activation(act_a[:, p, :], HA[p][:, :], ACT.Silu).then_inc(s["silu_ready"], 1)

            def step(j, b, r):
                p = b % 2
                if from_(j, 1):
                    silu(j - 1, 1 - p)
                if has(j, 1):
                    turned_out(j + 1, 1 - p)
                    weights(j + 1, 1 - p)

            act.wait_ge(s["who_ready"], 1)
            weights(0, 0)
            turned_out(0, 0)
            run(act, step, lambda j: silu(j - 1, (NS - 1) % 2))

        @block.vector
        def _(dve):
            for t in range(T4):
                last = nc.vector.bn_stats(stats[:, t, :], xres[:, NT - T4 + t, :])
            last.then_inc(s["stats_ready"], 1)
            dve.wait_ge(s["stats_ready"], 1)
            for t in range(T4):
                last = nc.vector.bn_aggr(aggr[:, t, :], stats[:, t, :])
            last.then_inc(s["aggr_ready"], 1)
            dve.wait_ge(s["aggr_ready"], 1)
            nc.vector.tensor_scalar(veps[:, :], aggr[:, :, 1], EPS, None, ALU.add).then_inc(s["veps_ready"], 1)
            dve.wait_ge(s["rstd_ready"], 1)
            for t in range(T4):
                last = nc.vector.tensor_scalar(rows[:, NT - T4 + t, 0:D], xres[:, NT - T4 + t, :], aggr[:, t, 0:1],
                                               rstd[:, t:t + 1], ALU.subtract, ALU.mult)
            last.then_inc(s["xn_ready"], 1)

            done = [0]

            def then(ins):
                done[0] += 1
                ins.then_inc(s["chain"], 1)
                dve.wait_ge(s["chain"], done[0])

            def over(ap, shape):
                return ap.broadcast_to(shape)

            dve.wait_ge(wts["ffn_loaded"], 16 * len(wts["ffn_weights"]))
            dve.wait_ge(s["set_up"], 1)
            dve.wait_ge(s["logits_ready"], NB)
            then(nc.vector.tensor_tensor(lg[:, :, :], LG[:, 0:NT * NE].rearrange("p (t e) -> p t e", e=NE),
                                         over(wts["rb"][:, :].rearrange("p (a e) -> p a e", a=1), [P, NT, NE]), ALU.add))
            then(nc.vector.tensor_reduce(mx[:, :], lg[:, :, :], AX.X, ALU.max))
            nc.vector.tensor_tensor(dif[:, :, :], lg[:, :, :], over(mx[:, :].rearrange("p (t a) -> p t a", a=1), [P, NT, NE]),
                                    ALU.subtract).then_inc(s["route"], 3)
            dve.wait_ge(s["route"], 3)
            then(nc.vector.scalar_tensor_tensor(out=eq[:, :, :], in0=dif[:, :, :], scalar=0.0,
                                                in1=over(wts["order"][:, :].rearrange("p (a e) -> p a e", a=1), [P, NT, NE]),
                                                op0=ALU.is_equal, op1=ALU.mult))
            then(nc.vector.tensor_reduce(first[:, :], eq[:, :, :], AX.X, ALU.min))
            nc.vector.tensor_tensor(hot[:, :, :], over(first[:, :].rearrange("p (t a) -> p t a", a=1), [P, NT, NE]),
                                    over(wts["order"][:, :].rearrange("p (a e) -> p a e", a=1), [P, NT, NE]),
                                    ALU.is_equal).then_inc(s["route"], 1)
            dve.wait_ge(s["exp_ready"], 1)
            then(nc.vector.tensor_reduce(ssum[:, :], ex[:, :, :], AX.X, ALU.add))
            then(nc.vector.reciprocal(rows[:, :, 2 * D + 1], ssum[:, :]))
            dve.wait_ge(s["ranks_ready"], 1)
            then(nc.vector.tensor_copy(cnt[:, :, :], LG[:, 256:512].rearrange("p (t e) -> p e t", e=NE)))
            then(nc.vector.tensor_tensor_scan(inc[:, :, :].rearrange("p e t -> p (e t)"), wts["again"][:, :],
                                              cnt[:, :, :].rearrange("p e t -> p (e t)"), 0.0, ALU.mult, ALU.add))
            then(nc.vector.tensor_scalar(numi[:, :], inc[:, :, NT - 1], float(P - 1), None, ALU.add))
            then(nc.vector.tensor_scalar(numi[:, :], numi[:, :], 7, None, ALU.arith_shift_right))
            then(nc.vector.tensor_copy(num[:, :], numi[:, :]))
            then(nc.vector.tensor_tensor_scan(ends[:, :], ones[:, :], num[:, :], 0.0, ALU.mult, ALU.add))
            then(nc.vector.tensor_tensor(base[:, :], ends[:, :], num[:, :], ALU.subtract))
            then(nc.vector.tensor_tensor(start[:, :, :].rearrange("p t e -> p e t"), inc[:, :, :], cnt[:, :, :], ALU.subtract))
            then(nc.vector.scalar_tensor_tensor(out=start[:, :, :], in0=over(base[:, :].rearrange("p (a e) -> p a e", a=1), [P, NT, NE]),
                                                scalar=float(P), in1=start[:, :, :], op0=ALU.mult, op1=ALU.add))
            then(nc.vector.tensor_tensor(start[:, :, :], LG[:, 0:256].rearrange("p (t e) -> p t e", e=NE), start[:, :, :], ALU.add))
            then(nc.vector.tensor_tensor(start[:, :, :], start[:, :, :], hot[:, :, :], ALU.mult))
            then(nc.vector.tensor_reduce(pos[:, :], start[:, :, :], AX.X, ALU.add))
            nc.vector.tensor_copy(posi[:, :], pos[:, :]).then_inc(s["sorted"], 1)
            then(nc.vector.tensor_tensor(below[:, :, :], over(ends[:, :].rearrange("p (a e) -> p a e", a=1), [P, NS, NE]),
                                         over(wts["tiles"][:, :].rearrange("p (j a) -> p j a", a=1), [P, NS, NE]), ALU.is_le))
            then(nc.vector.tensor_reduce(who[:, :], below[:, :, :], AX.X, ALU.add))
            nc.vector.tensor_scalar(whoi[:, :], who[:, :], float(NE - 1), None, ALU.min).then_inc(s["who_ready"], 1)

            def weights(j, p):
                e = dve.value_load(whoi[0:1, bass.ds(j, 1)], min_val=0, max_val=NE - 1)
                nc.vector.tensor_copy(w1c[:, p, F:2 * F], wts["w1"][:, bass.ds(e, 1), F:2 * F].rearrange("p a f -> p (a f)")).then_inc(s["w1g_ready"], 1)

            def gate(j, p):
                dve.wait_ge(s["silu_ready"], j + 1)
                if from_(j, 2):
                    dve.wait_ge(s["y_ready"], j - 1)
                nc.vector.tensor_tensor(act_h[:, p, :], HG[p][:, :], act_a[:, p, :], ALU.mult).then_inc(s["act_ready"], 1)

            def finish(j, b, r):
                dve.wait_ge(s["y_ready"], j + 1)
                dve.wait_ge(sx_in[b], 16 * (r + 1))
                nc.vector.scalar_tensor_tensor(out=fin[:, b, :], in0=Y[b % 2][:, 0:D], scalar=sx[:, b, 2 * D + 1:2 * D + 2],
                                               in1=sx[:, b, D:2 * D], op0=ALU.mult, op1=ALU.add).then_inc(s["fin_ready"], 1)

            def step(j, b, r):
                if from_(j, 1):
                    gate(j - 1, (b - 1) % 2)
                if from_(j, 2):
                    finish(j - 2, (b - 2) % DEEP, r if b >= 2 else r - 1)
                if has(j, 1):
                    weights(j + 1, (b + 1) % 2)

            def tail(j):
                gate(j - 1, (NS - 1) % 2)
                finish(j - 2, (NS - 2) % DEEP, (NS - 2) // DEEP)
                finish(j - 1, (NS - 1) % DEEP, (NS - 1) // DEEP)

            dve.wait_ge(s["who_ready"], 1)
            weights(0, 0)
            run(dve, step, tail)

        @block.tensor
        def _(pe):
            pe.wait_ge(wts["ffn_loaded"], 16 * len(wts["ffn_weights"]))
            for c in range(NB + AHEAD - 1):
                if c < NB:
                    if c >= AHEAD:
                        pe.wait_ge(s["turned_out"], c - AHEAD + 1)
                    if c == NB - 1:
                        pe.wait_ge(s["xn_ready"], 1)
                    for t in range(T4):
                        last = nc.tensor.transpose(turned[c % AHEAD][:, t * P:t * P + P], rows[:, c * T4 + t, 0:D], ident[:, :])
                    last.then_inc(s["turned"], 1)
                done = c - AHEAD + 1
                if done >= 0:
                    pe.wait_ge(s["turned_out"], done + 1)
                    for t in range(T4):
                        tile = done * T4 + t
                        last = nc.tensor.matmul(LG[:, tile * NE:(tile + 1) * NE], xt[:, done % AHEAD, t * P:t * P + P],
                                                wts["rw"][:, :], start=True, stop=True)
                    last.then_inc(s["logits_ready"], 1)
            pe.wait_ge(s["route"], 4)
            nc.tensor.matmul(LG[:, 0:256], wts["before"][:, :], hot[:, :, :].rearrange("p t e -> p (t e)"), start=True, stop=True)
            nc.tensor.matmul(LG[:, 256:512], wts["all"][:, :], hot[:, :, :].rearrange("p t e -> p (t e)"),
                             start=True, stop=True).then_inc(s["ranks_ready"], 1)
            pe.wait_ge(s["who_ready"], 1)

            def turn(j, b, r):
                pe.wait_ge(sx_in[b], 16 * (r + 1))
                if from_(j, 1):
                    pe.wait_ge(s["sx_out"], j)
                nc.tensor.transpose(XT[:, 0:P], sx[:, b, 0:D], ident[:, :]).then_inc(s["sx_turned"], 1)

            def up(j, p):
                pe.wait_ge(s["sx_out"], j + 1)
                pe.wait_ge(s["w1a_ready"], j + 1)
                pe.wait_ge(s["w1g_ready"], j + 1)
                if from_(j, 2):
                    pe.wait_ge(s["act_ready"], j - 1)
                for bank, at in ((HA[p], 0), (HG[p], F)):
                    for f in range(FC):
                        last = nc.tensor.matmul(bank[:, f * P:f * P + P], w1c[:, p, at + f * P:at + f * P + P], sxt[:, p, :],
                                                start=True, stop=True)
                last.then_inc(s["h_ready"], 1)

            def down(j, p):
                e = pe.value_load(whoi[0:1, bass.ds(j, 1)], min_val=0, max_val=NE - 1)
                pe.wait_ge(s["act_ready"], j + 1)
                if from_(j, 2):
                    pe.wait_ge(s["fin_ready"], j - 1)
                for f in range(FC):
                    last = nc.tensor.matmul(Y[p][:, 0:D], act_h[:, p, f * P:f * P + P], wts["w2"][:, bass.ds(e, 1), f, :].rearrange("p a n -> p (a n)"),
                                            start=(f == 0), stop=(f == FC - 1))
                last.then_inc(s["y_ready"], 1)

            def step(j, b, r):
                p = b % 2
                if has(j, 1):
                    turn(j + 1, (b + 1) % DEEP, r if b < DEEP - 1 else r + 1)
                up(j, p)
                if from_(j, 1):
                    down(j - 1, 1 - p)

            def tail(j):
                down(j - 1, (NS - 1) % 2)

            turn(0, 0, 0)
            run(pe, step, tail)


def layer(nc, t, out):
    NE, F = 8, 512
    NS = (B * SQ + NE * (P - 1)) // P
    slots = nc.dram_tensor("slots", (NS * P, ROW), F32).ap()
    with ExitStack() as ctx:
        def sb(name, shape, dt=F32):
            return ctx.enter_context(nc.sbuf_tensor(name, shape, dt))

        rows = sb("rows", [P, NT, ROW])
        xres = rows[:, :, D:2 * D]
        ident = sb("ident", [P, P])
        wts = {"wq": sb("a_wq", [D, 512]), "wk": sb("a_wk", [D, 512]), "wv": sb("a_wv", [D, P]), "wg": sb("a_wg", [D, P]),
               "wo": sb("a_wo", [P, D]), "wgk1": sb("a_wgk1", [D, 16]), "wgk2": sb("a_wgk2", [17, 512]), "gnw": sb("a_gnw", [P, 1]),
               "causal": sb("causal", [P, SQ], I32), "w1": sb("w1", [D, NE, 2 * F]), "w2": sb("w2", [P, NE, F // P, D]),
               "rw": sb("rw", [D, NE]), "rb": sb("rb", [P, NE]), "order": sb("order", [P, NE]), "again": sb("again", [P, NE * NT]),
               "before": sb("before", [P, P]), "all": sb("all", [P, P]), "tiles": sb("tiles", [P, NS]),
               "token": sb("token", [P, NT], I32),
               "low": sb("low", [17, B * SQ // 512, 512]), "am": sb("am", [P, 2, 512]), "reset": sb("reset", [P, 512]),
               "halfs": sb("g_halfs", [P, 16])}
        wts["pad"] = sb("pad", [P, ROW])
        wts["attn_weights"] = [(wts[k][:, :], t["L0_attn_" + n]) for k, n in
                               (("wq", "Wq"), ("wk", "Wk"), ("wv", "Wv"), ("wg", "Wg"), ("wo", "Wo"), ("wgk1", "Wgk1"))]
        wts["attn_weights"] += [(wts["wgk2"][0:16, :], t["L0_attn_Wgk2"]),
                                (wts["wgk2"][16:17, :], t["L0_attn_bgk2"].rearrange("(a n) -> a n", a=1)),
                                (wts["causal"][:, :], t["causal"])]
        wts["attn_weights"] += [(wts["gnw"][32 * h:32 * h + 32, :], t["L0_attn_gnw"].rearrange("(p a) -> p a", a=1)) for h in range(4)]
        wts["ffn_weights"] = [(wts["rw"][:, :], t["L0_ffn_router_w"]),
                              (wts["rb"][:, :], t["L0_ffn_router_b"].rearrange("(a n) -> a n", a=1).broadcast_to([P, NE]))]
        wts["ffn_weights"] += [(wts[k][:, :], t[k]) for k in ("order", "again", "before", "all", "tiles", "token")]
        wts["ffn_weights"] += [(wts["w1"][:, 2 * e:2 * e + 2, :], t["L0_ffn_w1"][2 * e:2 * e + 2].rearrange("e d f -> d e f"))
                               for e in range(NE // 2)]
        wts["ffn_weights"] += [(wts["w2"][:, 4 * e:4 * e + 4, :, :].rearrange("p e c n -> p (e c) n"),
                                t["L0_ffn_w2"][4 * e:4 * e + 4].rearrange("e (c p) n -> p (e c) n", p=P)) for e in range(NE // 4)]
        for n in ("attn_loaded", "ffn_loaded", "cleared"):
            wts[n] = ctx.enter_context(nc.semaphore(n))
        cross_attention(nc, rows, xres, ident, wts, slots, t["x"], t["ctx_1024"], t["mask_Bx1x1xS2_ik0"],
                        *(t["L0_xattn_" + n] for n in ("Wq", "bq", "Wk", "bk", "Wv", "bv", "Wo", "bo")), t["ident"], t["heads"])
        linear_attention(nc, rows, xres, ident, wts)
        experts(nc, rows, xres, ident, wts, slots, out)


def kernel(**inputs):
    import numpy as np
    import concourse.bacc as bacc
    from concourse.bass_utils import run_bass_kernel_spmd as launch

    f = np.float32
    p, q, e = np.arange(P)[:, None], np.arange(P)[None, :], np.arange(8)[None, :]
    ns = (B * SQ + 8 * (P - 1)) // P
    arrays = {n: np.ascontiguousarray(a) for n, a in inputs.items()}
    arrays["ident"] = np.eye(P, dtype=f)
    arrays["heads"] = ((p // DH == np.arange(H)[None, :]) * f(SCALE)).astype(f)
    arrays["causal"] = (q[:, :SQ] >= p % SQ).astype(np.int32)
    arrays["order"] = np.ascontiguousarray(np.broadcast_to(e - 8, (P, 8))).astype(f)
    arrays["again"] = np.ascontiguousarray(np.broadcast_to(np.arange(8 * NT)[None, :] % NT != 0, (P, 8 * NT))).astype(f)
    arrays["before"] = (p < q).astype(f)
    arrays["all"] = np.ones((P, P), f)
    arrays["tiles"] = np.ascontiguousarray(np.broadcast_to(np.arange(ns)[None, :], (P, ns))).astype(f)
    arrays["token"] = (p + P * np.arange(NT)[None, :]).astype(np.int32)
    nc = bacc.Bacc("TRN2", target_bir_lowering=False, num_devices=1)
    t, feeds = {}, {}
    for n, a in arrays.items():
        feeds[f"in_{n}_dram"] = a
        t[n] = nc.dram_tensor(f"in_{n}_dram", a.shape, mybir.dt.from_np(a.dtype), kind="ExternalInput").ap()
    out = nc.dram_tensor("out_0_dram", (B, SQ, D), F32, kind="ExternalOutput").ap()
    layer(nc, t, out)
    return launch(nc, [feeds], core_ids=[0]).results[0]["out_0_dram"]
```
